# Optimizing a Trainium2 kernel written in Bass

```python
import numpy as np
import jax
import jax.numpy as jnp

def _softmax(x, axis=-1):
    return jax.nn.softmax(x, axis=axis)

def _gelu(x):
    return jax.nn.gelu(x, approximate=True)

def _silu(x):
    return jax.nn.silu(x)

def _sigmoid(x):
    return jax.nn.sigmoid(x)

def _layernorm(x, axis=-1, eps=1e-05):
    m = jnp.mean(x, axis=axis, keepdims=True)
    v = jnp.var(x, axis=axis, keepdims=True)
    return (x - m) / jnp.sqrt(v + eps)

def _scatter_add(tgt, idx, src, axis=0):
    return tgt.at[idx].add(src)

def _segment_sum(src, seg, n):
    return jax.ops.segment_sum(src, seg, n)
kernel_name = 'mk_cond_seq_d4_seqx_r4_5d1871'

def setup_inputs(seed: int=0):
    np.random.seed(seed)
    _w = jnp.asarray

    def _rec_inputs():
        import jax
        import jax.numpy as jnp
        _rk = jax.random.key(seed)
        x = 1.648e-05 + 1 * jax.random.normal(jax.random.fold_in(_rk, 1), (2, 1024, 288), jnp.float32)
        _lenS = 1024 - jax.random.randint(jax.random.fold_in(_rk, 7), (2,), 0, max(1, 1024 // 4) + 1, jnp.int32)
        _lenS2 = 1024 - jax.random.randint(jax.random.fold_in(_rk, 8), (2,), 0, max(1, 1024 // 4) + 1, jnp.int32)
        cond_1152 = 0.00914911 + 1.00357 * jax.random.normal(jax.random.fold_in(_rk, 11), (2, 288), jnp.float32)
        return (x, cond_1152)
    x, cond_1152 = _rec_inputs()

    def _L0_cond_setup():
        import jax, jax.numpy as jnp
        import numpy as np
        B, L, C = (8, 256, 288)
        H = 16
        D = C // H
        FF = int(C * 4.0)
        EPS = 1e-06

        def _layernorm(x):
            mu = jnp.mean(x, axis=-1, keepdims=True)
            var = jnp.mean(jnp.square(x - mu), axis=-1, keepdims=True)
            return (x - mu) * jax.lax.rsqrt(var + EPS)

        def _modulate(x, shift, scale):
            return x * (1.0 + scale) + shift

        def _attention(h, W_qkv, b_qkv, W_proj, b_proj):
            b, l, c = h.shape
            qkv = h @ W_qkv + b_qkv
            qkv = qkv.reshape(b, l, 3, H, D)
            q, k, v = (qkv[:, :, 0], qkv[:, :, 1], qkv[:, :, 2])
            scale = D ** (-0.5)
            scores = jnp.einsum('blhd,bmhd->bhlm', q * scale, k)
            attn = jax.nn.softmax(scores, axis=-1)
            o = jnp.einsum('bhlm,bmhd->blhd', attn, v).reshape(b, l, c)
            return o @ W_proj + b_proj
        key = jax.random.key(seed)
        ks = jax.random.split(key, 12)
        s = 0.02
        return {'x': jax.random.normal(ks[0], (B, L, C), jnp.float32), 'c': jax.random.normal(ks[1], (B, 1, C), jnp.float32), 'W_qkv': jax.random.normal(ks[2], (C, 3 * C), jnp.float32) * s, 'b_qkv': jnp.zeros((3 * C,), jnp.float32), 'W_proj': jax.random.normal(ks[3], (C, C), jnp.float32) * s, 'b_proj': jnp.zeros((C,), jnp.float32), 'W_fc1': jax.random.normal(ks[4], (C, FF), jnp.float32) * s, 'b_fc1': jnp.zeros((FF,), jnp.float32), 'W_fc2': jax.random.normal(ks[5], (FF, C), jnp.float32) * s, 'b_fc2': jnp.zeros((C,), jnp.float32), 'W_ada': jax.random.normal(ks[6], (C, 6 * C), jnp.float32) * s, 'b_ada': jnp.zeros((6 * C,), jnp.float32)}
    _L0_cond_all = _L0_cond_setup()
    _L0_cond_in = {k: v for k, v in _L0_cond_all.items() if k in ('W_qkv', 'b_qkv', 'W_proj', 'b_proj', 'W_fc1', 'b_fc1', 'W_fc2', 'b_fc2', 'W_ada', 'b_ada')}
    del _L0_cond_all

    def _L1_cond_setup():
        import jax, jax.numpy as jnp
        import numpy as np
        from jax.scipy.linalg import expm
        N, D, COND_DIM = (288, 64, 288)
        B, T = (16, 256)

        def _rotation(cond, W, b):
            v = jax.nn.silu(cond) @ W.T + b
            iu, ju = jnp.triu_indices(D, k=1)
            A = jnp.zeros((cond.shape[0], D, D), dtype=v.dtype)
            A = A.at[:, iu, ju].set(v).at[:, ju, iu].set(-v)
            return expm(A)
        key = jax.random.key(seed)
        k1, k2, k3, k4, k5 = jax.random.split(key, 5)
        x = jax.random.normal(k1, (B, T, N), dtype=jnp.float32)
        cond = jax.random.normal(k2, (B, COND_DIM), dtype=jnp.float32)
        P = jax.random.normal(k3, (N, D), dtype=jnp.float32)
        n_skew = D * (D - 1) // 2
        bound = 1.0 / np.sqrt(COND_DIM)
        W = jax.random.uniform(k4, (n_skew, COND_DIM), minval=-bound, maxval=bound, dtype=jnp.float32)
        b = jax.random.uniform(k5, (n_skew,), minval=-bound, maxval=bound, dtype=jnp.float32)
        return {'x': x, 'cond': cond, 'P': P, 'W': W, 'b': b}
    _L1_cond_all = _L1_cond_setup()
    _L1_cond_in = {k: v for k, v in _L1_cond_all.items() if k in ('P', 'W', 'b')}
    del _L1_cond_all

    def _L2_cond_setup():
        import jax, jax.numpy as jnp
        import numpy as np
        NUM_HEADS = 16
        NUM_EXPERTS = 4
        TOP_K = 2
        LN_EPS = 1e-06

        def _ln(h):
            mu = jnp.mean(h, axis=-1, keepdims=True)
            var = jnp.var(h, axis=-1, keepdims=True)
            return (h - mu) * jax.lax.rsqrt(var + LN_EPS)

        def _modulate(h, shift, scale):
            return h * (1.0 + scale[:, None, :]) + shift[:, None, :]
        key = jax.random.key(seed)
        ks = jax.random.split(key, 12)
        B, N, C = (8, 256, 288)
        H = 4 * C
        E = NUM_EXPERTS
        s = 0.02
        return {'x': jax.random.normal(ks[0], (B, N, C), jnp.float32), 'c': jax.random.normal(ks[1], (B, C), jnp.float32), 'w_adaln': jax.random.normal(ks[2], (C, 6 * C), jnp.float32) * s, 'b_adaln': jnp.zeros((6 * C,), jnp.float32), 'w_qkv': jax.random.normal(ks[3], (C, 3 * C), jnp.float32) * s, 'b_qkv': jnp.zeros((3 * C,), jnp.float32), 'w_proj': jax.random.normal(ks[4], (C, C), jnp.float32) * s, 'b_proj': jnp.zeros((C,), jnp.float32), 'w_gate': jax.random.normal(ks[5], (C, E), jnp.float32) * s, 'w1': jax.random.normal(ks[6], (E, C, H), jnp.float32) * s, 'b1': jnp.zeros((E, H), jnp.float32), 'w2': jax.random.normal(ks[7], (E, H, C), jnp.float32) * s, 'b2': jnp.zeros((E, C), jnp.float32)}
    _L2_cond_all = _L2_cond_setup()
    _L2_cond_in = {k: v for k, v in _L2_cond_all.items() if k in ('w_adaln', 'b_adaln', 'w_qkv', 'b_qkv', 'w_proj', 'b_proj', 'w_gate', 'w1', 'b1', 'w2', 'b2')}
    del _L2_cond_all

    def _L3_cond_setup():
        import jax, jax.numpy as jnp
        import numpy as np
        H = 288
        NH = 16
        HD = H // NH
        MLP = int(H * 4.0)
        EPS = 1e-06

        def _ln(z, scale=None):
            m = jnp.mean(z, axis=-1, keepdims=True)
            v = jnp.mean(jnp.square(z - m), axis=-1, keepdims=True)
            y = (z - m) * jax.lax.rsqrt(v + EPS)
            if scale is not None:
                y = y * scale
            return y
        key = jax.random.key(seed)
        ks = jax.random.split(key, 16)
        B, N = (16, 256)
        x = jax.random.normal(ks[0], (B, N, H), dtype=jnp.float32)
        c = jax.random.normal(ks[1], (B, H), dtype=jnp.float32)

        def xav(k, fan_in, fan_out):
            lim = np.sqrt(6.0 / (fan_in + fan_out))
            return jax.random.uniform(k, (fan_in, fan_out), jnp.float32, -lim, lim)
        w_mod = 0.02 * jax.random.normal(ks[2], (H, 6 * H), dtype=jnp.float32)
        b_mod = 0.02 * jax.random.normal(ks[3], (6 * H,), dtype=jnp.float32)
        w_qkv = xav(ks[4], H, 3 * H)
        b_qkv = jnp.zeros((3 * H,), jnp.float32)
        g_q = jnp.ones((HD,), jnp.float32)
        g_k = jnp.ones((HD,), jnp.float32)
        w_proj = xav(ks[5], H, H)
        b_proj = jnp.zeros((H,), jnp.float32)
        w1 = xav(ks[6], H, MLP)
        b1 = jnp.zeros((MLP,), jnp.float32)
        w2 = xav(ks[7], MLP, H)
        b2 = jnp.zeros((H,), jnp.float32)
        return dict(x=x, c=c, w_mod=w_mod, b_mod=b_mod, w_qkv=w_qkv, b_qkv=b_qkv, g_q=g_q, g_k=g_k, w_proj=w_proj, b_proj=b_proj, w1=w1, b1=b1, w2=w2, b2=b2)
    _L3_cond_all = _L3_cond_setup()
    _L3_cond_in = {k: v for k, v in _L3_cond_all.items() if k in ('w_mod', 'b_mod', 'w_qkv', 'b_qkv', 'g_q', 'g_k', 'w_proj', 'b_proj', 'w1', 'b1', 'w2', 'b2')}
    del _L3_cond_all
    return {'x': x, 'cond_1152': cond_1152, 'L0_cond_W_qkv': _L0_cond_in['W_qkv'], 'L0_cond_b_qkv': _L0_cond_in['b_qkv'], 'L0_cond_W_proj': _L0_cond_in['W_proj'], 'L0_cond_b_proj': _L0_cond_in['b_proj'], 'L0_cond_W_fc1': _L0_cond_in['W_fc1'], 'L0_cond_b_fc1': _L0_cond_in['b_fc1'], 'L0_cond_W_fc2': _L0_cond_in['W_fc2'], 'L0_cond_b_fc2': _L0_cond_in['b_fc2'], 'L0_cond_W_ada': _L0_cond_in['W_ada'], 'L0_cond_b_ada': _L0_cond_in['b_ada'], 'L1_cond_P': _L1_cond_in['P'], 'L1_cond_W': _L1_cond_in['W'], 'L1_cond_b': _L1_cond_in['b'], 'L2_cond_w_adaln': _L2_cond_in['w_adaln'], 'L2_cond_b_adaln': _L2_cond_in['b_adaln'], 'L2_cond_w_qkv': _L2_cond_in['w_qkv'], 'L2_cond_b_qkv': _L2_cond_in['b_qkv'], 'L2_cond_w_proj': _L2_cond_in['w_proj'], 'L2_cond_b_proj': _L2_cond_in['b_proj'], 'L2_cond_w_gate': _L2_cond_in['w_gate'], 'L2_cond_w1': _L2_cond_in['w1'], 'L2_cond_b1': _L2_cond_in['b1'], 'L2_cond_w2': _L2_cond_in['w2'], 'L2_cond_b2': _L2_cond_in['b2'], 'L3_cond_w_mod': _L3_cond_in['w_mod'], 'L3_cond_b_mod': _L3_cond_in['b_mod'], 'L3_cond_w_qkv': _L3_cond_in['w_qkv'], 'L3_cond_b_qkv': _L3_cond_in['b_qkv'], 'L3_cond_g_q': _L3_cond_in['g_q'], 'L3_cond_g_k': _L3_cond_in['g_k'], 'L3_cond_w_proj': _L3_cond_in['w_proj'], 'L3_cond_b_proj': _L3_cond_in['b_proj'], 'L3_cond_w1': _L3_cond_in['w1'], 'L3_cond_b1': _L3_cond_in['b1'], 'L3_cond_w2': _L3_cond_in['w2'], 'L3_cond_b2': _L3_cond_in['b2']}

def reference(x, cond_1152, L0_cond_W_qkv, L0_cond_b_qkv, L0_cond_W_proj, L0_cond_b_proj, L0_cond_W_fc1, L0_cond_b_fc1, L0_cond_W_fc2, L0_cond_b_fc2, L0_cond_W_ada, L0_cond_b_ada, L1_cond_P, L1_cond_W, L1_cond_b, L2_cond_w_adaln, L2_cond_b_adaln, L2_cond_w_qkv, L2_cond_b_qkv, L2_cond_w_proj, L2_cond_b_proj, L2_cond_w_gate, L2_cond_w1, L2_cond_b1, L2_cond_w2, L2_cond_b2, L3_cond_w_mod, L3_cond_b_mod, L3_cond_w_qkv, L3_cond_b_qkv, L3_cond_g_q, L3_cond_g_k, L3_cond_w_proj, L3_cond_b_proj, L3_cond_w1, L3_cond_b1, L3_cond_w2, L3_cond_b2):
    import jax
    import jax.numpy as jnp

    def _L0_cond_ref(x, c, W_qkv, b_qkv, W_proj, b_proj, W_fc1, b_fc1, W_fc2, b_fc2, W_ada, b_ada):
        import jax, jax.numpy as jnp
        import numpy as np
        B, L, C = (8, 256, 288)
        H = 16
        D = C // H
        FF = int(C * 4.0)
        EPS = 1e-06

        def _layernorm(x):
            mu = jnp.mean(x, axis=-1, keepdims=True)
            var = jnp.mean(jnp.square(x - mu), axis=-1, keepdims=True)
            return (x - mu) * jax.lax.rsqrt(var + EPS)

        def _modulate(x, shift, scale):
            return x * (1.0 + scale) + shift

        def _attention(h, W_qkv, b_qkv, W_proj, b_proj):
            b, l, c = h.shape
            qkv = h @ W_qkv + b_qkv
            qkv = qkv.reshape(b, l, 3, H, D)
            q, k, v = (qkv[:, :, 0], qkv[:, :, 1], qkv[:, :, 2])
            scale = D ** (-0.5)
            scores = jnp.einsum('blhd,bmhd->bhlm', q * scale, k)
            attn = jax.nn.softmax(scores, axis=-1)
            o = jnp.einsum('bhlm,bmhd->blhd', attn, v).reshape(b, l, c)
            return o @ W_proj + b_proj
        ada = jax.nn.silu(c) @ W_ada + b_ada
        shift_msa, scale_msa, gate_msa, shift_mlp, scale_mlp, gate_mlp = jnp.split(ada, 6, axis=-1)
        h = _modulate(_layernorm(x), shift_msa, scale_msa)
        x = x + gate_msa * _attention(h, W_qkv, b_qkv, W_proj, b_proj)
        h = _modulate(_layernorm(x), shift_mlp, scale_mlp)
        mlp = jax.nn.gelu(h @ W_fc1 + b_fc1, approximate=True) @ W_fc2 + b_fc2
        x = x + gate_mlp * mlp
        return x

    def _L1_cond_ref(x, cond, P, W, b):
        import jax, jax.numpy as jnp
        import numpy as np
        from jax.scipy.linalg import expm
        N, D, COND_DIM = (288, 64, 288)
        B, T = (16, 256)

        def _rotation(cond, W, b):
            v = jax.nn.silu(cond) @ W.T + b
            iu, ju = jnp.triu_indices(D, k=1)
            A = jnp.zeros((cond.shape[0], D, D), dtype=v.dtype)
            A = A.at[:, iu, ju].set(v).at[:, ju, iu].set(-v)
            return expm(A)
        U, _ = jnp.linalg.qr(P)
        R = _rotation(cond, W, b)
        z = jnp.einsum('btn,nd->btd', x, U)
        z_rot = jnp.einsum('btd,bde->bte', z, R)
        x_rot = x + jnp.einsum('btd,nd->btn', z_rot - z, U)
        return x_rot

    def _L2_cond_ref(x, c, w_adaln, b_adaln, w_qkv, b_qkv, w_proj, b_proj, w_gate, w1, b1, w2, b2):
        import jax, jax.numpy as jnp
        import numpy as np
        NUM_HEADS = 16
        NUM_EXPERTS = 4
        TOP_K = 2
        LN_EPS = 1e-06

        def _ln(h):
            mu = jnp.mean(h, axis=-1, keepdims=True)
            var = jnp.var(h, axis=-1, keepdims=True)
            return (h - mu) * jax.lax.rsqrt(var + LN_EPS)

        def _modulate(h, shift, scale):
            return h * (1.0 + scale[:, None, :]) + shift[:, None, :]
        B, N, C = x.shape
        nh = NUM_HEADS
        hd = C // nh
        mod = jax.nn.silu(c) @ w_adaln + b_adaln
        sh_msa, sc_msa, g_msa, sh_mlp, sc_mlp, g_mlp = jnp.split(mod, 6, axis=-1)
        h = _modulate(_ln(x), sh_msa, sc_msa)
        qkv = (h @ w_qkv + b_qkv).reshape(B, N, 3, nh, hd).transpose(2, 0, 3, 1, 4)
        q, k, v = (qkv[0], qkv[1], qkv[2])
        attn = jax.nn.softmax(jnp.einsum('bhqd,bhkd->bhqk', q, k) * hd ** (-0.5), axis=-1)
        o = jnp.einsum('bhqk,bhkd->bhqd', attn, v).transpose(0, 2, 1, 3).reshape(B, N, C)
        o = o @ w_proj + b_proj
        x = x + g_msa[:, None, :] * o
        xn = _modulate(_ln(x), sh_mlp, sc_mlp)
        xf = xn.reshape(-1, C)
        gate_logits = xf @ w_gate
        topk_logits, topk_idx = jax.lax.top_k(gate_logits, TOP_K)
        gates = jax.nn.softmax(topk_logits, axis=-1)
        cw = jnp.sum(jax.nn.one_hot(topk_idx, NUM_EXPERTS, dtype=xf.dtype) * gates[..., None], axis=1)
        hmid = jax.nn.gelu(jnp.einsum('tc,ech->eth', xf, w1) + b1[:, None, :], approximate=True)
        eo = jnp.einsum('eth,ehc->etc', hmid, w2) + b2[:, None, :]
        moe = jnp.einsum('te,etc->tc', cw, eo).reshape(B, N, C)
        return x + g_mlp[:, None, :] * moe

    def _L3_cond_ref(x, c, w_mod, b_mod, w_qkv, b_qkv, g_q, g_k, w_proj, b_proj, w1, b1, w2, b2):
        import jax, jax.numpy as jnp
        import numpy as np
        H = 288
        NH = 16
        HD = H // NH
        MLP = int(H * 4.0)
        EPS = 1e-06

        def _ln(z, scale=None):
            m = jnp.mean(z, axis=-1, keepdims=True)
            v = jnp.mean(jnp.square(z - m), axis=-1, keepdims=True)
            y = (z - m) * jax.lax.rsqrt(v + EPS)
            if scale is not None:
                y = y * scale
            return y
        B, N, _ = x.shape
        mod = jax.nn.swish(c) @ w_mod + b_mod
        sh_msa, sc_msa, g_msa, sh_mlp, sc_mlp, g_mlp = jnp.split(mod, 6, axis=1)
        xn = _ln(x) * (1 + sc_msa[:, None, :]) + sh_msa[:, None, :]
        qkv = xn @ w_qkv + b_qkv
        qkv = qkv.reshape(B, N, 3, NH, HD).transpose(2, 0, 3, 1, 4)
        q, k, v = (qkv[0], qkv[1], qkv[2])
        q = _ln(q, g_q)
        k = _ln(k, g_k)
        attn = jax.nn.softmax(jnp.einsum('bhqd,bhkd->bhqk', q, k) * HD ** (-0.5), axis=-1)
        o = jnp.einsum('bhqk,bhkd->bhqd', attn, v)
        o = o.transpose(0, 2, 1, 3).reshape(B, N, H) @ w_proj + b_proj
        x = x + g_msa[:, None, :] * o
        xn2 = _ln(x) * (1 + sc_mlp[:, None, :]) + sh_mlp[:, None, :]
        h = jax.nn.gelu(xn2 @ w1 + b1, approximate=True)
        x = x + g_mlp[:, None, :] * (h @ w2 + b2)
        return x
    x = _L0_cond_ref(x, cond_1152[:, None, :], L0_cond_W_qkv, L0_cond_b_qkv, L0_cond_W_proj, L0_cond_b_proj, L0_cond_W_fc1, L0_cond_b_fc1, L0_cond_W_fc2, L0_cond_b_fc2, L0_cond_W_ada, L0_cond_b_ada)
    x = _L1_cond_ref(x, cond_1152, L1_cond_P, L1_cond_W, L1_cond_b)
    x = _L2_cond_ref(x, cond_1152, L2_cond_w_adaln, L2_cond_b_adaln, L2_cond_w_qkv, L2_cond_b_qkv, L2_cond_w_proj, L2_cond_b_proj, L2_cond_w_gate, L2_cond_w1, L2_cond_b1, L2_cond_w2, L2_cond_b2)
    x = _L3_cond_ref(x, cond_1152, L3_cond_w_mod, L3_cond_b_mod, L3_cond_w_qkv, L3_cond_b_qkv, L3_cond_g_q, L3_cond_g_k, L3_cond_w_proj, L3_cond_b_proj, L3_cond_w1, L3_cond_b1, L3_cond_w2, L3_cond_b2)
    return x

_drawn_inputs = setup_inputs


def setup_inputs(seed=0):
    import zlib

    import numpy as np

    out = dict(_drawn_inputs(seed))
    spreads = {'L0_cond_b_qkv': (0.0, 0.8),
     'L0_cond_b_proj': (0.0, 0.335),
     'L0_cond_b_fc1': (0.0, 0.8),
     'L0_cond_b_fc2': (0.0, 0.357),
     'L0_cond_b_ada': (0.0, 0.385),
     'L2_cond_b_adaln': (0.0, 0.442),
     'L2_cond_b_qkv': (0.0, 0.8),
     'L2_cond_b_proj': (0.0, 0.325),
     'L2_cond_b1': (0.0, 0.8),
     'L2_cond_b2': (0.0, 0.467),
     'L3_cond_b_qkv': (0.0, 1.183),
     'L3_cond_g_q': (1.0, 0.6),
     'L3_cond_g_k': (1.0, 0.6),
     'L3_cond_b_proj': (0.0, 1.283),
     'L3_cond_b1': (0.0, 1.651),
     'L3_cond_b2': (0.0, 1.169)}
    factors = {'L0_cond_W_qkv': 8.0,
     'L0_cond_W_proj': 5.249,
     'L2_cond_w_qkv': 8.0,
     'L2_cond_w_proj': 5.324,
     'L2_cond_w_gate': 2.718,
     'L2_cond_w1': 2.683,
     'L3_cond_b_mod': 5.339}
    for name, (base, spread) in spreads.items():
        noise = np.random.default_rng([zlib.crc32(name.encode()), seed]).standard_normal(out[name].shape)
        drawn = base * np.exp(spread * noise) if base else spread * noise
        out[name] = jnp.asarray(drawn.astype(out[name].dtype))
    for name, factor in factors.items():
        out[name] = (out[name] * factor).astype(out[name].dtype)
    return out
```

```python
from contextlib import ExitStack

import concourse.bass as bass
from concourse import mybir

F32 = mybir.dt.float32
F32R = mybir.dt.float32r
BF16 = mybir.dt.bfloat16
ALU = mybir.AluOpType
ACT = mybir.ActivationFunctionType
AX_X = mybir.AxisListType.X

P = 128
B, L, C = 2, 1024, 288
H = 16
D = C // H
TB = L // P
NT = B * TB
R = C - 2 * P
RS = 3 * R
RA = RS + 2
SLAB = (P, P, RS)
XN = 2 * P + RA
FF = 4 * C
NF = FF // P
EXPERTS = 4
RK = 64
QR_P, QR_T = 96, 3
PARTS = 6
KD = PARTS * D
KA = KD + 3
SW = 112
G = H // 4
SCALE = float(D) ** -0.5
EPS = 1e-6
CREDIT = 64
SQUARINGS = 20
TAYLOR = 12


class Signal:

    def __init__(self, sem):
        self.sem = sem
        self.base = CREDIT

    def at(self, n):
        return self.base + n

    def passed(self, n):
        self.base += n


class Chain:

    def __init__(self, eng, counted):
        self.eng, self.counted, self.n = eng, counted, 0

    def __call__(self, ins):
        self.n += 1
        ins.then_inc(self.counted.sem, 1)
        self.eng.wait_ge(self.counted.sem, self.counted.at(self.n))
        return self.n


def build(nc, x_in, out, w, upto=99, tap=None):
    top = ExitStack()
    with top:
        used = {}

        def fresh(name):
            used[name] = used.get(name, 0) + 1
            return name if used[name] == 1 else f"{name}_{used[name]}"

        def sb(name, shape, dt=F32, ctx=top):
            name = fresh(name)
            return ctx.enter_context(nc.sbuf_tensor(name, shape, dt))

        def bank(name, ctx, shape=(P, 512), dt=F32):
            return ctx.enter_context(nc.psum_tensor(fresh(name), list(shape), dt))

        signals = []

        def signal(name):
            s = Signal(top.enter_context(nc.semaphore(name)))
            signals.append(s)
            return s

        loaded = signal("loaded")
        stored = signal("stored")
        max_rows_in = signal("max_rows_in")
        dve_done = signal("dve_done")
        act_done = signal("act_done")
        pe_done = signal("pe_done")
        pool_done = signal("pool_done")
        stats_in = signal("stats_in")
        std_ready = signal("std_ready")
        rstd_ready = signal("rstd_ready")
        normed = signal("normed")
        turned = signal("turned")
        modulated = signal("modulated")
        hi_ready = signal("hi_ready")
        split_done = signal("split_done")
        qkv_ready = signal("qkv_ready")
        qkv_taken = signal("qkv_taken")
        qk_step = signal("qk_step")
        qk_std = signal("qk_std")
        qk_split = signal("qk_split")
        t_filled = signal("t_filled")
        t_taken = signal("t_taken")
        rowscores = signal("rowscores")
        rowmax = signal("rowmax")
        colscores = signal("colscores")
        probs = signal("probs")
        weighed = signal("weighed")
        o_copied = signal("o_copied")
        o_normed = signal("o_normed")
        inv_ready = signal("inv_ready")
        max_step = signal("max_step")
        v_staged = signal("v_staged")
        mm_done = signal("mm_done")
        gated = signal("gated")
        added = signal("added")
        up_ready = signal("up_ready")
        gelu_done = signal("gelu_done")
        g_hi = signal("g_hi")
        g_split = signal("g_split")
        w_step = signal("w_step")
        qr_col = signal("qr_col")
        qr_dots = signal("qr_dots")
        qr_copy = signal("qr_copy")
        qr_step = signal("qr_step")

        x = sb("x", [P, NT, C])
        stats = sb("stats", [P, NT, 6])
        mv = sb("mv", [P, NT, 2])
        std = sb("std", [P, NT])
        rstd = sb("rstd", [P, NT])
        modc = sb("modc", [P, 3, 4, 3, B])
        gate_b = sb("gate_b", [P, 3, 2, B, C])
        ident = sb("ident", [P, P])
        identb = sb("identb", [P, P], BF16)
        m_rot = sb("m_rot", [P, B, 3, C])
        cw = sb("cw", [P, NT, EXPERTS])
        eps_col = sb("eps_col", [P, 1])
        mix = sb("mix", [P, 4])
        sel_den = sb("sel_den", [P, P])

        with nc.Block() as block:
            @block.gpsimd
            def _(pool):
                for s in signals:
                    pool.nop().then_inc(s.sem, CREDIT)
                pool.memset(eps_col[:, :], EPS)

        def modulation():
            with ExitStack() as ctx:
                wa = sb("wa", [P, 3, 3, 6 * C], ctx=ctx)
                condT = sb("condT", [P, 3, B], ctx=ctx)
                sT = sb("sT", [P, 3, B], ctx=ctx)
                sTb = sb("sTb", [P, 3, B, P], ctx=ctx)
                bias_c = sb("bias_c", [P, 3, 4, 3], ctx=ctx)
                bias_g = sb("bias_g", [P, 3, 2, C], ctx=ctx)
                col_ps = bank("col_ps", ctx, (P, 3, 4, 3, 8))
                gate_ps = bank("gate_ps", ctx, (P, 4, 512))
                KROWS = (P, P, R)
                n_load = 0
                with nc.Block() as block:
                    @block.sync
                    def _(sp):
                        nonlocal n_load

                        def load(dst, src):
                            nonlocal n_load
                            sp.dma_start(dst, src).then_inc(loaded.sem, 16)
                            n_load += 1

                        for s in range(3):
                            load(condT[0:KROWS[s], s, :], w["condT"][s * P:s * P + KROWS[s], :])
                        load(ident[:, :], w["const_ident"])
                        load(mix[:, :], w["const_mix"])
                        load(sel_den[:, :], w["const_sel"])
                        load(x[:, :, :], x_in.rearrange("b (t p) c -> p (b t) c", p=P))
                        for l in range(3):
                            wd, bd = w["ada_w"][l], w["ada_b"][l]
                            for s in range(3):
                                load(wa[0:KROWS[s], l, s, :], wd[s * P:s * P + KROWS[s], :])
                            for gi, six in enumerate((2, 5)):
                                load(bias_g[:, l, gi, :],
                                     bd[six * C:six * C + C].rearrange("(o c) -> o c", o=1).broadcast_to([P, C]))
                            for ki, six in enumerate((0, 1, 3, 4)):
                                for s in range(2):
                                    load(bias_c[:, l, ki, s:s + 1],
                                         bd[six * C + s * P:six * C + s * P + P].rearrange("(c o) -> c o", o=1))
                                for r in range(3):
                                    load(bias_c[R * r:R * r + R, l, ki, 2:3],
                                         bd[six * C + 2 * P:six * C + C].rearrange("(c o) -> c o", o=1))

                    ALL = n_load

                    @block.scalar
                    def _(act):
                        act.wait_ge(loaded.sem, loaded.at(16 * ALL))
                        for s in range(3):
                            act.activation(sT[0:KROWS[s], s, :], condT[0:KROWS[s], s, :], ACT.Silu).then_inc(
                                act_done.sem, 1)

                    @block.gpsimd
                    def _(pool):
                        pool.memset(modc[:, :, :, :, :], 0.0).then_inc(pool_done.sem, 1)
                        pool.wait_ge(pool_done.sem, pool_done.at(1))
                        for ki in (1, 3):
                            pool.memset(modc[:, :, ki, :, :], 1.0).then_inc(pool_done.sem, 1)
                        pool.memset(cw[:, :, :], 1.0).then_inc(pool_done.sem, 1)

                    @block.tensor
                    def _(pe):
                        pe.wait_ge(dve_done.sem, dve_done.at(3))
                        for l in range(3):
                            for ki, six in enumerate((0, 1, 3, 4)):
                                for s in range(3):
                                    for r in range(3 if s == 2 else 1):
                                        n = R if s == 2 else P
                                        for kt in range(3):
                                            K = KROWS[kt]
                                            pe.matmul(col_ps[R * r:R * r + n, l, ki, s, 0:B],
                                                      wa[0:K, l, kt, six * C + s * P:six * C + s * P + n],
                                                      sT[0:K, kt, :], start=kt == 0, stop=kt == 2)
                            for gi, six in enumerate((2, 5)):
                                for b in range(B):
                                    n = 2 * gi + b
                                    if l > 0 and n == 0:
                                        pe.wait_ge(dve_done.sem, dve_done.at(4 + 4 * l))
                                    for kt in range(3):
                                        K = KROWS[kt]
                                        mm = pe.matmul(gate_ps[:, n, 0:C], sTb[0:K, kt, b, :],
                                                       wa[0:K, l, kt, six * C:six * C + C],
                                                       start=kt == 0, stop=kt == 2)
                            mm.then_inc(pe_done.sem, 1)

                    @block.vector
                    def _(dve):
                        dve.wait_ge(act_done.sem, act_done.at(3))
                        for s in range(3):
                            K = KROWS[s]
                            dve.tensor_copy(sTb[0:K, s, :, :],
                                            sT[0:K, s, :].unsqueeze(2).broadcast_to([K, B, P])).then_inc(dve_done.sem, 1)
                        dve.tensor_copy(identb[:, :], ident[:, :]).then_inc(dve_done.sem, 1)
                        for l in range(3):
                            dve.wait_ge(pe_done.sem, pe_done.at(l + 1))
                            for gi in range(2):
                                for b in range(B):
                                    dve.tensor_tensor(gate_b[:, l, gi, b, :], gate_ps[:, 2 * gi + b, 0:C],
                                                      bias_g[:, l, gi, :], ALU.add).then_inc(dve_done.sem, 1)
                        dve.wait_ge(pool_done.sem, pool_done.at(4))
                        for l in range(3):
                            for ki in range(4):
                                for s in range(3):
                                    n = SLAB[s]
                                    dve.tensor_scalar(modc[0:n, l, ki, s, :], col_ps[0:n, l, ki, s, 0:B],
                                                      bias_c[0:n, l, ki, s:s + 1], float(ki % 2), ALU.add, ALU.add
                                                      ).then_inc(dve_done.sem, 1)
                        for t in range(NT):
                            dve.bn_stats(stats[:, t, :], x[:, t, :]).then_inc(dve_done.sem, 1)
                loaded.passed(16 * ALL)
                act_done.passed(3)
                pool_done.passed(4)
                pe_done.passed(3)
                dve_done.passed(4 + 12 + 36 + NT)

        def rotation():
            with ExitStack() as ctx:
                z = sb("z", [QR_P, QR_T, RK], ctx=ctx)
                row_mask = sb("row_mask", [QR_P, QR_T, RK], ctx=ctx)
                v = sb("v", [QR_P, QR_T], ctx=ctx)
                e = sb("e", [QR_P, 1], ctx=ctx)
                vb = sb("vb", [QR_P, QR_T + 1, QR_P], ctx=ctx)
                ya = sb("ya", [QR_P, 2, RK], ctx=ctx)
                small = sb("small", [QR_P, 8], ctx=ctx)
                wr = sb("wr", [QR_P, RK], ctx=ctx)
                dots = bank("dots", ctx)
                two = bank("two", ctx)
                wide = bank("wide", ctx)
                wide2 = bank("wide2", ctx)
                with nc.Block() as block:
                    @block.sync
                    def _(sp):
                        sp.dma_start(z[:, :, :], w["rot_P"].rearrange("(t p) d -> p t d", p=QR_P)).then_inc(loaded.sem, 16)
                        sp.dma_start(row_mask[:, :, :], w["const_rows"].rearrange("(t p) d -> p t d", p=QR_P)
                                     ).then_inc(loaded.sem, 16)

                    @block.vector
                    def _(dve):
                        dve.wait_ge(loaded.sem, loaded.at(32))
                        with dve.Fori(0, RK) as j:
                            STEPS = 11

                            def chain(ins, k):
                                ins.then_inc(qr_step.sem, 1)
                                dve.wait_ge(qr_step.sem, qr_step.at(STEPS * j + k))

                            chain(dve.tensor_tensor(v[:, :], z[:, :, bass.ds(j, 1)].rearrange("p t o -> p (t o)"),
                                                    row_mask[:, :, bass.ds(j, 1)].rearrange("p t o -> p (t o)"),
                                                    ALU.mult), 1)
                            dve.tensor_copy(vb[:, 0:QR_T, :], v[:, :].unsqueeze(2).broadcast_to([QR_P, QR_T, QR_P]))
                            dve.tensor_copy(e[:, :], ident[0:QR_P, bass.ds(j, 1)])
                            dve.tensor_copy(vb[:, QR_T, :], ident[0:QR_P, bass.ds(j, 1)].broadcast_to([QR_P, QR_P])
                                            ).then_inc(qr_col.sem, 1)
                            dve.wait_ge(qr_copy.sem, qr_copy.at(2 * j + 2))
                            alpha = ya[:, 1, bass.ds(j, 1)]
                            norm2 = ya[:, 0, bass.ds(j, 1)]
                            chain(dve.tensor_scalar(small[:, 1:2], alpha, 0.0, 2.0, ALU.is_ge, ALU.mult), 2)
                            chain(dve.scalar_tensor_tensor(small[:, 2:3], small[:, 1:2], -1.0, small[:, 0:1],
                                                           ALU.add, ALU.mult), 3)
                            chain(dve.scalar_tensor_tensor(small[:, 3:4], alpha, small[:, 2:3], norm2,
                                                           ALU.mult, ALU.add), 4)
                            chain(dve.tensor_scalar(small[:, 4:5], small[:, 3:4], 1e-37, None, ALU.max), 5)
                            chain(dve.reciprocal(small[:, 5:6], small[:, 4:5]), 6)
                            chain(dve.scalar_tensor_tensor(wr[:, :], ya[:, 1, :], small[:, 2:3], ya[:, 0, :],
                                                           ALU.mult, ALU.add), 7)
                            chain(dve.scalar_tensor_tensor(v[:, 0:1], e[:, :], small[:, 2:3], v[:, 0:1],
                                                           ALU.mult, ALU.add), 8)
                            chain(dve.tensor_scalar(wr[:, :], wr[:, :], small[:, 5:6], -1.0, ALU.mult, ALU.mult), 9)
                            for t in range(QR_T):
                                ins = dve.scalar_tensor_tensor(z[:, t, :], wr[:, :], v[:, t:t + 1], z[:, t, :],
                                                               ALU.mult, ALU.add)
                                if t == 1:
                                    ins.then_inc(qr_step.sem, 1)
                            chain(ins, 11)

                    @block.tensor
                    def _(pe):
                        with pe.Fori(0, RK) as j:
                            pe.wait_ge(qr_col.sem, qr_col.at(j + 1))
                            pe.wait_ge(qr_copy.sem, qr_copy.at(2 * j))
                            for t in range(QR_T):
                                pe.matmul(dots[0:QR_P, 0:RK], vb[:, t, :], z[:, t, :], start=t == 0, stop=t == QR_T - 1)
                            pe.matmul(dots[0:QR_P, RK:2 * RK], vb[:, QR_T, :], z[:, 0, :], start=True, stop=True
                                      ).then_inc(qr_dots.sem, 1)

                    @block.scalar
                    def _(act):
                        act.preload_act_table(ACT.Sqrt)
                        with act.Fori(0, RK) as j:
                            act.wait_ge(qr_dots.sem, qr_dots.at(j + 1))
                            act.activation(ya[:, :, :].rearrange("p a b -> p (a b)"), dots[0:QR_P, 0:2 * RK], ACT.Copy
                                           ).then_inc(qr_copy.sem, 1)
                            act.activation(small[:, 0:1], dots[0:QR_P, bass.ds(j, 1)], ACT.Sqrt).then_inc(qr_copy.sem, 1)
                loaded.passed(32)
                qr_step.passed(11 * RK)
                qr_col.passed(RK)
                qr_dots.passed(RK)
                qr_copy.passed(2 * RK)

                INV = 6
                KROWS = (P, P, R)
                tri = sb("tri", [RK, 2, RK], ctx=ctx)
                pT = sb("pT", [RK, C], ctx=ctx)
                uT = sb("uT", [RK, C], ctx=ctx)
                power = sb("power", [RK, 2, RK], ctx=ctx)
                prod = sb("prod", [RK, RK], ctx=ctx)
                tmp = sb("tmp", [RK, RK], ctx=ctx)
                s1 = sb("s1", [RK, 8], ctx=ctx)
                wv = sb("wv", [P, 3, 8, 512], ctx=ctx)
                bias_v = sb("bias_v", [B, 8, 512], ctx=ctx)
                vrow = sb("vrow", [B, 8, 512], ctx=ctx)
                skew = sb("skew", [RK, B, 2, RK], ctx=ctx)
                up = sb("up", [RK, B, RK], ctx=ctx)
                term = sb("term", [RK, B, 2, RK], ctx=ctx)
                sq = sb("sq", [RK, B, 2, RK], ctx=ctx)
                kept = sb("kept", [RK, B, 2, RK], ctx=ctx)
                absA = sb("absA", [RK, B, RK], ctx=ctx)
                rs = sb("rs", [RK, B], ctx=ctx)
                big = sb("big", [B, 1], ctx=ctx)
                bigd = sb("bigd", [B, B], ctx=ctx)
                onesr = sb("onesr", [B, RK], ctx=ctx)
                nrm = sb("nrm", [RK, B], ctx=ctx)
                pw = sb("pw", [RK, 3, SQUARINGS], ctx=ctx)
                gt = sb("gt", [RK, B, SQUARINGS], ctx=ctx)
                ngt = sb("ngt", [RK, B, SQUARINGS], ctx=ctx)
                sf = sb("sf", [RK, B, SQUARINGS], ctx=ctx)
                sc = sb("sc", [RK, B], ctx=ctx)
                g_u = sb("g_u", [RK, B, C], ctx=ctx)
                condT = sb("condT2", [P, 3, B], ctx=ctx)
                NL = 3 + 2 * 3 + B
                HORNER = TAYLOR - 1
                mark = {}
                eye4 = tri[:, 1, :].unsqueeze(1).broadcast_to([RK, 2 * B, RK])
                sk4 = skew[:, :, :, :].rearrange("p b s c -> p (b s) c")
                tm4 = term[:, :, :, :].rearrange("p b s c -> p (b s) c")
                sq4 = sq[:, :, :, :].rearrange("p b s c -> p (b s) c")
                two4 = two[0:RK, 0:2 * B * RK].rearrange("p (a c) -> p a c", a=2 * B)

                with nc.Block() as block:
                    @block.vector
                    def _(dve):
                        step = Chain(dve, dve_done)
                        products = 0

                        def product():
                            nonlocal products
                            products += 1
                            dve.wait_ge(pe_done.sem, pe_done.at(products))

                        dve.wait_ge(loaded.sem, loaded.at(16 * NL))
                        for c in range(8):
                            product()
                            mark["row", c] = step(dve.tensor_tensor(vrow[:, c, :], (wide if c % 2 == 0 else wide2)[0:B, :],
                                                                    bias_v[:, c, :], ALU.add))
                        dve.wait_ge(loaded.sem, loaded.at(16 * (NL + B)))
                        product()
                        tr = two[0:RK, 0:B * RK].rearrange("p (b c) -> p b c", b=B)
                        step(dve.tensor_tensor(skew[:, :, 0, :], up[:, :, :], tr, ALU.subtract))
                        step(dve.tensor_scalar(skew[:, :, 1, :], skew[:, :, 0, :], -1.0, None, ALU.mult))
                        step(dve.tensor_tensor(absA[:, :, :], skew[:, :, 0, :], skew[:, :, 1, :], ALU.max))
                        step(dve.tensor_reduce(rs[:, :], absA[:, :, :], AX_X, ALU.add))
                        mark["sums"] = step(dve.memset(onesr[:, :], 1.0))
                        product()
                        step(dve.tensor_reduce(big[:, :], wide[0:B, 0:RK], AX_X, ALU.max))
                        mark["norm"] = step(dve.tensor_scalar(bigd[:, :], ident[0:B, 0:B], big[:, 0:1], None, ALU.mult))
                        product()
                        step(dve.tensor_copy(nrm[:, :], wide2[0:RK, 0:B]))
                        for b in range(B):
                            step(dve.tensor_scalar(gt[:, b, :], pw[:, 0, :], nrm[:, b:b + 1], None, ALU.is_lt))
                        step(dve.tensor_scalar(ngt[:, :, :], gt[:, :, :], -1.0, 1.0, ALU.mult, ALU.add))
                        step(dve.tensor_tensor(sf[:, :, :], gt[:, :, :],
                                               pw[:, 1, :].unsqueeze(1).broadcast_to([RK, B, SQUARINGS]), ALU.mult))
                        step(dve.tensor_reduce(sc[:, :], sf[:, :, :], AX_X, ALU.min))
                        step(dve.tensor_scalar(sc[:, :], sc[:, :], 1.0, None, ALU.add))
                        for b in range(B):
                            step(dve.tensor_scalar(skew[:, b, :, :], skew[:, b, :, :], sc[:, b:b + 1], None, ALU.mult))
                        step(dve.tensor_scalar(sq4, sk4, 1.0 / TAYLOR, None, ALU.mult))
                        mark["first"] = step(dve.tensor_tensor(tm4, sq4, eye4, ALU.add))
                        with dve.Fori(0, HORNER) as i:
                            dve.wait_ge(up_ready.sem, up_ready.at(i + 1))
                            dve.tensor_scalar(sq4, two4, pw[:, 2, bass.ds(i, 1)], None, ALU.mult).then_inc(g_hi.sem, 1)
                            dve.wait_ge(g_hi.sem, g_hi.at(i + 1))
                            dve.tensor_tensor(tm4, sq4, eye4, ALU.add).then_inc(g_split.sem, 1)
                        dve.wait_ge(g_split.sem, g_split.at(HORNER))
                        with dve.Fori(0, SQUARINGS) as i:
                            for b in range(B):
                                dve.tensor_scalar(kept[:, b, :, :], term[:, b, :, :], ngt[:, b, bass.ds(i, 1)], None,
                                                  ALU.mult).then_inc(modulated.sem, 1)
                            dve.wait_ge(modulated.sem, modulated.at(2 * i + 2))
                            dve.wait_ge(mm_done.sem, mm_done.at(i + 1))
                            for b in range(B):
                                ins = dve.scalar_tensor_tensor(
                                    term[:, b, :, :], two[0:RK, 2 * b * RK:(2 * b + 2) * RK].rearrange("p (s c) -> p s c", s=2),
                                    gt[:, b, bass.ds(i, 1)], kept[:, b, :, :], ALU.mult, ALU.add)
                            ins.then_inc(added.sem, 1)
                            dve.wait_ge(added.sem, added.at(i + 1))
                        step(dve.tensor_tensor(tm4, tm4, eye4, ALU.subtract))

                        step(dve.tensor_tensor(tmp[:, :], z[0:RK, 0, :], tri[:, 1, :], ALU.mult))
                        step(dve.tensor_reduce(s1[:, 0:1], tmp[:, :], AX_X, ALU.add))
                        step(dve.reciprocal(s1[:, 1:2], s1[:, 0:1]))
                        step(dve.tensor_tensor(tmp[:, :], z[0:RK, 0, :], tri[:, 0, :], ALU.mult))
                        step(dve.tensor_scalar(power[:, 0, :], tmp[:, :], s1[:, 1:2], -1.0, ALU.mult, ALU.mult))
                        mark["power", 0] = step(dve.tensor_tensor(prod[:, :], power[:, 0, :], tri[:, 1, :], ALU.add))
                        product()
                        mark["turned"] = step(dve.tensor_copy(power[:, 1, :], wide[0:RK, 0:RK]))
                        for k in range(1, INV):
                            product()
                            mark["power", k] = step(dve.tensor_copy(power[:, :, :].rearrange("p a c -> p (a c)"),
                                                                    wide[0:RK, 0:2 * RK]))
                            product()
                            mark["prod", k] = step(dve.tensor_tensor(prod[:, :], wide2[0:RK, 0:RK], prod[:, :], ALU.add))
                        product()
                        mark["uT"] = step(dve.tensor_scalar(uT[:, :], wide2[0:RK, 0:C], s1[:, 1:2], None, ALU.mult))
                        product()
                        for b in range(B):
                            mark["g", b] = step(dve.tensor_copy(g_u[:, b, :], (wide if b == 0 else wide2)[0:RK, 0:C]))
                        for i in range(3 * B):
                            K = KROWS[i % 3]
                            product()
                            mark["m", i] = step(dve.tensor_copy(m_rot[0:K, i // 3, i % 3, :],
                                                                (wide if i % 2 == 0 else wide2)[0:K, 0:C]))
                        mark["steps"] = step.n
                        mark["products"] = products

                    @block.sync
                    def _(sp):
                        def load(dst, src):
                            sp.dma_start(dst, src).then_inc(loaded.sem, 16)
                        load(tri[:, :, :], w["const_tri"])
                        load(pT[:, :], w["rot_PT"])
                        load(pw[:, :, :], w["const_pow"])
                        for s in range(3):
                            load(condT[0:KROWS[s], s, :], w["condT"][s * P:s * P + KROWS[s], :])
                            load(wv[0:KROWS[s], s, :, :].rearrange("p a b -> p (a b)"), w["rot_W"][s * P:s * P + KROWS[s], :])
                        for b in range(B):
                            load(bias_v[b:b + 1, :, :].rearrange("p a b -> p (a b)"), w["rot_b"])
                        sp.wait_ge(dve_done.sem, dve_done.at(mark["row", 7]))
                        for b in range(B):
                            load(up[:, b, :], vrow[b:b + 1, :, :].rearrange("o a b -> o (a b)").rearrange(
                                "o (i j) -> o i j", j=RK))

                    @block.scalar
                    def _(act):
                        act.wait_ge(loaded.sem, loaded.at(16 * NL))
                        for s in range(3):
                            act.activation(condT[0:KROWS[s], s, :], condT[0:KROWS[s], s, :], ACT.Silu).then_inc(
                                act_done.sem, 1)

                    @block.tensor
                    def _(pe):
                        def after(name):
                            pe.wait_ge(dve_done.sem, dve_done.at(mark[name]))

                        def done(ins):
                            ins.then_inc(pe_done.sem, 1)

                        pe.wait_ge(act_done.sem, act_done.at(3))
                        for c in range(8):
                            if c > 1:
                                after(("row", c - 2))
                            for kt in range(3):
                                K = KROWS[kt]
                                mm = pe.matmul((wide if c % 2 == 0 else wide2)[0:B, :], condT[0:K, kt, :], wv[0:K, kt, c, :],
                                               start=kt == 0, stop=kt == 2)
                            done(mm)
                        pe.wait_ge(loaded.sem, loaded.at(16 * (NL + B)))
                        for b in range(B):
                            mm = pe.transpose(two[0:RK, b * RK:(b + 1) * RK], up[:, b, :], ident[0:RK, 0:RK])
                        done(mm)
                        after("sums")
                        done(pe.transpose(wide[0:B, 0:RK], rs[:, :], ident[0:RK, 0:RK]))
                        after("norm")
                        done(pe.matmul(wide2[0:RK, 0:B], onesr[:, :], bigd[:, :], start=True, stop=True))
                        after("first")

                        def four(left):
                            for b in range(B):
                                for s in (1, 0):
                                    o = (2 * b + s) * RK
                                    if b == 0 and s == 1:
                                        pe.matmul(two[:, o:o + RK], left[:, b, :, :].rearrange("p s c -> p (s c)"),
                                                  term[:, b, s, :], start=True, stop=True)
                                        continue
                                    mm = pe.matmul(two[0:RK, o:o + RK], left[:, b, 1 - s, :], term[:, b, s, :],
                                                   start=True, stop=True)
                            return mm

                        with pe.Fori(0, HORNER) as i:
                            pe.wait_ge(g_split.sem, g_split.at(i))
                            four(skew).then_inc(up_ready.sem, 1)
                        pe.wait_ge(g_split.sem, g_split.at(HORNER))
                        with pe.Fori(0, SQUARINGS) as i:
                            pe.wait_ge(added.sem, added.at(i))
                            four(term).then_inc(mm_done.sem, 1)
                        after(("power", 0))
                        done(pe.transpose(wide[0:RK, 0:RK], power[:, 0, :], ident[0:RK, 0:RK]))
                        after("turned")
                        for k in range(1, INV):
                            pe.matmul(wide[0:RK, 0:RK], power[:, 1, :], power[:, 0, :], start=True, stop=True)
                            done(pe.matmul(wide[0:RK, RK:2 * RK], power[:, 0, :], power[:, 1, :], start=True, stop=True))
                            after(("power", k))
                            done(pe.matmul(wide2[0:RK, 0:RK], power[:, 1, :], prod[:, :], start=True, stop=True))
                            after(("prod", k))
                        done(pe.matmul(wide2[0:RK, 0:C], prod[:, :], pT[:, :], start=True, stop=True))
                        after("uT")
                        for b in range(B):
                            mm = pe.matmul((wide if b == 0 else wide2)[0:RK, 0:C], term[:, b, 1, :], uT[:, :],
                                           start=True, stop=True)
                        done(mm)
                        after(("g", 1))
                        for i in range(3 * B):
                            if i > 1:
                                after(("m", i - 2))
                            K, s = KROWS[i % 3], i % 3
                            done(pe.matmul((wide if i % 2 == 0 else wide2)[0:K, 0:C], uT[:, s * P:s * P + K],
                                           g_u[:, i // 3, :], start=True, stop=True))
                loaded.passed(16 * (NL + B))
                act_done.passed(3)
                dve_done.passed(mark["steps"])
                pe_done.passed(mark["products"])
                for s in (up_ready, g_hi, g_split):
                    s.passed(HORNER)
                modulated.passed(2 * SQUARINGS)
                mm_done.passed(SQUARINGS)
                added.passed(SQUARINGS)

        def split_weights(block, ctx, name, width, w_dram, bias_dram, hi, lo, third, n_load, raw, cols=None):
            tail = sb(name + "_tail", [RA, width], ctx=ctx)
            given = cols or width
            loads = 5 if bias_dram is None else 7

            @block.sync
            def _(sp):
                if bias_dram is None:
                    sp.wait_ge(pool_done.sem, pool_done.at(1))
                for s in range(2):
                    sp.dma_start(raw[:, s, 0:given], w_dram[s * P:s * P + P, :]).then_inc(loaded.sem, 16)
                for r in range(3):
                    sp.dma_start(raw[R * r:R * r + R, 2, 0:given], w_dram[2 * P:C, :]).then_inc(loaded.sem, 16)
                for r in range(2 if bias_dram is not None else 0):
                    sp.dma_start(raw[RS + r:RS + r + 1, 2, 0:width], bias_dram).then_inc(loaded.sem, 16)

            @block.vector
            def _(dve):
                step = Chain(dve, w_step)
                dve.wait_ge(loaded.sem, loaded.at(16 * loads))
                step(dve.tensor_copy(hi[:, :, :], raw[:, 0:2, 0:width]))
                dve.tensor_tensor(lo[:, :, :], raw[:, 0:2, 0:width], hi[:, :, :].bitcast(F32), ALU.subtract)
                step(dve.tensor_copy(third[0:RA, :], raw[0:RA, 2, 0:width]))
                step(dve.tensor_tensor(tail[:, :], raw[0:RA, 2, 0:width], third[0:RA, :].bitcast(F32), ALU.subtract))
                step(dve.tensor_scalar(tail[:, :], tail[:, :], mix[0:RA, 1:2], None, ALU.mult))
                step(dve.scalar_tensor_tensor(third[0:RA, :], third[0:RA, :].bitcast(F32), mix[0:RA, 0:1], tail[:, :],
                                              ALU.mult, ALU.add))
            return 5

        def deviations(dve, act, tiles):
            t0, t1 = tiles
            if dve is not None:
                for t in range(t0, t1):
                    dve.bn_aggr(mv[:, t, :], stats[:, t, :]).then_inc(stats_in.sem, 1)
                dve.wait_ge(std_ready.sem, std_ready.at(1))
                dve.reciprocal(rstd[:, t0:t1], std[:, t0:t1]).then_inc(rstd_ready.sem, 1)
                dve.wait_ge(rstd_ready.sem, rstd_ready.at(1))
            if act is not None:
                act.preload_act_table(ACT.Sqrt)
                act.wait_ge(stats_in.sem, stats_in.at(t1 - t0))
                act.activation(std[:, t0:t1], mv[:, t0:t1, 1], ACT.Sqrt, bias=eps_col[:, 0:1]).then_inc(std_ready.sem, 1)

        def norm_stages(ctx, l, ki, xn, m, turn_ps, hi_at, lo_at, third_at, reused):

            def normalise(dve, t, tile, k):
                dve.wait_ge(turned.sem, turned.at(t - 1))
                dve.tensor_scalar(xn[:, k, 0:2 * P], x[:, tile, 0:2 * P], mv[:, tile, 0:1], rstd[:, bass.ds(tile, 1)], ALU.subtract, ALU.mult)
                dve.tensor_scalar(xn[:, k, 2 * P:2 * P + RS].rearrange("p (r c) -> p r c", r=3),
                                  x[:, tile, 2 * P:C].unsqueeze(1).broadcast_to([P, 3, R]), mv[:, tile, 0:1],
                                  rstd[:, bass.ds(tile, 1)],
                                  ALU.subtract, ALU.mult).then_inc(normed.sem, 1)

            def turn(pe, t, k):
                pe.wait_ge(normed.sem, normed.at(t + 1))
                pe.wait_ge(modulated.sem, modulated.at(t - 1))
                for s in range(3):
                    n = RA if s == 2 else P
                    mm = pe.transpose(turn_ps[k][0:n, s * P:s * P + P], xn[:, k, s * P:s * P + n], ident[:, :])
                mm.then_inc(turned.sem, 1)

            def modulate(act, t, b, k):
                act.wait_ge(turned.sem, turned.at(t + 1))
                act.wait_ge(split_done.sem, split_done.at(t - 1))
                for s in range(3):
                    n = RA if s == 2 else P
                    a = act.activation(m[0:n, k, s, :], turn_ps[k][0:n, s * P:s * P + P], ACT.Identity,
                                       scale=modc[0:n, l, ki + 1, s, b:b + 1], bias=modc[0:n, l, ki, s, b:b + 1])
                a.then_inc(modulated.sem, 1)

            def split(dve, t, k):
                dve.wait_ge(modulated.sem, modulated.at(t + 1))
                if reused:
                    dve.wait_ge(qkv_ready.sem, qkv_ready.at(t - 1))
                hi, lo, third = hi_at(t, k), lo_at(t, k), third_at(t, k)
                dve.tensor_copy(hi, m[:, k, 0:2, :])
                dve.tensor_copy(third[0:RA], m[0:RA, k, 2, :]).then_inc(hi_ready.sem, 1)
                dve.wait_ge(hi_ready.sem, hi_ready.at(t + 1))
                dve.tensor_tensor(lo, m[:, k, 0:2, :], hi.bitcast(F32), ALU.subtract)
                dve.tensor_tensor(third[R:2 * R], m[R:2 * R, k, 2, :], third[R:2 * R].bitcast(F32), ALU.subtract
                                  ).then_inc(split_done.sem, 1)
            return normalise, turn, modulate, split

        def split_products(pe, out_ap, lhs, rhs):
            (lh, ll, l3), (rh, rl, r3) = lhs, rhs
            n = 0
            for s in range(2):
                for a, b in ((lh, rh), (lh, rl), (ll, rh)):
                    pe.matmul(out_ap, a(s), b(s), start=n == 0, stop=False)
                    n += 1
            return pe.matmul(out_ap, l3, r3, start=False, stop=True)

        def qkv_phase(l, b, first, wq, stack, val):
            wh, wl, w3 = wq
            with ExitStack() as ctx:
                n_load = 0
                xn = sb(f"xn{l}{b}", [P, 2, XN], ctx=ctx)
                m = sb(f"m{l}{b}", [P, 2, 3, P], ctx=ctx)
                ph = sb(f"ph{l}{b}", [P, 2, 2, P], F32R, ctx=ctx)
                pl = sb(f"pl{l}{b}", [P, 2, 2, P], F32R, ctx=ctx)
                p3 = sb(f"p3{l}{b}", [RA, 2, P], F32R, ctx=ctx)
                qk = sb(f"qk{l}{b}", [P, 2, 2, H, D], ctx=ctx)
                rem = sb(f"rem{l}{b}", [P, 2, H, D], ctx=ctx)
                turn_ps = [bank(f"turn{l}{b}{k}", ctx) for k in range(2)]
                qkv_ps = [[bank(f"qkv{l}{b}{k}{n}", ctx) for n in range(3)] for k in range(2)]
                is3 = l == 2
                if is3:
                    cen = sb(f"cen{b}", [P, 2 * H, D], ctx=ctx)
                    hs = sb(f"hs{b}", [P, 4, 2 * H], ctx=ctx)
                    gqk = sb(f"gqk{b}", [P, 2, D], ctx=ctx)
                steps_w = 0
                if first:
                    raw = sb(f"rawq{l}", [P, 3, 3 * C], ctx=ctx)
                    with nc.Block() as block:
                        steps_w = split_weights(block, ctx, f"wq{l}", 3 * C, w["qkv_w"][l], w["qkv_b"][l], wh, wl, w3, 0, raw)
                    loaded.passed(16 * 7)
                    w_step.passed(steps_w)
                normalise, turn, modulate, split = norm_stages(
                    ctx, l, 0, xn, m, turn_ps, lambda t, k: ph[:, k], lambda t, k: pl[:, k], lambda t, k: p3[:, k], True)

                with nc.Block() as block:
                    @block.sync
                    def _(sp):
                        if is3:
                            for n, g in enumerate((w["g_q"], w["g_k"])):
                                sp.dma_start(gqk[:, n, :], g.rearrange("(o c) -> o c", o=1).broadcast_to([P, D])
                                             ).then_inc(loaded.sem, 16)

                    @block.gpsimd
                    def _(pool):
                        pool.memset(xn[:, :, 2 * P + RS:XN], 1.0).then_inc(pool_done.sem, 1)
                        for t in range(TB):
                            pool.memset(stack[:, t, 1, :, KD:KA], 1.0).then_inc(pool_done.sem, 1)
                        pool.memset(val[:, :, :, D:D + 1], 1.0).then_inc(pool_done.sem, 1)
                        pool.memset(val[:, :, :, D + 1:32], 0.0).then_inc(pool_done.sem, 1)
                        with pool.Fori(0, TB) as t:
                            pool.wait_ge(qk_split.sem, qk_split.at(t + 1))

                            def slot(a, s):
                                return stack[:, t, a, :, s * D:(s + 1) * D]

                            pool.tensor_copy(slot(0, 3), slot(0, 0))
                            pool.tensor_copy(slot(0, 4), slot(0, 0))
                            pool.tensor_copy(slot(0, 5), slot(0, 1))
                            pool.tensor_copy(slot(1, 2), slot(1, 0))
                            pool.tensor_copy(slot(1, 5), slot(1, 0))
                            pool.tensor_copy(slot(1, 3), slot(1, 1))

                    def qkv(pe, t, k):
                        pe.wait_ge(split_done.sem, split_done.at(t + 1))
                        pe.wait_ge(qkv_taken.sem, qkv_taken.at(t - 1))
                        for n in range(3):
                            cols = slice(n * C, n * C + C)
                            mm = split_products(
                                pe, qkv_ps[k][n][:, 0:C],
                                (lambda s: ph[:, k, s, :], lambda s: pl[:, k, s, :], p3[0:RA, k, :]),
                                (lambda s: wh[:, s, cols], lambda s: wl[:, s, cols], w3[0:RA, cols]))
                        mm.then_inc(qkv_ready.sem, 1)

                    def take(act, t, k):
                        act.wait_ge(qkv_ready.sem, qkv_ready.at(t + 1))
                        act.wait_ge(qk_split.sem, qk_split.at(t - 1))
                        for n in range(2):
                            act.activation(qk[:, k, n, :, :].rearrange("p h d -> p (h d)"), qkv_ps[k][n][:, 0:C], ACT.Copy,
                                           scale=SCALE if n == 0 and not is3 else 1.0)
                        act.activation(val[:, t, :, 0:D], qkv_ps[k][2][:, 0:C].rearrange("p (h d) -> p h d", h=H),
                                       ACT.Copy).then_inc(qkv_taken.sem, 1)
                        if is3:
                            act.wait_ge(qk_step.sem, qk_step.at(11 * t + 5))
                            act.activation(hs[:, 2, :], hs[:, 1, :], ACT.Sqrt, scale=1.0 / D, bias=eps_col[:, 0:1]
                                           ).then_inc(qk_std.sem, 1)

                    per = 11 if is3 else 3

                    def parts(dve, t, k):
                        n = 0

                        def link(ins):
                            nonlocal n
                            n += 1
                            ins.then_inc(qk_step.sem, 1)
                            dve.wait_ge(qk_step.sem, qk_step.at(per * t + n))
                        dve.wait_ge(qkv_taken.sem, qkv_taken.at(t + 1))
                        both = qk[:, k, :, :, :].rearrange("p a h d -> p (a h) d")
                        if is3:
                            link(dve.tensor_reduce(hs[:, 0, :], both, AX_X, ALU.add))
                            link(dve.tensor_scalar(hs[:, 0, :], hs[:, 0, :], 1.0 / D, None, ALU.mult))
                            link(dve.tensor_tensor(both, both, hs[:, 0, :].unsqueeze(2).broadcast_to([P, 2 * H, D]),
                                                   ALU.subtract))
                            link(dve.tensor_tensor(cen[:, :, :], both, both, ALU.mult))
                            link(dve.tensor_reduce(hs[:, 1, :], cen[:, :, :], AX_X, ALU.add))
                            dve.wait_ge(qk_std.sem, qk_std.at(t + 1))
                            link(dve.reciprocal(hs[:, 3, :], hs[:, 2, :]))
                            link(dve.tensor_tensor(both, both, hs[:, 3, :].unsqueeze(2).broadcast_to([P, 2 * H, D]),
                                                   ALU.mult))
                            link(dve.tensor_tensor(qk[:, k, :, :, :].rearrange("p a h d -> p a h d"), qk[:, k, :, :, :],
                                                   gqk[:, :, :].unsqueeze(2).broadcast_to([P, 2, H, D]), ALU.mult))
                        src = qk[:, k, :, :, :]
                        def slot(a, s):
                            return stack[:, t, a, :, s * D:(s + 1) * D]
                        for a in range(2):
                            ins = dve.tensor_copy(slot(a, 0), src[:, a])
                        link(ins)
                        for a in range(2):
                            ins = dve.tensor_tensor(rem[:, a, :, :], src[:, a], slot(a, 0), ALU.subtract)
                        link(ins)
                        for a in range(2):
                            ins = dve.tensor_copy(slot(a, 1), rem[:, a, :, :])
                        link(ins)
                        dve.tensor_tensor(slot(0, 2), rem[:, 0, :, :], slot(0, 1), ALU.subtract)
                        dve.tensor_tensor(slot(1, 4), rem[:, 1, :, :], slot(1, 1), ALU.subtract).then_inc(qk_split.sem, 1)

                    @block.tensor
                    def _(pe):
                        turn(pe, 0, 0)
                        with pe.Fori(0, TB // 2 - 1) as i:
                            for k in range(2):
                                turn(pe, 2 * i + k + 1, 1 - k)
                                qkv(pe, 2 * i + k, k)
                        turn(pe, TB - 1, 1)
                        qkv(pe, TB - 2, 0)
                        qkv(pe, TB - 1, 1)

                    @block.scalar
                    def _(act):
                        if is3:
                            act.wait_ge(loaded.sem, loaded.at(32))
                        deviations(None, act, (TB * b, TB * b + TB))
                        modulate(act, 0, b, 0)
                        with act.Fori(0, TB // 2 - 1) as i:
                            for k in range(2):
                                modulate(act, 2 * i + k + 1, b, 1 - k)
                                take(act, 2 * i + k, k)
                        modulate(act, TB - 1, b, 1)
                        take(act, TB - 2, 0)
                        take(act, TB - 1, 1)

                    @block.vector
                    def _(dve):
                        if is3:
                            dve.wait_ge(loaded.sem, loaded.at(32))
                            dve.tensor_scalar(gqk[:, 0, :], gqk[:, 0, :], SCALE, None, ALU.mult).then_inc(w_step.sem, 1)
                            dve.wait_ge(w_step.sem, w_step.at(1))
                        dve.wait_ge(pool_done.sem, pool_done.at(TB + 3))
                        deviations(dve, None, (TB * b, TB * b + TB))

                        def both(t, tile, k):
                            normalise(dve, t, tile, k)
                            split(dve, t, k)
                        both(0, TB * b, 0)
                        with dve.Fori(0, TB // 2 - 1) as i:
                            for k in range(2):
                                both(2 * i + k + 1, 2 * i + (k + 1 + TB * b), 1 - k)
                                parts(dve, 2 * i + k, k)
                        both(TB - 1, TB * b + TB - 1, 1)
                        parts(dve, TB - 2, 0)
                        parts(dve, TB - 1, 1)
                if is3:
                    loaded.passed(32)
                    w_step.passed(1)
                    qk_std.passed(TB)
                pool_done.passed(TB + 3)
                stats_in.passed(TB)
                for s in (std_ready, rstd_ready):
                    s.passed(1)
                for s in (normed, turned, modulated, hi_ready, split_done, qkv_ready, qkv_taken, qk_split):
                    s.passed(TB)
                qk_step.passed(per * TB)

        def attention_phase(l, b, stack, val, oT):
            with ExitStack() as ctx:
                qs = sb(f"qs{l}{b}", [KA, 2, 4, L], BF16, ctx=ctx)
                ks = sb(f"ks{l}{b}", [KA, 2, 4, L], BF16, ctx=ctx)
                pr = sb(f"pr{l}{b}", [P, 4, 2, 512], ctx=ctx)
                vg = sb(f"vg{l}{b}", [P, TB, 4, 32], ctx=ctx)
                o_sb = sb(f"o_sb{l}{b}", [P, 2, 512], ctx=ctx)
                inv = sb(f"inv{l}{b}", [P, 512], ctx=ctx)
                mx = sb(f"mx{l}{b}", [P, 4, TB, 2], ctx=ctx)
                nm = sb(f"nm{l}{b}", [P, 4, TB], ctx=ctx)
                mr = sb(f"mr{l}{b}", [P, 4, TB], ctx=ctx)
                mp = sb(f"mp{l}{b}", [P, 4, 3, TB], BF16, ctx=ctx)
                mpT = sb(f"mpT{l}{b}", [4 * 3 * TB, P], BF16, ctx=ctx)
                t_ps = bank(f"t_ps{l}{b}", ctx)
                t_bf = t_ps[:, :].bitcast(BF16)
                row_ps = [bank(f"row_ps{l}{b}{i}", ctx) for i in range(2)]
                col_ps = [bank(f"cps{l}{b}{i}", ctx, (P, 2, 512)) for i in range(2)]
                o_ps = bank(f"o_ps{l}{b}", ctx)
                QH, KT_N = 2, TB
                SLOTS = QH * KT_N
                LAG = 2

                def fills(do_max, do_exp):
                    f = []
                    for s in range(SLOTS + LAG + 1):
                        if do_max and s == 0:
                            f += [("q", 0), ("k", 0)]
                        if do_max and s % 4 == 1 and s // 4 < 3:
                            f.append(("q", s // 4 + 1))
                        if do_max and s % 4 == 2 and s // 4 < 3:
                            f.append(("k", s // 4 + 1))
                        if do_exp and s == KT_N + LAG + 1:
                            f.append(("den", 0))
                        if do_max and s == SLOTS + 1:
                            f.append(("max", 0))
                    if do_exp:
                        f.append(("den", 1))
                    return f

                N_FIRST, N_ALL, N_LAST = (len(fills(*a)) for a in ((True, False), (True, True), (False, True)))
                TOTAL = N_FIRST + (G - 1) * N_ALL + N_LAST

                def filled_before(it):
                    return 0 if isinstance(it, int) and it == 0 else N_FIRST + (it - 1) * N_ALL

                def pe_iteration(pe, it, do_max, do_exp):
                    order = fills(do_max, do_exp)
                    par, was = it % 2, (it + 1) % 2
                    ge = it - 1

                    def fill(kind, j):
                        n = filled_before(it) + order.index((kind, j))
                        pe.wait_ge(t_taken.sem, t_taken.at(n))
                        if kind in "qk":
                            rows = KD if kind == "q" else KA
                            a = 0 if kind == "q" else 1
                            for t in range(TB):
                                ins = pe.transpose(t_bf[0:rows, t * P:t * P + P],
                                                   stack[:, t, a, 4 * it + j, 0:rows], identb[:, :])
                        elif kind == "max":
                            pe.wait_ge(max_step.sem, max_step.at(6 * it + 6))
                            ins = pe.transpose(t_bf[0:4 * 3 * TB, 0:P], mp[:, :, :, :].rearrange("p j i t -> p (j i t)"),
                                               identb[:, :])
                        else:
                            pe.wait_ge(o_copied.sem, o_copied.at(2 * ge + j + 1))
                            ins = pe.matmul(t_ps[:, :], sel_den[:, :], o_sb[:, j, :], start=True, stop=True)
                        ins.then_inc(t_filled.sem, 1)

                    def scores(e):
                        qh, kt = e // KT_N, e % KT_N
                        for pair in range(2):
                            n = 32 * ge + 2 * e + pair
                            pe.wait_ge(probs.sem, probs.at(n - 1))
                            for h in range(2):
                                ins = pe.matmul(col_ps[pair][:, h, :],
                                                ks[0:KA, was, 2 * pair + h, kt * P:kt * P + P],
                                                qs[0:KA, was, 2 * pair + h, qh * 512:qh * 512 + 512], start=True, stop=True)
                            ins.then_inc(colscores.sem, 1)

                    def weigh(e):
                        qh, kt = e // KT_N, e % KT_N
                        if e == 0:
                            pe.wait_ge(v_staged.sem, v_staged.at(ge + 1))
                        if kt == 0:
                            pe.wait_ge(o_copied.sem, o_copied.at(2 * ge + qh))
                        pe.wait_ge(probs.sem, probs.at(32 * ge + 2 * e + 2))
                        for j in range(4):
                            ins = pe.matmul(o_ps[32 * j:32 * j + 32, :], vg[:, kt, j, :], pr[:, (2 * e + j // 2) % 4, j % 2, :],
                                            start=kt == 0, stop=kt == KT_N - 1)
                        ins.then_inc(weighed.sem, 1)

                    def maxima(s):
                        j = s // 4
                        if s % 4 == 0:
                            n = filled_before(it) + order.index(("k", j)) + 1
                            pe.wait_ge(t_taken.sem, t_taken.at(n))
                        for u in range(4):
                            n = 64 * it + 4 * s + u
                            t, half = (s % 4) * 2 + u // 2, u % 2
                            pe.wait_ge(rowmax.sem, rowmax.at(n - 1))
                            pe.matmul(row_ps[u % 2][:, :], qs[0:KD, par, j, t * P:t * P + P],
                                      ks[0:KD, par, j, half * 512:half * 512 + 512], start=True, stop=True
                                      ).then_inc(rowscores.sem, 1)

                    for s in range(SLOTS + LAG + 1):
                        if do_max and s == 0:
                            fill("q", 0)
                            fill("k", 0)
                        if do_exp and s == LAG:
                            pe.wait_ge(max_rows_in.sem, max_rows_in.at(64 * it))
                        if do_exp and LAG <= s < SLOTS + LAG:
                            scores(s - LAG)
                        if do_max and s < SLOTS:
                            maxima(s)
                        if do_exp and s > LAG:
                            weigh(s - LAG - 1)
                        if do_max and s % 4 == 1 and s // 4 < 3:
                            fill("q", s // 4 + 1)
                        if do_max and s % 4 == 2 and s // 4 < 3:
                            fill("k", s // 4 + 1)
                        if do_exp and s == KT_N + LAG + 1:
                            fill("den", 0)
                        if do_max and s == SLOTS + 1:
                            fill("max", 0)
                    if do_exp:
                        fill("den", 1)

                def act_iteration(act, it, do_max, do_exp):
                    order = fills(do_max, do_exp)
                    par = it % 2
                    ge = it - 1

                    def wait_fill(kind, j):
                        act.wait_ge(t_filled.sem, t_filled.at(filled_before(it) + order.index((kind, j)) + 1))

                    def take_q(j):
                        wait_fill("q", j)
                        act.activation(qs[0:KD, par, j, :], t_bf[0:KD, :], ACT.Copy).then_inc(t_taken.sem, 1)

                    def exps(e):
                        for pair in range(2):
                            n = 32 * ge + 2 * e + pair
                            act.wait_ge(colscores.sem, colscores.at(n + 1))
                            if pair == 0:
                                act.wait_ge(weighed.sem, weighed.at(16 * ge + e - 1))
                            act.activation(pr[:, (2 * e + pair) % 4, :, :], col_ps[pair][:, :, :], ACT.Exp
                                           ).then_inc(probs.sem, 1)

                    def copy_o(qh):
                        act.wait_ge(weighed.sem, weighed.at(16 * ge + KT_N * (qh + 1)))
                        act.wait_ge(o_normed.sem, o_normed.at(2 * ge + qh - 1))
                        act.activation(o_sb[:, qh, :], o_ps[:, :], ACT.Copy).then_inc(o_copied.sem, 1)

                    for s in range(SLOTS + LAG + 1):
                        if do_max and s == 0:
                            take_q(0)
                        if do_exp and LAG <= s < SLOTS + LAG:
                            exps(s - LAG)
                        if do_max and s % 4 == 1 and s // 4 < 3:
                            take_q(s // 4 + 1)
                        if do_exp and s == KT_N + LAG:
                            copy_o(0)
                        if do_max and s == SLOTS + 1:
                            wait_fill("max", 0)
                            act.wait_ge(max_rows_in.sem, max_rows_in.at(64 * it))
                            act.activation(mpT[:, :], t_bf[0:4 * 3 * TB, 0:P], ACT.Copy).then_inc(t_taken.sem, 1)
                    if do_exp:
                        copy_o(1)

                def dve_iteration(dve, it, do_max, do_exp):
                    order = fills(do_max, do_exp)
                    par = it % 2
                    ge = it - 1

                    def wait_fill(kind, j):
                        dve.wait_ge(t_filled.sem, t_filled.at(filled_before(it) + order.index((kind, j)) + 1))

                    def take_k(j):
                        wait_fill("k", j)
                        dve.tensor_copy(ks[0:KA, par, j, :], t_bf[0:KA, :]).then_inc(t_taken.sem, 1)

                    def reduce(s):
                        j = s // 4
                        for u in range(4):
                            t, half = (s % 4) * 2 + u // 2, u % 2
                            dve.wait_ge(rowscores.sem, rowscores.at(64 * it + 4 * s + u + 1))
                            dve.tensor_reduce(mx[:, j, t, half:half + 1], row_ps[u % 2][:, :], AX_X, ALU.max
                                              ).then_inc(rowmax.sem, 1)

                    def normalise(qh):
                        wait_fill("den", qh)
                        dve.wait_ge(o_normed.sem, o_normed.at(2 * ge + qh))
                        dve.reciprocal(inv[:, :], t_ps[:, :]).then_inc(t_taken.sem, 1)
                        dve.wait_ge(t_taken.sem, t_taken.at(filled_before(it) + order.index(("den", qh)) + 1))
                        dve.tensor_tensor(oT[:, ge, qh * 512:qh * 512 + 512], o_sb[:, qh, :], inv[:, :], ALU.mult
                                          ).then_inc(o_normed.sem, 1)

                    def maximum_parts():
                        n = 0

                        def link(ins):
                            nonlocal n
                            n += 1
                            ins.then_inc(max_step.sem, 1)
                            dve.wait_ge(max_step.sem, max_step.at(6 * it + n))
                        dve.wait_ge(rowmax.sem, rowmax.at(64 * it + 64))
                        link(dve.tensor_reduce(nm[:, :, :], mx[:, :, :, :], AX_X, ALU.max))
                        link(dve.tensor_scalar(mp[:, :, 0, :], nm[:, :, :], -1.0, None, ALU.mult))
                        link(dve.scalar_tensor_tensor(mr[:, :, :], nm[:, :, :], -1.0, mp[:, :, 0, :], ALU.mult, ALU.subtract))
                        link(dve.tensor_copy(mp[:, :, 1, :], mr[:, :, :]))
                        link(dve.tensor_tensor(mr[:, :, :], mr[:, :, :], mp[:, :, 1, :], ALU.subtract))
                        link(dve.tensor_copy(mp[:, :, 2, :], mr[:, :, :]))

                    for s in range(SLOTS + LAG + 1):
                        if do_max and s == 0:
                            take_k(0)
                        if do_max and s < SLOTS:
                            reduce(s)
                        if do_max and s % 4 == 2 and s // 4 < 3:
                            take_k(s // 4 + 1)
                        if do_exp and s == KT_N + LAG + 1:
                            normalise(0)
                        if do_max and s == SLOTS - 1:
                            maximum_parts()
                    if do_exp:
                        normalise(1)

                def iterate(eng, one):
                    one(eng, 0, True, False)
                    with eng.Fori(1, G) as it:
                        one(eng, it, True, True)
                    one(eng, G, False, True)

                with nc.Block() as block:
                    @block.tensor
                    def _(pe):
                        iterate(pe, pe_iteration)

                    @block.scalar
                    def _(act):
                        act.preload_act_table(ACT.Exp)
                        iterate(act, act_iteration)

                    @block.vector
                    def _(dve):
                        iterate(dve, dve_iteration)

                    @block.gpsimd
                    def _(pool):
                        with pool.Fori(0, G) as g:
                            pool.wait_ge(weighed.sem, weighed.at(16 * g))
                            for j in range(4):
                                ins = pool.tensor_copy(vg[:, :, j, :], val[:, :, 4 * g + j, :].rearrange("p t d -> p t d"))
                            ins.then_inc(v_staged.sem, 1)

                    @block.sync
                    def _(sp):
                        with sp.Fori(0, G) as g:
                            sp.wait_ge(t_taken.sem, t_taken.at(N_FIRST + g * N_ALL))
                            for j in range(4):
                                sp.dma_start(qs[KD:KA, g % 2, j, :], mpT[3 * TB * j:3 * TB * (j + 1), :]).then_inc(max_rows_in.sem, 16)
                t_filled.passed(TOTAL)
                t_taken.passed(TOTAL)
                rowscores.passed(64 * G)
                rowmax.passed(64 * G)
                colscores.passed(32 * G)
                probs.passed(32 * G)
                weighed.passed(16 * G)
                o_copied.passed(2 * G)
                o_normed.passed(2 * G)
                max_step.passed(6 * G)
                v_staged.passed(G)
                max_rows_in.passed(64 * G)

        def project_phase(l, b, oT):
            with ExitStack() as ctx:
                wp = sb(f"wp{l}{b}", [P, G, C], ctx=ctx)
                y = sb(f"y{l}{b}", [P, 2, C], ctx=ctx)
                ps = [bank(f"pp{l}{b}{k}", ctx) for k in range(2)]
                with nc.Block() as block:
                    @block.gpsimd
                    def _(pool):
                        pool.memset(wp[:, :, :], 0.0).then_inc(pool_done.sem, 1)

                    @block.sync
                    def _(sp):
                        sp.wait_ge(pool_done.sem, pool_done.at(1))
                        for g in range(G):
                            for j in range(4):
                                h = 4 * g + j
                                sp.dma_start(wp[32 * j:32 * j + D, g, :], w["proj_w"][l][h * D:(h + 1) * D, :]
                                             ).then_inc(loaded.sem, 16)
                        sp.dma_start(wp[D:D + 1, 0, :], w["proj_b"][l]).then_inc(loaded.sem, 16)

                    @block.tensor
                    def _(pe):
                        pe.wait_ge(loaded.sem, loaded.at(16 * 17))
                        for t in range(TB):
                            if t > 1:
                                pe.wait_ge(gated.sem, gated.at(t - 1))
                            for g in range(G):
                                mm = pe.matmul(ps[t % 2][:, 0:C], oT[:, g, t * P:t * P + P], wp[:, g, :],
                                               start=g == 0, stop=g == G - 1)
                            mm.then_inc(mm_done.sem, 1)

                    @block.vector
                    def _(dve):
                        for t in range(TB):
                            tile = TB * b + t
                            dve.wait_ge(mm_done.sem, mm_done.at(t + 1))
                            dve.tensor_tensor(y[:, t % 2, :], ps[t % 2][:, 0:C], gate_b[:, l, 0, b, :], ALU.mult
                                              ).then_inc(gated.sem, 1)
                            dve.wait_ge(gated.sem, gated.at(t + 1))
                            dve.tensor_tensor(x[:, tile, :], x[:, tile, :], y[:, t % 2, :], ALU.add).then_inc(added.sem, 1)
                            dve.wait_ge(added.sem, added.at(t + 1))
                            dve.bn_stats(stats[:, tile, :], x[:, tile, :])
                pool_done.passed(1)
                loaded.passed(16 * 17)
                for s in (mm_done, gated, added):
                    s.passed(TB)

        def mlp_phases(l, experts):
            CH = 256
            NCH = NT * P // CH
            with ExitStack() as ctx:
                hh = sb(f"hh{l}", [P, 2, NT * P], F32R, ctx=ctx)
                hl = sb(f"hl{l}", [P, 2, NT * P], F32R, ctx=ctx)
                h3 = sb(f"h3{l}", [RA, NT * P], F32R, ctx=ctx)
                with ExitStack() as ctx2:
                    xn = sb(f"xm{l}", [P, 2, XN], ctx=ctx2)
                    m = sb(f"mm{l}", [P, 2, 3, P], ctx=ctx2)
                    turn_ps = [bank(f"tm{l}{k}", ctx2) for k in range(2)]

                    def cols(t):
                        return bass.ds(t * P, P)
                    normalise, turn, modulate, split = norm_stages(
                        ctx2, l, 2, xn, m, turn_ps, lambda t, k: hh[:, :, cols(t)], lambda t, k: hl[:, :, cols(t)],
                        lambda t, k: h3[:, cols(t)], False)
                    with nc.Block() as block:
                        @block.gpsimd
                        def _(pool):
                            pool.memset(xn[:, :, 2 * P + RS:XN], 1.0).then_inc(pool_done.sem, 1)

                        @block.tensor
                        def _(pe):
                            pe.wait_ge(pool_done.sem, pool_done.at(1))
                            with pe.Fori(0, NT // 2) as i:
                                for k in range(2):
                                    turn(pe, 2 * i + k, k)

                        @block.scalar
                        def _(act):
                            deviations(None, act, (0, NT))
                            for b in range(B):
                                with act.Fori(0, TB // 2) as i:
                                    for k in range(2):
                                        modulate(act, 2 * i + (k + TB * b), b, k)

                        @block.vector
                        def _(dve):
                            deviations(dve, None, (0, NT))
                            normalise(dve, 0, 0, 0)
                            with dve.Fori(0, NT // 2 - 1) as i:
                                for k in range(2):
                                    normalise(dve, 2 * i + k + 1, 2 * i + k + 1, 1 - k)
                                    split(dve, 2 * i + k, k)
                            normalise(dve, NT - 1, NT - 1, 1)
                            split(dve, NT - 2, 0)
                            split(dve, NT - 1, 1)
                    pool_done.passed(1)
                    stats_in.passed(NT)
                    std_ready.passed(1)
                    rstd_ready.passed(1)
                    for s in (normed, turned, modulated, hi_ready, split_done):
                        s.passed(NT)
                if experts > 1:
                    gate_phase(hh, hl, h3)
                w1r = sb(f"w1r{l}", [P, 3, FF], ctx=ctx)
                w1h = sb(f"w1h{l}", [P, 2, FF], F32R, ctx=ctx)
                w1l = sb(f"w1l{l}", [P, 2, FF], F32R, ctx=ctx)
                w13 = sb(f"w13{l}", [RA, FF], F32R, ctx=ctx)
                w2r = sb(f"w2r{l}", [P, NF + 1, C], ctx=ctx)
                w2h = sb(f"w2h{l}", [P, NF + 1, C], F32R, ctx=ctx)
                w2l = sb(f"w2l{l}", [P, NF, C], F32R, ctx=ctx)
                ones2 = sb(f"ones2{l}", [P, P], F32R, ctx=ctx)
                for ex in range(experts):
                    with ExitStack() as ctx2:
                        with nc.Block() as block:
                            @block.gpsimd
                            def _(pool):
                                pool.memset(w2r[:, NF, :], 0.0).then_inc(pool_done.sem, 1)

                            @block.sync
                            def _(sp):
                                sp.dma_start(w2r[:, 0:NF, :], w["fc2_w"][l][ex].rearrange("(k p) c -> p k c", p=P)
                                             ).then_inc(loaded.sem, 16)
                                sp.wait_ge(pool_done.sem, pool_done.at(1))
                                for r in range(2):
                                    sp.dma_start(w2r[r:r + 1, NF, :], w["fc2_b"][l][ex]).then_inc(loaded.sem, 16)

                            @block.vector
                            def _(dve):
                                step = Chain(dve, dve_done)
                                dve.wait_ge(loaded.sem, loaded.at(48))
                                step(dve.tensor_copy(ones2[:, :], mix[:, 2:3].broadcast_to([P, P])))
                                step(dve.tensor_copy(w2h[:, :, :], w2r[:, :, :]))
                                step(dve.tensor_tensor(w2l[:, :, :], w2r[:, 0:NF, :], w2h[:, 0:NF, :].bitcast(F32), ALU.subtract))
                                step(dve.tensor_tensor(w2r[:, NF, :], w2r[:, NF, :], w2h[:, NF, :].bitcast(F32), ALU.subtract))
                                step(dve.tensor_scalar(w2r[:, NF, :], w2r[:, NF, :], mix[:, 3:4], None, ALU.mult))
                                step(dve.scalar_tensor_tensor(w2h[:, NF, :], w2h[:, NF, :].bitcast(F32), ident[:, 0:1],
                                                              w2r[:, NF, :], ALU.mult, ALU.add))
                        loaded.passed(48)
                        pool_done.passed(1)
                        dve_done.passed(6)
                        with nc.Block() as block:
                            n = split_weights(block, ctx2, f"w1{l}{ex}", FF, w["fc1_w"][l][ex], w["fc1_b"][l][ex],
                                              w1h, w1l, w13, 0, w1r)
                        loaded.passed(16 * 7)
                        w_step.passed(n)
                    with ExitStack() as ctx2:
                        PAIRS = (NF + 1) // 2
                        g = sb(f"g{l}{ex}", [P, 2, 2, CH], ctx=ctx2)
                        gh = sb(f"gh{l}{ex}", [P, 2, NF, CH], F32R, ctx=ctx2)
                        gl = sb(f"gl{l}{ex}", [P, 2, NF, CH], F32R, ctx=ctx2)
                        y = sb(f"ym{l}{ex}", [P, 2, C], ctx=ctx2)
                        up_ps = [bank(f"up{l}{ex}{i}", ctx2) for i in range(PAIRS)]
                        dn_ps = [bank(f"dn{l}{ex}{i}", ctx2) for i in range(2)]
                        size = [min(2, NF - 2 * q) for q in range(PAIRS)]

                        def up(pe, c, k):
                            for q in range(PAIRS):
                                n = PAIRS * c + q
                                pe.wait_ge(gelu_done.sem, gelu_done.at(n - PAIRS + 1))
                                pbank = up_ps[q]
                                for i in range(size[q]):
                                    f = 2 * q + i
                                    cols = slice(f * P, f * P + P)
                                    mm = split_products(
                                        pe, pbank[:, i * CH:i * CH + CH],
                                        (lambda s: w1h[:, s, cols], lambda s: w1l[:, s, cols], w13[0:RA, cols]),
                                        (lambda s: hh[:, s, bass.ds(c * CH, CH)], lambda s: hl[:, s, bass.ds(c * CH, CH)],
                                         h3[0:RA, bass.ds(c * CH, CH)]))
                                mm.then_inc(up_ready.sem, 1)

                        def gelu(act, c, k):
                            for q in range(PAIRS):
                                n = PAIRS * c + q
                                act.wait_ge(up_ready.sem, up_ready.at(n + 1))
                                act.wait_ge(g_split.sem, g_split.at(n - 1 if q else n))
                                act.activation(g[:, q % 2, 0:size[q], :].rearrange("p i c -> p (i c)"),
                                               up_ps[q][:, 0:size[q] * CH], ACT.Gelu_apprx_tanh).then_inc(gelu_done.sem, 1)

                        def split_g(dve, c, k):
                            dve.wait_ge(mm_done.sem, mm_done.at(2 * (c - 1)))
                            for q in range(PAIRS):
                                n = PAIRS * c + q
                                dve.wait_ge(gelu_done.sem, gelu_done.at(n + 1))
                                fs = slice(2 * q, 2 * q + size[q])
                                dve.tensor_copy(gh[:, k, fs, :], g[:, q % 2, 0:size[q], :]).then_inc(g_hi.sem, 1)
                                dve.wait_ge(g_hi.sem, g_hi.at(n + 1))
                                dve.tensor_tensor(gl[:, k, fs, :], g[:, q % 2, 0:size[q], :], gh[:, k, fs, :].bitcast(F32),
                                                  ALU.subtract).then_inc(g_split.sem, 1)

                        def down(pe, c, k):
                            pe.wait_ge(g_split.sem, g_split.at(PAIRS * (c + 1)))
                            for i in range(2):
                                n = 2 * c + i
                                pe.wait_ge(gated.sem, gated.at(n - 1))
                                o = dn_ps[i][:, 0:C]
                                tok = slice(i * P, i * P + P)
                                for f in range(NF):
                                    pe.matmul(o, gh[:, k, f, tok], w2h[:, f, :], start=f == 0, stop=False)
                                    pe.matmul(o, gh[:, k, f, tok], w2l[:, f, :], start=False, stop=False)
                                    pe.matmul(o, gl[:, k, f, tok], w2h[:, f, :], start=False, stop=False)
                                pe.matmul(o, ones2[:, :], w2h[:, NF, :], start=False, stop=True).then_inc(mm_done.sem, 1)

                        def residual(dve, c, b, k):
                            for i in range(2):
                                n = 2 * c + i
                                dve.wait_ge(mm_done.sem, mm_done.at(n + 1))
                                dve.scalar_tensor_tensor(y[:, i, :], dn_ps[i][:, 0:C], cw[:, n, ex:ex + 1],
                                                         gate_b[:, l, 1, b, :], ALU.mult, ALU.mult).then_inc(gated.sem, 1)
                                dve.wait_ge(gated.sem, gated.at(n + 1))
                                dve.tensor_tensor(x[:, n, :], x[:, n, :], y[:, i, :], ALU.add).then_inc(added.sem, 1)
                                if ex == experts - 1:
                                    dve.wait_ge(added.sem, added.at(n + 1))
                                    dve.bn_stats(stats[:, n, :], x[:, n, :])

                        with nc.Block() as block:
                            @block.tensor
                            def _(pe):
                                up(pe, 0, 0)
                                with pe.Fori(0, NCH // 2 - 1) as i:
                                    for k in range(2):
                                        up(pe, 2 * i + k + 1, 1 - k)
                                        down(pe, 2 * i + k, k)
                                up(pe, NCH - 1, 1)
                                down(pe, NCH - 2, 0)
                                down(pe, NCH - 1, 1)

                            @block.scalar
                            def _(act):
                                act.preload_act_table(ACT.Gelu_apprx_tanh)
                                with act.Fori(0, NCH) as c:
                                    gelu(act, c, 0)

                            @block.vector
                            def _(dve):
                                split_g(dve, 0, 0)
                                with dve.Fori(0, NCH // 2 - 1) as i:
                                    for k in range(2):
                                        split_g(dve, 2 * i + k + 1, 1 - k)
                                        residual(dve, 2 * i + k, i // (NCH // 2 // B), k)
                                split_g(dve, NCH - 1, 1)
                                residual(dve, NCH - 2, B - 1, 0)
                                residual(dve, NCH - 1, B - 1, 1)
                    for s in (up_ready, gelu_done, g_hi, g_split):
                        s.passed(PAIRS * NCH)
                    for s in (mm_done, gated, added):
                        s.passed(NT)

        def gate_phase(hh, hl, h3):
            with ExitStack() as ctx:
                raw = sb("wg_raw", [P, 3, P], ctx=ctx)
                gh = sb("wg_h", [P, 2, P], F32R, ctx=ctx)
                gl = sb("wg_l", [P, 2, P], F32R, ctx=ctx)
                g3 = sb("wg_3", [RA, P], F32R, ctx=ctx)
                lT = sb("lT", [EXPERTS, NT * P], ctx=ctx)
                lg = sb("lg", [P, NT, EXPERTS], ctx=ctx)
                top1 = sb("top1", [P, NT], ctx=ctx)
                ex = sb("ex", [P, NT, EXPERTS], ctx=ctx)
                rank = sb("rank", [P, NT, EXPERTS], ctx=ctx)
                cmp = sb("cmp", [P, NT, EXPERTS], ctx=ctx)
                ps = [bank(f"lg_ps{i}", ctx) for i in range(4)]
                col = bank("lg_col", ctx)
                with nc.Block() as block:
                    @block.gpsimd
                    def _(pool):
                        pool.memset(raw[:, :, :], 0.0).then_inc(pool_done.sem, 1)
                    split_weights(block, ctx, "wg", P, w["gate_w"], None, gh, gl, g3, 0, raw, cols=EXPERTS)
                loaded.passed(16 * 5)
                pool_done.passed(1)
                w_step.passed(5)
                with nc.Block() as block:
                    @block.tensor
                    def _(pe):
                        for c in range(4):
                            cols = slice(c * 512, c * 512 + 512)
                            split_products(pe, ps[c][:, :],
                                           (lambda s: gh[:, s, :], lambda s: gl[:, s, :], g3[0:RA, :]),
                                           (lambda s: hh[:, s, cols], lambda s: hl[:, s, cols], h3[0:RA, cols])
                                           ).then_inc(pe_done.sem, 1)
                        for c in range(4):
                            pe.wait_ge(act_done.sem, act_done.at(c + 1))
                            for t in range(4 * c, 4 * c + 4):
                                mm = pe.transpose(col[:, 4 * t:4 * t + 4], lT[:, t * P:t * P + P], ident[0:4, 0:4])
                        mm.then_inc(pe_done.sem, 1)

                    @block.scalar
                    def _(act):
                        for c in range(4):
                            act.wait_ge(pe_done.sem, pe_done.at(c + 1))
                            act.activation(lT[:, c * 512:c * 512 + 512], ps[c][0:EXPERTS, :], ACT.Copy).then_inc(act_done.sem, 1)
                        act.wait_ge(dve_done.sem, dve_done.at(3))
                        act.activation(ex[:, :, :], cmp[:, :, :], ACT.Exp).then_inc(act_done.sem, 1)

                    @block.vector
                    def _(dve):
                        step = Chain(dve, dve_done)
                        dve.wait_ge(pe_done.sem, pe_done.at(5))
                        step(dve.tensor_copy(lg[:, :, :].rearrange("p t e -> p (t e)"), col[:, 0:NT * EXPERTS]))
                        step(dve.tensor_reduce(top1[:, :], lg[:, :, :], AX_X, ALU.max))
                        step(dve.tensor_tensor(cmp[:, :, :], lg[:, :, :],
                                               top1[:, :].unsqueeze(2).broadcast_to([P, NT, EXPERTS]), ALU.subtract))
                        step(dve.memset(rank[:, :, :], 0.0))
                        dve.wait_ge(act_done.sem, act_done.at(5))
                        for f in range(EXPERTS):
                            step(dve.tensor_tensor(cmp[:, :, :], lg[:, :, f:f + 1].broadcast_to([P, NT, EXPERTS]),
                                                   lg[:, :, :], ALU.is_gt))
                            step(dve.tensor_tensor(rank[:, :, :], rank[:, :, :], cmp[:, :, :], ALU.add))
                            if f < EXPERTS - 1:
                                n = EXPERTS - 1 - f
                                step(dve.tensor_tensor(cmp[:, :, f + 1:], lg[:, :, f:f + 1].broadcast_to([P, NT, n]),
                                                       lg[:, :, f + 1:], ALU.is_equal))
                                step(dve.tensor_tensor(rank[:, :, f + 1:], rank[:, :, f + 1:], cmp[:, :, f + 1:], ALU.add))
                        step(dve.scalar_tensor_tensor(ex[:, :, :], rank[:, :, :], 2.0, ex[:, :, :], ALU.is_lt, ALU.mult))
                        step(dve.tensor_reduce(top1[:, :], ex[:, :, :], AX_X, ALU.add))
                        step(dve.reciprocal(top1[:, :], top1[:, :]))
                        step(dve.tensor_tensor(cw[:, :, :], ex[:, :, :],
                                               top1[:, :].unsqueeze(2).broadcast_to([P, NT, EXPERTS]), ALU.mult))
                pe_done.passed(5)
                act_done.passed(5)
                dve_done.passed(4 + 4 * 2 + 3 * 2 + 4)

        def rotate_phase():
            with ExitStack() as ctx:
                xT = sb("xT", [P, 2, 3, P], ctx=ctx)
                turn_ps = [bank(f"rt{k}", ctx) for k in range(2)]
                ps = [bank(f"rp{k}", ctx) for k in range(2)]
                KROWS = (P, P, R)

                def turn(pe, t, k):
                    pe.wait_ge(modulated.sem, modulated.at(t - 1))
                    for s in range(3):
                        mm = pe.transpose(turn_ps[k][0:KROWS[s], s * P:s * P + P], x[:, t, s * P:s * P + KROWS[s]], ident[:, :])
                    mm.then_inc(turned.sem, 1)

                with nc.Block() as block:
                    @block.tensor
                    def _(pe):
                        turn(pe, 0, 0)
                        for t in range(NT):
                            if t + 1 < NT:
                                turn(pe, t + 1, (t + 1) % 2)
                            pe.wait_ge(modulated.sem, modulated.at(t + 1))
                            pe.wait_ge(added.sem, added.at(t - 1))
                            for s in range(3):
                                K = KROWS[s]
                                mm = pe.matmul(ps[t % 2][:, 0:C], xT[0:K, t % 2, s, :], m_rot[0:K, t // TB, s, :],
                                               start=s == 0, stop=s == 2)
                            mm.then_inc(mm_done.sem, 1)

                    @block.scalar
                    def _(act):
                        for t in range(NT):
                            act.wait_ge(turned.sem, turned.at(t + 1))
                            act.wait_ge(mm_done.sem, mm_done.at(t - 1))
                            act.activation(xT[:, t % 2, 0:2, :].rearrange("p s c -> p (s c)"), turn_ps[t % 2][:, 0:2 * P], ACT.Copy)
                            act.activation(xT[0:R, t % 2, 2, :], turn_ps[t % 2][0:R, 2 * P:3 * P], ACT.Copy
                                           ).then_inc(modulated.sem, 1)

                    @block.vector
                    def _(dve):
                        for t in range(NT):
                            dve.wait_ge(mm_done.sem, mm_done.at(t + 1))
                            dve.tensor_tensor(x[:, t, :], x[:, t, :], ps[t % 2][:, 0:C], ALU.add).then_inc(added.sem, 1)
                            dve.wait_ge(added.sem, added.at(t + 1))
                            dve.bn_stats(stats[:, t, :], x[:, t, :])
                for s in (turned, modulated, mm_done, added):
                    s.passed(NT)

        modulation()
        rotation()
        stage = 0
        for l in range(3):
            if l == 1:
                rotate_phase()
            if upto == stage:
                break
            stage += 1
            for b in range(B):
                with ExitStack() as ctx:
                    if b == 0:
                        wctx = ctx.enter_context(ExitStack())
                    oT = sb(f"oT{l}{b}", [P, G, L], ctx=ctx)
                    with ExitStack() as ctx2:
                        stack = sb(f"stack{l}{b}", [P, TB, 2, H, SW], BF16, ctx=ctx2)
                        val = sb(f"val{l}{b}", [P, TB, H, 32], ctx=ctx2)
                        with ExitStack() as ctx3:
                            wq = (sb(f"wqh{l}{b}", [P, 2, 3 * C], F32R, ctx=ctx3),
                                  sb(f"wql{l}{b}", [P, 2, 3 * C], F32R, ctx=ctx3),
                                  sb(f"wq3{l}{b}", [RA, 3 * C], F32R, ctx=ctx3))
                            qkv_phase(l, b, True, wq, stack, val)
                        attention_phase(l, b, stack, val, oT)
                    project_phase(l, b, oT)
            if upto == stage:
                break
            stage += 1
            mlp_phases(l, EXPERTS if l == 1 else 1)
            if l == 1:
                with nc.Block() as block:
                    @block.gpsimd
                    def _(pool):
                        pool.memset(cw[:, :, :], 1.0)
            if upto == stage:
                break
            stage += 1
        with nc.Block() as block:
            @block.sync
            def _(sp):
                sp.dma_start(out.rearrange("b (t p) c -> p (b t) c", p=P), x[:, :, :]).then_inc(stored.sem, 16)
                sp.wait_ge(stored.sem, stored.at(16))


def constants():
    import numpy as np
    f = np.float32
    eye = np.eye(P, dtype=f)
    mix = np.zeros((P, 4), f)
    mix[0:2 * R, 0] = 1
    mix[RS, 0] = 1
    mix[0:RA, 1] = 1 - mix[0:RA, 0]
    mix[0:2, 2] = 1
    mix[1, 3] = 1
    sel = np.zeros((P, P), f)
    for j in range(4):
        sel[32 * j + D, 32 * j:32 * j + 32] = 1
    rows = (np.arange(C)[:, None] >= np.arange(RK)[None, :]).astype(f)
    tri = np.stack([np.triu(np.ones((RK, RK), f), 1), np.eye(RK, dtype=f)], 1)
    i = np.arange(SQUARINGS)
    k = 1.0 / np.maximum(TAYLOR - 1 - i, 1)
    pw = np.broadcast_to(np.stack([2.0 ** i, 2.0 ** -(i + 1) - 1, k])[None], (RK, 3, SQUARINGS)).astype(f)
    return {"const_ident": eye, "const_mix": mix, "const_sel": sel, "const_rows": rows, "const_tri": tri, "const_pow": pw}


def laid_out(inputs):
    import numpy as np
    a = {k: np.ascontiguousarray(v) for k, v in inputs.items()}
    r = {
        "x": a["x"], "condT": np.ascontiguousarray(a["cond_1152"].T),
        "rot_P": a["L1_cond_P"], "rot_PT": np.ascontiguousarray(a["L1_cond_P"].T),
        "g_q": a["L3_cond_g_q"], "g_k": a["L3_cond_g_k"], "gate_w": a["L2_cond_w_gate"],
    }
    iu, ju = np.triu_indices(RK, k=1)
    grid = np.zeros((C, RK, RK), a["L1_cond_W"].dtype)
    grid[:, iu, ju] = a["L1_cond_W"].T
    r["rot_W"] = grid.reshape(C, RK * RK)
    grid = np.zeros((RK, RK), a["L1_cond_b"].dtype)
    grid[iu, ju] = a["L1_cond_b"]
    r["rot_b"] = grid.reshape(1, RK * RK)
    names = [("L0_cond_W_qkv", "L0_cond_b_qkv", "L0_cond_W_proj", "L0_cond_b_proj", "L0_cond_W_ada", "L0_cond_b_ada",
              "L0_cond_W_fc1", "L0_cond_b_fc1", "L0_cond_W_fc2", "L0_cond_b_fc2"),
             ("L2_cond_w_qkv", "L2_cond_b_qkv", "L2_cond_w_proj", "L2_cond_b_proj", "L2_cond_w_adaln", "L2_cond_b_adaln",
              "L2_cond_w1", "L2_cond_b1", "L2_cond_w2", "L2_cond_b2"),
             ("L3_cond_w_qkv", "L3_cond_b_qkv", "L3_cond_w_proj", "L3_cond_b_proj", "L3_cond_w_mod", "L3_cond_b_mod",
              "L3_cond_w1", "L3_cond_b1", "L3_cond_w2", "L3_cond_b2")]
    kinds = ("qkv_w", "qkv_b", "proj_w", "proj_b", "ada_w", "ada_b", "fc1_w", "fc1_b", "fc2_w", "fc2_b")
    for l, row in enumerate(names):
        for kind, name in zip(kinds, row):
            r[f"{kind}{l}"] = a[name]
    return r


def declare(nc, arrays):
    import numpy as np
    ap = {}
    for name, v in arrays.items():
        ap[name] = nc.dram_tensor(f"in_{name}", v.shape, mybir.dt.from_np(v.dtype), kind="ExternalInput").ap()
    out = nc.dram_tensor("out", (B, L, C), F32, kind="ExternalOutput").ap()
    w = {k: v for k, v in ap.items()}

    def row(v):
        return v.rearrange("(o c) -> o c", o=1)
    w["qkv_w"] = [ap[f"qkv_w{l}"] for l in range(3)]
    w["qkv_b"] = [row(ap[f"qkv_b{l}"]) for l in range(3)]
    w["proj_w"] = [ap[f"proj_w{l}"] for l in range(3)]
    w["proj_b"] = [row(ap[f"proj_b{l}"]) for l in range(3)]
    w["ada_w"] = [ap[f"ada_w{l}"] for l in range(3)]
    w["ada_b"] = [ap[f"ada_b{l}"] for l in range(3)]
    for kind in ("fc1_w", "fc2_w"):
        w[kind] = [[ap[f"{kind}{l}"][e] for e in range(EXPERTS)] if l == 1 else [ap[f"{kind}{l}"]] for l in range(3)]
    for kind in ("fc1_b", "fc2_b"):
        w[kind] = [[ap[f"{kind}{l}"][e:e + 1, :] for e in range(EXPERTS)] if l == 1 else [row(ap[f"{kind}{l}"])]
                   for l in range(3)]
    return ap["x"], out, w


def kernel(**inputs):
    import concourse.bacc as bacc
    from concourse.bass_utils import run_bass_kernel_spmd

    nc = bacc.Bacc("TRN2", target_bir_lowering=False, num_devices=1)
    arrays = {**laid_out(inputs), **constants()}
    x_in, out, w = declare(nc, arrays)
    build(nc, x_in, out, w)
    r = run_bass_kernel_spmd(nc, [{f"in_{k}": v for k, v in arrays.items()}], core_ids=[0])
    return r.results[0]["out"]
```

```python
from contextlib import ExitStack

import concourse.bass as bass
from concourse import mybir

F32 = mybir.dt.float32
F32R = mybir.dt.float32r
BF16 = mybir.dt.bfloat16
ALU = mybir.AluOpType
ACT = mybir.ActivationFunctionType
AX_X = mybir.AxisListType.X

P = 128
B, L, C = 2, 1024, 288
H = 16
D = C // H
TB = L // P
NT = B * TB
R = C - 2 * P
RS = 3 * R
RA = RS + 2
SLAB = (P, P, RS)
XN = 2 * P + RA
FF = 4 * C
NF = FF // P
EXPERTS = 4
RK = 64
QR_P, QR_T = 96, 3
PARTS = 6
KD = PARTS * D
KA = KD + 3
SW = 112
G = H // 4
SCALE = float(D) ** -0.5
EPS = 1e-6
CREDIT = 64
SPLIT_STEPS = 5
RING = 10
SQUARINGS = 20
TAYLOR = 12


class Signal:

    def __init__(self, sem):
        self.sem = sem
        self.base = CREDIT

    def at(self, n):
        return self.base + n

    def passed(self, n):
        self.base += n


class Chain:

    def __init__(self, eng, counted):
        self.eng, self.counted, self.n = eng, counted, 0

    def __call__(self, ins):
        self.n += 1
        ins.then_inc(self.counted.sem, 1)
        self.eng.wait_ge(self.counted.sem, self.counted.at(self.n))
        return self.n


def build(nc, x_in, out, w, upto=99, tap=None):
    top = ExitStack()
    with top:
        used = {}

        def fresh(name):
            used[name] = used.get(name, 0) + 1
            return name if used[name] == 1 else f"{name}_{used[name]}"

        def sb(name, shape, dt=F32, ctx=top):
            name = fresh(name)
            return ctx.enter_context(nc.sbuf_tensor(name, shape, dt))

        def bank(name, ctx, shape=(P, 512), dt=F32):
            return ctx.enter_context(nc.psum_tensor(fresh(name), list(shape), dt))

        signals = []

        def signal(name):
            s = Signal(top.enter_context(nc.semaphore(name)))
            signals.append(s)
            return s

        loaded = signal("loaded")
        w_loaded = signal("w_loaded")
        gate_step = signal("gate_step")
        w2_loaded = signal("w2_loaded")
        w2_step = signal("w2_step")
        proj_loaded = signal("proj_loaded")
        wp_cleared = signal("wp_cleared")
        stored = signal("stored")
        max_rows_in = signal("max_rows_in")
        dve_done = signal("dve_done")
        act_done = signal("act_done")
        pe_done = signal("pe_done")
        pool_done = signal("pool_done")
        stats_in = signal("stats_in")
        std_ready = signal("std_ready")
        rstd_ready = signal("rstd_ready")
        normed = signal("normed")
        turned = signal("turned")
        modulated = signal("modulated")
        hi_ready = signal("hi_ready")
        split_done = signal("split_done")
        qkv_ready = signal("qkv_ready")
        qkv_taken = signal("qkv_taken")
        qk_step = signal("qk_step")
        qk_std = signal("qk_std")
        qk_split = signal("qk_split")
        t_filled = signal("t_filled")
        t_taken = signal("t_taken")
        rowscores = signal("rowscores")
        rowmax = signal("rowmax")
        colscores = signal("colscores")
        probs = signal("probs")
        weighed = signal("weighed")
        o_copied = signal("o_copied")
        o_normed = signal("o_normed")
        inv_ready = signal("inv_ready")
        max_step = signal("max_step")
        v_staged = signal("v_staged")
        mm_done = signal("mm_done")
        gated = signal("gated")
        added = signal("added")
        up_ready = signal("up_ready")
        gelu_done = signal("gelu_done")
        g_hi = signal("g_hi")
        g_split = signal("g_split")
        w_step = signal("w_step")
        qr_col = signal("qr_col")
        qr_dots = signal("qr_dots")
        qr_copy = signal("qr_copy")
        qr_step = signal("qr_step")

        x = sb("x", [P, NT, C])
        stats = sb("stats", [P, NT, 6])
        mv = sb("mv", [P, NT, 2])
        std = sb("std", [P, NT])
        rstd = sb("rstd", [P, NT])
        modc = sb("modc", [P, 3, 4, 3, B])
        gate_b = sb("gate_b", [P, 3, 2, B, C])
        ident = sb("ident", [P, P])
        identb = sb("identb", [P, P], BF16)
        m_rot = sb("m_rot", [P, B, 3, C])
        cw = sb("cw", [P, NT, EXPERTS])
        eps_col = sb("eps_col", [P, 1])
        mix = sb("mix", [P, 4])
        sel_den = sb("sel_den", [P, 4])

        with nc.Block() as block:
            @block.gpsimd
            def _(pool):
                for s in signals:
                    pool.nop().then_inc(s.sem, CREDIT)
                pool.memset(eps_col[:, :], EPS)

        def modulation(mem):
            with ExitStack() as ctx:
                wa = sb("wa", [P, 3, 3, 6 * C], ctx=ctx)
                condT = sb("condT", [P, 3, B], ctx=ctx)
                sT = sb("sT", [P, 3, B], ctx=ctx)
                sTb = sb("sTb", [P, 3, B, P], ctx=ctx)
                bias_c = sb("bias_c", [P, 3, 4, 3], ctx=ctx)
                bias_g = sb("bias_g", [P, 3, 2, C], ctx=ctx)
                col_ps = bank("col_ps", ctx, (P, 3, 4, 3, 8))
                gate_ps = bank("gate_ps", ctx, (P, 4, 512))
                KROWS = (P, P, R)
                n_load = 0
                with nc.Block() as block:
                    @block.sync
                    def _(sp):
                        nonlocal n_load

                        def load(dst, src):
                            nonlocal n_load
                            sp.dma_start(dst, src).then_inc(loaded.sem, 16)
                            n_load += 1

                        for s in range(3):
                            load(condT[0:KROWS[s], s, :], w["condT"][s * P:s * P + KROWS[s], :])
                        load(ident[:, :], w["const_ident"])
                        load(mix[:, :], w["const_mix"])
                        load(sel_den[:, :], w["const_sel"])
                        load(x[:, :, :], x_in.rearrange("b (t p) c -> p (b t) c", p=P))
                        for l in range(3):
                            wd, bd = w["ada_w"][l], w["ada_b"][l]
                            for s in range(3):
                                load(wa[0:KROWS[s], l, s, :], wd[s * P:s * P + KROWS[s], :])
                            for gi, six in enumerate((2, 5)):
                                load(bias_g[:, l, gi, :],
                                     bd[six * C:six * C + C].rearrange("(o c) -> o c", o=1).broadcast_to([P, C]))
                            for ki, six in enumerate((0, 1, 3, 4)):
                                for s in range(2):
                                    load(bias_c[:, l, ki, s:s + 1],
                                         bd[six * C + s * P:six * C + s * P + P].rearrange("(c o) -> c o", o=1))
                                for r in range(3):
                                    load(bias_c[R * r:R * r + R, l, ki, 2:3],
                                         bd[six * C + 2 * P:six * C + C].rearrange("(c o) -> c o", o=1))

                        mem.load_qkv(sp)

                    ALL = n_load

                    @block.scalar
                    def _(act):
                        act.wait_ge(loaded.sem, loaded.at(16 * ALL))
                        for s in range(3):
                            act.activation(sT[0:KROWS[s], s, :], condT[0:KROWS[s], s, :], ACT.Silu).then_inc(
                                act_done.sem, 1)

                    @block.gpsimd
                    def _(pool):
                        pool.memset(modc[:, :, :, :, :], 0.0).then_inc(pool_done.sem, 1)
                        pool.wait_ge(pool_done.sem, pool_done.at(1))
                        for ki in (1, 3):
                            pool.memset(modc[:, :, ki, :, :], 1.0).then_inc(pool_done.sem, 1)
                        pool.memset(cw[:, :, :], 1.0).then_inc(pool_done.sem, 1)

                    @block.tensor
                    def _(pe):
                        pe.wait_ge(dve_done.sem, dve_done.at(3))
                        for l in range(3):
                            for ki, six in enumerate((0, 1, 3, 4)):
                                for s in range(3):
                                    for r in range(3 if s == 2 else 1):
                                        n = R if s == 2 else P
                                        for kt in range(3):
                                            K = KROWS[kt]
                                            pe.matmul(col_ps[R * r:R * r + n, l, ki, s, 0:B],
                                                      wa[0:K, l, kt, six * C + s * P:six * C + s * P + n],
                                                      sT[0:K, kt, :], start=kt == 0, stop=kt == 2)
                            for gi, six in enumerate((2, 5)):
                                for b in range(B):
                                    n = 2 * gi + b
                                    if l > 0 and n == 0:
                                        pe.wait_ge(dve_done.sem, dve_done.at(4 + 4 * l))
                                    for kt in range(3):
                                        K = KROWS[kt]
                                        mm = pe.matmul(gate_ps[:, n, 0:C], sTb[0:K, kt, b, :],
                                                       wa[0:K, l, kt, six * C:six * C + C],
                                                       start=kt == 0, stop=kt == 2)
                            mm.then_inc(pe_done.sem, 1)

                    @block.vector
                    def _(dve):
                        dve.wait_ge(act_done.sem, act_done.at(3))
                        for s in range(3):
                            K = KROWS[s]
                            dve.tensor_copy(sTb[0:K, s, :, :],
                                            sT[0:K, s, :].unsqueeze(2).broadcast_to([K, B, P])).then_inc(dve_done.sem, 1)
                        dve.tensor_copy(identb[:, :], ident[:, :]).then_inc(dve_done.sem, 1)
                        for l in range(3):
                            dve.wait_ge(pe_done.sem, pe_done.at(l + 1))
                            for gi in range(2):
                                for b in range(B):
                                    dve.tensor_tensor(gate_b[:, l, gi, b, :], gate_ps[:, 2 * gi + b, 0:C],
                                                      bias_g[:, l, gi, :], ALU.add).then_inc(dve_done.sem, 1)
                        dve.wait_ge(pool_done.sem, pool_done.at(4))
                        for l in range(3):
                            for ki in range(4):
                                for s in range(3):
                                    n = SLAB[s]
                                    dve.tensor_scalar(modc[0:n, l, ki, s, :], col_ps[0:n, l, ki, s, 0:B],
                                                      bias_c[0:n, l, ki, s:s + 1], float(ki % 2), ALU.add, ALU.add
                                                      ).then_inc(dve_done.sem, 1)
                        for t in range(NT):
                            dve.bn_stats(stats[:, t, :], x[:, t, :]).then_inc(dve_done.sem, 1)
                loaded.passed(16 * ALL)
                act_done.passed(3)
                pool_done.passed(4)
                pe_done.passed(3)
                dve_done.passed(4 + 12 + 36 + NT)

        def rotation():
            with ExitStack() as ctx:
                z = sb("z", [QR_P, QR_T, RK], ctx=ctx)
                row_mask = sb("row_mask", [QR_P, QR_T, RK], ctx=ctx)
                v = sb("v", [QR_P, QR_T], ctx=ctx)
                e = sb("e", [QR_P, 1], ctx=ctx)
                ya = sb("ya", [QR_P, 2, RK], ctx=ctx)
                small = sb("small", [QR_P, 8], ctx=ctx)
                wr = sb("wr", [QR_P, RK], ctx=ctx)
                dots = bank("dots", ctx)
                two = bank("two", ctx)
                wide = bank("wide", ctx)
                wide2 = bank("wide2", ctx)
                with nc.Block() as block:
                    @block.sync
                    def _(sp):
                        sp.dma_start(z[:, :, :], w["rot_P"].rearrange("(t p) d -> p t d", p=QR_P)).then_inc(loaded.sem, 16)
                        sp.dma_start(row_mask[:, :, :], w["const_rows"].rearrange("(t p) d -> p t d", p=QR_P)
                                     ).then_inc(loaded.sem, 16)

                    @block.vector
                    def _(dve):
                        dve.wait_ge(loaded.sem, loaded.at(32))
                        with dve.Fori(0, RK) as j:
                            STEPS = 11

                            def chain(ins, k):
                                ins.then_inc(qr_step.sem, 1)
                                dve.wait_ge(qr_step.sem, qr_step.at(STEPS * j + k))

                            chain(dve.tensor_tensor(v[:, :], z[:, :, bass.ds(j, 1)].rearrange("p t o -> p (t o)"),
                                                    row_mask[:, :, bass.ds(j, 1)].rearrange("p t o -> p (t o)"),
                                                    ALU.mult), 1)
                            dve.tensor_copy(e[:, :], ident[0:QR_P, bass.ds(j, 1)]).then_inc(qr_col.sem, 1)
                            dve.wait_ge(qr_copy.sem, qr_copy.at(2 * j + 2))
                            alpha = ya[:, 1, bass.ds(j, 1)]
                            norm2 = ya[:, 0, bass.ds(j, 1)]
                            chain(dve.tensor_scalar(small[:, 1:2], alpha, 0.0, 2.0, ALU.is_ge, ALU.mult), 2)
                            chain(dve.scalar_tensor_tensor(small[:, 2:3], small[:, 1:2], -1.0, small[:, 0:1],
                                                           ALU.add, ALU.mult), 3)
                            chain(dve.scalar_tensor_tensor(small[:, 3:4], alpha, small[:, 2:3], norm2,
                                                           ALU.mult, ALU.add), 4)
                            chain(dve.tensor_scalar(small[:, 4:5], small[:, 3:4], 1e-37, None, ALU.max), 5)
                            chain(dve.reciprocal(small[:, 5:6], small[:, 4:5]), 6)
                            chain(dve.scalar_tensor_tensor(wr[:, :], ya[:, 1, :], small[:, 2:3], ya[:, 0, :],
                                                           ALU.mult, ALU.add), 7)
                            chain(dve.scalar_tensor_tensor(v[:, 0:1], e[:, :], small[:, 2:3], v[:, 0:1],
                                                           ALU.mult, ALU.add), 8)
                            chain(dve.tensor_scalar(wr[:, :], wr[:, :], small[:, 5:6], -1.0, ALU.mult, ALU.mult), 9)
                            for t in range(QR_T):
                                ins = dve.scalar_tensor_tensor(z[:, t, :], wr[:, :], v[:, t:t + 1], z[:, t, :],
                                                               ALU.mult, ALU.add)
                                if t == 1:
                                    ins.then_inc(qr_step.sem, 1)
                            chain(ins, 11)

                    @block.tensor
                    def _(pe):
                        with pe.Fori(0, RK) as j:
                            pe.wait_ge(qr_col.sem, qr_col.at(j + 1))
                            pe.wait_ge(qr_copy.sem, qr_copy.at(2 * j))
                            for t in range(QR_T):
                                pe.matmul(dots[0:QR_P, 0:RK], v[:, t:t + 1].broadcast_to([QR_P, QR_P]), z[:, t, :], start=t == 0, stop=t == QR_T - 1)
                            pe.matmul(dots[0:QR_P, RK:2 * RK], e[:, :].broadcast_to([QR_P, QR_P]), z[:, 0, :], start=True, stop=True
                                      ).then_inc(qr_dots.sem, 1)

                    @block.scalar
                    def _(act):
                        act.preload_act_table(ACT.Sqrt)
                        with act.Fori(0, RK) as j:
                            act.wait_ge(qr_dots.sem, qr_dots.at(j + 1))
                            act.activation(ya[:, :, :].rearrange("p a b -> p (a b)"), dots[0:QR_P, 0:2 * RK], ACT.Copy
                                           ).then_inc(qr_copy.sem, 1)
                            act.activation(small[:, 0:1], dots[0:QR_P, bass.ds(j, 1)], ACT.Sqrt).then_inc(qr_copy.sem, 1)
                loaded.passed(32)
                qr_step.passed(11 * RK)
                qr_col.passed(RK)
                qr_dots.passed(RK)
                qr_copy.passed(2 * RK)

                INV = 6
                KROWS = (P, P, R)
                tri = sb("tri", [RK, 2, RK], ctx=ctx)
                pT = sb("pT", [RK, C], ctx=ctx)
                uT = sb("uT", [RK, C], ctx=ctx)
                power = sb("power", [RK, 2, RK], ctx=ctx)
                prod = sb("prod", [RK, RK], ctx=ctx)
                tmp = sb("tmp", [RK, RK], ctx=ctx)
                s1 = sb("s1", [RK, 8], ctx=ctx)
                wv = sb("wv", [P, 3, 8, 512], ctx=ctx)
                bias_v = sb("bias_v", [B, 8, 512], ctx=ctx)
                vrow = sb("vrow", [B, 8, 512], ctx=ctx)
                skew = sb("skew", [RK, B, 2, RK], ctx=ctx)
                up = sb("up", [RK, B, RK], ctx=ctx)
                term = sb("term", [RK, B, 2, RK], ctx=ctx)
                sq = sb("sq", [RK, B, 2, RK], ctx=ctx)
                kept = sb("kept", [RK, B, 2, RK], ctx=ctx)
                absA = sb("absA", [RK, B, RK], ctx=ctx)
                rs = sb("rs", [RK, B], ctx=ctx)
                big = sb("big", [B, 1], ctx=ctx)
                bigd = sb("bigd", [B, B], ctx=ctx)
                onesr = sb("onesr", [B, RK], ctx=ctx)
                nrm = sb("nrm", [RK, B], ctx=ctx)
                pw = sb("pw", [RK, 3, SQUARINGS], ctx=ctx)
                gt = sb("gt", [RK, B, SQUARINGS], ctx=ctx)
                ngt = sb("ngt", [RK, B, SQUARINGS], ctx=ctx)
                sf = sb("sf", [RK, B, SQUARINGS], ctx=ctx)
                sc = sb("sc", [RK, B], ctx=ctx)
                g_u = sb("g_u", [RK, B, C], ctx=ctx)
                condT = sb("condT2", [P, 3, B], ctx=ctx)
                NL = 3 + 2 * 3 + B
                HORNER = TAYLOR - 1
                mark = {}
                eye4 = tri[:, 1, :].unsqueeze(1).broadcast_to([RK, 2 * B, RK])
                sk4 = skew[:, :, :, :].rearrange("p b s c -> p (b s) c")
                tm4 = term[:, :, :, :].rearrange("p b s c -> p (b s) c")
                sq4 = sq[:, :, :, :].rearrange("p b s c -> p (b s) c")
                two4 = two[0:RK, 0:2 * B * RK].rearrange("p (a c) -> p a c", a=2 * B)

                with nc.Block() as block:
                    @block.vector
                    def _(dve):
                        step = Chain(dve, dve_done)
                        products = 0

                        def product():
                            nonlocal products
                            products += 1
                            dve.wait_ge(pe_done.sem, pe_done.at(products))

                        dve.wait_ge(loaded.sem, loaded.at(16 * NL))
                        for c in range(8):
                            product()
                            mark["row", c] = step(dve.tensor_tensor(vrow[:, c, :], (wide if c % 2 == 0 else wide2)[0:B, :],
                                                                    bias_v[:, c, :], ALU.add))
                        dve.wait_ge(loaded.sem, loaded.at(16 * (NL + B)))
                        product()
                        tr = two[0:RK, 0:B * RK].rearrange("p (b c) -> p b c", b=B)
                        step(dve.tensor_tensor(skew[:, :, 0, :], up[:, :, :], tr, ALU.subtract))
                        step(dve.tensor_scalar(skew[:, :, 1, :], skew[:, :, 0, :], -1.0, None, ALU.mult))
                        step(dve.tensor_tensor(absA[:, :, :], skew[:, :, 0, :], skew[:, :, 1, :], ALU.max))
                        step(dve.tensor_reduce(rs[:, :], absA[:, :, :], AX_X, ALU.add))
                        mark["sums"] = step(dve.memset(onesr[:, :], 1.0))
                        product()
                        step(dve.tensor_reduce(big[:, :], wide[0:B, 0:RK], AX_X, ALU.max))
                        mark["norm"] = step(dve.tensor_scalar(bigd[:, :], ident[0:B, 0:B], big[:, 0:1], None, ALU.mult))
                        product()
                        step(dve.tensor_copy(nrm[:, :], wide2[0:RK, 0:B]))
                        for b in range(B):
                            step(dve.tensor_scalar(gt[:, b, :], pw[:, 0, :], nrm[:, b:b + 1], None, ALU.is_lt))
                        step(dve.tensor_scalar(ngt[:, :, :], gt[:, :, :], -1.0, 1.0, ALU.mult, ALU.add))
                        step(dve.tensor_tensor(sf[:, :, :], gt[:, :, :],
                                               pw[:, 1, :].unsqueeze(1).broadcast_to([RK, B, SQUARINGS]), ALU.mult))
                        step(dve.tensor_reduce(sc[:, :], sf[:, :, :], AX_X, ALU.min))
                        step(dve.tensor_scalar(sc[:, :], sc[:, :], 1.0, None, ALU.add))
                        for b in range(B):
                            step(dve.tensor_scalar(skew[:, b, :, :], skew[:, b, :, :], sc[:, b:b + 1], None, ALU.mult))
                        step(dve.tensor_scalar(sq4, sk4, 1.0 / TAYLOR, None, ALU.mult))
                        mark["first"] = step(dve.tensor_tensor(tm4, sq4, eye4, ALU.add))
                        with dve.Fori(0, HORNER) as i:
                            dve.wait_ge(up_ready.sem, up_ready.at(i + 1))
                            dve.tensor_scalar(sq4, two4, pw[:, 2, bass.ds(i, 1)], None, ALU.mult).then_inc(g_hi.sem, 1)
                            dve.wait_ge(g_hi.sem, g_hi.at(i + 1))
                            dve.tensor_tensor(tm4, sq4, eye4, ALU.add).then_inc(g_split.sem, 1)
                        dve.wait_ge(g_split.sem, g_split.at(HORNER))
                        with dve.Fori(0, SQUARINGS) as i:
                            for b in range(B):
                                dve.tensor_scalar(kept[:, b, :, :], term[:, b, :, :], ngt[:, b, bass.ds(i, 1)], None,
                                                  ALU.mult).then_inc(modulated.sem, 1)
                            dve.wait_ge(modulated.sem, modulated.at(2 * i + 2))
                            dve.wait_ge(mm_done.sem, mm_done.at(i + 1))
                            for b in range(B):
                                ins = dve.scalar_tensor_tensor(
                                    term[:, b, :, :], two[0:RK, 2 * b * RK:(2 * b + 2) * RK].rearrange("p (s c) -> p s c", s=2),
                                    gt[:, b, bass.ds(i, 1)], kept[:, b, :, :], ALU.mult, ALU.add)
                            ins.then_inc(added.sem, 1)
                            dve.wait_ge(added.sem, added.at(i + 1))
                        step(dve.tensor_tensor(tm4, tm4, eye4, ALU.subtract))

                        step(dve.tensor_tensor(tmp[:, :], z[0:RK, 0, :], tri[:, 1, :], ALU.mult))
                        step(dve.tensor_reduce(s1[:, 0:1], tmp[:, :], AX_X, ALU.add))
                        step(dve.reciprocal(s1[:, 1:2], s1[:, 0:1]))
                        step(dve.tensor_tensor(tmp[:, :], z[0:RK, 0, :], tri[:, 0, :], ALU.mult))
                        step(dve.tensor_scalar(power[:, 0, :], tmp[:, :], s1[:, 1:2], -1.0, ALU.mult, ALU.mult))
                        mark["power", 0] = step(dve.tensor_tensor(prod[:, :], power[:, 0, :], tri[:, 1, :], ALU.add))
                        product()
                        mark["turned"] = step(dve.tensor_copy(power[:, 1, :], wide[0:RK, 0:RK]))
                        for k in range(1, INV):
                            product()
                            mark["power", k] = step(dve.tensor_copy(power[:, :, :].rearrange("p a c -> p (a c)"),
                                                                    wide[0:RK, 0:2 * RK]))
                            product()
                            mark["prod", k] = step(dve.tensor_tensor(prod[:, :], wide2[0:RK, 0:RK], prod[:, :], ALU.add))
                        product()
                        mark["uT"] = step(dve.tensor_scalar(uT[:, :], wide2[0:RK, 0:C], s1[:, 1:2], None, ALU.mult))
                        product()
                        for b in range(B):
                            mark["g", b] = step(dve.tensor_copy(g_u[:, b, :], (wide if b == 0 else wide2)[0:RK, 0:C]))
                        for i in range(3 * B):
                            K = KROWS[i % 3]
                            product()
                            mark["m", i] = step(dve.tensor_copy(m_rot[0:K, i // 3, i % 3, :],
                                                                (wide if i % 2 == 0 else wide2)[0:K, 0:C]))
                        mark["steps"] = step.n
                        mark["products"] = products

                    @block.sync
                    def _(sp):
                        def load(dst, src):
                            sp.dma_start(dst, src).then_inc(loaded.sem, 16)
                        load(tri[:, :, :], w["const_tri"])
                        load(pT[:, :], w["rot_PT"])
                        load(pw[:, :, :], w["const_pow"])
                        for s in range(3):
                            load(condT[0:KROWS[s], s, :], w["condT"][s * P:s * P + KROWS[s], :])
                            load(wv[0:KROWS[s], s, :, :].rearrange("p a b -> p (a b)"), w["rot_W"][s * P:s * P + KROWS[s], :])
                        for b in range(B):
                            load(bias_v[b:b + 1, :, :].rearrange("p a b -> p (a b)"), w["rot_b"])
                        sp.wait_ge(dve_done.sem, dve_done.at(mark["row", 7]))
                        for b in range(B):
                            load(up[:, b, :], vrow[b:b + 1, :, :].rearrange("o a b -> o (a b)").rearrange(
                                "o (i j) -> o i j", j=RK))

                    @block.scalar
                    def _(act):
                        act.wait_ge(loaded.sem, loaded.at(16 * NL))
                        for s in range(3):
                            act.activation(condT[0:KROWS[s], s, :], condT[0:KROWS[s], s, :], ACT.Silu).then_inc(
                                act_done.sem, 1)

                    @block.tensor
                    def _(pe):
                        def after(name):
                            pe.wait_ge(dve_done.sem, dve_done.at(mark[name]))

                        def done(ins):
                            ins.then_inc(pe_done.sem, 1)

                        pe.wait_ge(act_done.sem, act_done.at(3))
                        for c in range(8):
                            if c > 1:
                                after(("row", c - 2))
                            for kt in range(3):
                                K = KROWS[kt]
                                mm = pe.matmul((wide if c % 2 == 0 else wide2)[0:B, :], condT[0:K, kt, :], wv[0:K, kt, c, :],
                                               start=kt == 0, stop=kt == 2)
                            done(mm)
                        pe.wait_ge(loaded.sem, loaded.at(16 * (NL + B)))
                        for b in range(B):
                            mm = pe.transpose(two[0:RK, b * RK:(b + 1) * RK], up[:, b, :], ident[0:RK, 0:RK])
                        done(mm)
                        after("sums")
                        done(pe.transpose(wide[0:B, 0:RK], rs[:, :], ident[0:RK, 0:RK]))
                        after("norm")
                        done(pe.matmul(wide2[0:RK, 0:B], onesr[:, :], bigd[:, :], start=True, stop=True))
                        after("first")

                        def four(left):
                            for b in range(B):
                                for s in (1, 0):
                                    o = (2 * b + s) * RK
                                    if b == 0 and s == 1:
                                        pe.matmul(two[:, o:o + RK], left[:, b, :, :].rearrange("p s c -> p (s c)"),
                                                  term[:, b, s, :], start=True, stop=True)
                                        continue
                                    mm = pe.matmul(two[0:RK, o:o + RK], left[:, b, 1 - s, :], term[:, b, s, :],
                                                   start=True, stop=True)
                            return mm

                        with pe.Fori(0, HORNER) as i:
                            pe.wait_ge(g_split.sem, g_split.at(i))
                            four(skew).then_inc(up_ready.sem, 1)
                        pe.wait_ge(g_split.sem, g_split.at(HORNER))
                        with pe.Fori(0, SQUARINGS) as i:
                            pe.wait_ge(added.sem, added.at(i))
                            four(term).then_inc(mm_done.sem, 1)
                        after(("power", 0))
                        done(pe.transpose(wide[0:RK, 0:RK], power[:, 0, :], ident[0:RK, 0:RK]))
                        after("turned")
                        for k in range(1, INV):
                            pe.matmul(wide[0:RK, 0:RK], power[:, 1, :], power[:, 0, :], start=True, stop=True)
                            done(pe.matmul(wide[0:RK, RK:2 * RK], power[:, 0, :], power[:, 1, :], start=True, stop=True))
                            after(("power", k))
                            done(pe.matmul(wide2[0:RK, 0:RK], power[:, 1, :], prod[:, :], start=True, stop=True))
                            after(("prod", k))
                        done(pe.matmul(wide2[0:RK, 0:C], prod[:, :], pT[:, :], start=True, stop=True))
                        after("uT")
                        for b in range(B):
                            mm = pe.matmul((wide if b == 0 else wide2)[0:RK, 0:C], term[:, b, 1, :], uT[:, :],
                                           start=True, stop=True)
                        done(mm)
                        after(("g", 1))
                        for i in range(3 * B):
                            if i > 1:
                                after(("m", i - 2))
                            K, s = KROWS[i % 3], i % 3
                            done(pe.matmul((wide if i % 2 == 0 else wide2)[0:K, 0:C], uT[:, s * P:s * P + K],
                                           g_u[:, i // 3, :], start=True, stop=True))
                loaded.passed(16 * (NL + B))
                act_done.passed(3)
                dve_done.passed(mark["steps"])
                pe_done.passed(mark["products"])
                for s in (up_ready, g_hi, g_split):
                    s.passed(HORNER)
                modulated.passed(2 * SQUARINGS)
                mm_done.passed(SQUARINGS)
                added.passed(SQUARINGS)

        def split_weights(width, hi, lo, third, raw, tail, bias, landed, counted, cols=None):
            given = cols or width

            def load(sp, w_dram, bias_dram):
                for s in range(2):
                    sp.dma_start(raw[:, s, 0:given], w_dram[s * P:s * P + P, :]).then_inc(landed.sem, 16)
                for r in range(3):
                    sp.dma_start(raw[R * r:R * r + R, 2, 0:given], w_dram[2 * P:C, :]).then_inc(landed.sem, 16)
                for r in range(2 if bias else 0):
                    sp.dma_start(raw[RS + r:RS + r + 1, 2, 0:width], bias_dram).then_inc(landed.sem, 16)

            def split(dve):
                step = Chain(dve, counted)
                dve.wait_ge(landed.sem, landed.at(loads))
                step(dve.tensor_copy(hi[:, :, :], raw[:, 0:2, 0:width]))
                dve.tensor_tensor(lo[:, :, :], raw[:, 0:2, 0:width], hi[:, :, :].bitcast(F32), ALU.subtract)
                step(dve.tensor_copy(third[0:RA, :], raw[0:RA, 2, 0:width]))
                step(dve.tensor_tensor(tail[:, :], raw[0:RA, 2, 0:width], third[0:RA, :].bitcast(F32), ALU.subtract))
                step(dve.tensor_scalar(tail[:, :], tail[:, :], mix[0:RA, 1:2], None, ALU.mult))
                step(dve.scalar_tensor_tensor(third[0:RA, :], third[0:RA, :].bitcast(F32), mix[0:RA, 0:1], tail[:, :],
                                              ALU.mult, ALU.add))

            loads = 16 * (7 if bias else 5)

            def passed():
                landed.passed(loads)
                counted.passed(SPLIT_STEPS)
            return load, split, passed

        def deviations(dve, act, tiles):
            t0, t1 = tiles
            if dve is not None:
                for t in range(t0, t1):
                    dve.bn_aggr(mv[:, t, :], stats[:, t, :]).then_inc(stats_in.sem, 1)
                dve.wait_ge(std_ready.sem, std_ready.at(1))
                dve.reciprocal(rstd[:, t0:t1], std[:, t0:t1]).then_inc(rstd_ready.sem, 1)
                dve.wait_ge(rstd_ready.sem, rstd_ready.at(1))
            if act is not None:
                act.preload_act_table(ACT.Sqrt)
                act.wait_ge(stats_in.sem, stats_in.at(t1 - t0))
                act.activation(std[:, t0:t1], mv[:, t0:t1, 1], ACT.Sqrt, bias=eps_col[:, 0:1]).then_inc(std_ready.sem, 1)

        def norm_stages(ctx, l, ki, xn, m, turn_ps, hi_at, lo_at, third_at, reused):

            def normalise(dve, t, tile, k):
                dve.wait_ge(turned.sem, turned.at(t - 1))
                dve.tensor_scalar(xn[:, k, 0:2 * P], x[:, tile, 0:2 * P], mv[:, tile, 0:1], rstd[:, bass.ds(tile, 1)], ALU.subtract, ALU.mult)
                dve.tensor_scalar(xn[:, k, 2 * P:2 * P + RS].rearrange("p (r c) -> p r c", r=3),
                                  x[:, tile, 2 * P:C].unsqueeze(1).broadcast_to([P, 3, R]), mv[:, tile, 0:1],
                                  rstd[:, bass.ds(tile, 1)],
                                  ALU.subtract, ALU.mult).then_inc(normed.sem, 1)

            def turn(pe, t, k):
                pe.wait_ge(normed.sem, normed.at(t + 1))
                pe.wait_ge(modulated.sem, modulated.at(t - 1))
                for s in range(3):
                    n = RA if s == 2 else P
                    mm = pe.transpose(turn_ps[k][0:n, s * P:s * P + P], xn[:, k, s * P:s * P + n], ident[:, :])
                mm.then_inc(turned.sem, 1)

            def modulate(act, t, b, k):
                act.wait_ge(turned.sem, turned.at(t + 1))
                act.wait_ge(split_done.sem, split_done.at(t - 1))
                for s in range(3):
                    n = RA if s == 2 else P
                    a = act.activation(m[0:n, k, s, :], turn_ps[k][0:n, s * P:s * P + P], ACT.Identity,
                                       scale=modc[0:n, l, ki + 1, s, b:b + 1], bias=modc[0:n, l, ki, s, b:b + 1])
                a.then_inc(modulated.sem, 1)

            def split(dve, t, k):
                dve.wait_ge(modulated.sem, modulated.at(t + 1))
                if reused:
                    dve.wait_ge(qkv_ready.sem, qkv_ready.at(t - 1))
                hi, lo, third = hi_at(t, k), lo_at(t, k), third_at(t, k)
                dve.tensor_copy(hi, m[:, k, 0:2, :])
                dve.tensor_copy(third[0:RA], m[0:RA, k, 2, :]).then_inc(hi_ready.sem, 1)
                dve.wait_ge(hi_ready.sem, hi_ready.at(t + 1))
                dve.tensor_tensor(lo, m[:, k, 0:2, :], hi.bitcast(F32), ALU.subtract)
                dve.tensor_tensor(third[R:2 * R], m[R:2 * R, k, 2, :], third[R:2 * R].bitcast(F32), ALU.subtract
                                  ).then_inc(split_done.sem, 1)
            return normalise, turn, modulate, split

        def split_products(pe, out_ap, lhs, rhs):
            (lh, ll, l3), (rh, rl, r3) = lhs, rhs
            n = 0
            for s in range(2):
                for a, b in ((lh, rh), (lh, rl), (ll, rh)):
                    pe.matmul(out_ap, a(s), b(s), start=n == 0, stop=False)
                    n += 1
            return pe.matmul(out_ap, l3, r3, start=False, stop=True)

        class LayerMemory:

            def __init__(self, l, ctx):
                self.l = l
                self.qs = sb(f"qs{l}", [P, RING, L], BF16, ctx=ctx)
                self.ks = sb(f"ks{l}", [P, RING, L], BF16, ctx=ctx)
                self.wp = sb(f"wp{l}", [P, G, C], ctx=ctx)
                given = self.ks[:, :, :].rearrange("p r c -> p (r c)").bitcast(F32)
                self.raw = given[:, 0:9 * C].rearrange("p (s c) -> p s c", s=3)
                self.tail = given[0:RA, 9 * C:12 * C]

            def splitter(self, ctx):
                self.hi = sb(f"wqh{self.l}", [P, 2, 3 * C], F32R, ctx=ctx)
                self.lo = sb(f"wql{self.l}", [P, 2, 3 * C], F32R, ctx=ctx)
                self.third = sb(f"wq3{self.l}", [RA, 3 * C], F32R, ctx=ctx)
                return split_weights(3 * C, self.hi, self.lo, self.third, self.raw, self.tail, True, w_loaded, w_step)

            def load_qkv(self, sp):
                w_dram, bias_dram = w["qkv_w"][self.l], w["qkv_b"][self.l]
                for s in range(2):
                    sp.dma_start(self.raw[:, s, :], w_dram[s * P:s * P + P, :]).then_inc(w_loaded.sem, 16)
                for r in range(3):
                    sp.dma_start(self.raw[R * r:R * r + R, 2, :], w_dram[2 * P:C, :]).then_inc(w_loaded.sem, 16)
                for r in range(2):
                    sp.dma_start(self.raw[RS + r:RS + r + 1, 2, :], bias_dram).then_inc(w_loaded.sem, 16)

            def clear_projection(self, pool):
                pool.memset(self.wp[:, :, :], 0.0).then_inc(wp_cleared.sem, 1)

            def load_projection(self, sp):
                sp.wait_ge(wp_cleared.sem, wp_cleared.at(1))
                for g in range(G):
                    for j in range(4):
                        h = 4 * g + j
                        sp.dma_start(self.wp[32 * j:32 * j + D, g, :], w["proj_w"][self.l][h * D:(h + 1) * D, :]
                                     ).then_inc(proj_loaded.sem, 16)
                sp.dma_start(self.wp[D:D + 1, 0, :], w["proj_b"][self.l]).then_inc(proj_loaded.sem, 16)

        def qkv_phase(l, b, mem, stack, val):
            with ExitStack() as ctx:
                load_wq, split_wq, wq_passed = mem.splitter(ctx)
                wh, wl, w3 = mem.hi, mem.lo, mem.third
                xn = sb(f"xn{l}{b}", [P, 2, XN], ctx=ctx)
                m = sb(f"m{l}{b}", [P, 2, 3, P], ctx=ctx)
                ph = sb(f"ph{l}{b}", [P, 2, 2, P], F32R, ctx=ctx)
                pl = sb(f"pl{l}{b}", [P, 2, 2, P], F32R, ctx=ctx)
                p3 = sb(f"p3{l}{b}", [RA, 2, P], F32R, ctx=ctx)
                qk = sb(f"qk{l}{b}", [P, 2, 2, H, D], ctx=ctx)
                rem = sb(f"rem{l}{b}", [P, 2, H, D], ctx=ctx)
                turn_ps = [bank(f"turn{l}{b}{k}", ctx) for k in range(2)]
                qkv_ps = [[bank(f"qkv{l}{b}{k}{n}", ctx) for n in range(3)] for k in range(2)]
                is3 = l == 2
                if is3:
                    cen = mem.qs[:, 0:2, :].rearrange("p r c -> p (r c)").bitcast(F32)[:, 0:2 * C].rearrange("p (h d) -> p h d", d=D)
                    hs = sb(f"hs{b}", [P, 4, 2 * H], ctx=ctx)
                    gqk = sb(f"gqk{b}", [P, 2, D], ctx=ctx)
                normalise, turn, modulate, split = norm_stages(
                    ctx, l, 0, xn, m, turn_ps, lambda t, k: ph[:, k], lambda t, k: pl[:, k], lambda t, k: p3[:, k], True)

                with nc.Block() as block:
                    @block.sync
                    def _(sp):
                        if is3:
                            for n, g in enumerate((w["g_q"], w["g_k"])):
                                sp.dma_start(gqk[:, n, :], g.rearrange("(o c) -> o c", o=1).broadcast_to([P, D])
                                             ).then_inc(loaded.sem, 16)
                        if is3 and b == 0:
                            mem.load_qkv(sp)
                        if b == 0:
                            mem.load_projection(sp)

                    @block.gpsimd
                    def _(pool):
                        pool.memset(xn[:, :, 2 * P + RS:XN], 1.0).then_inc(pool_done.sem, 1)
                        if b == 0:
                            mem.clear_projection(pool)
                        for t in range(TB):
                            pool.memset(stack[:, t, 1, :, KD:KA], 1.0).then_inc(pool_done.sem, 1)
                        pool.memset(val[:, :, :, D:D + 1], 1.0).then_inc(pool_done.sem, 1)
                        pool.memset(val[:, :, :, D + 1:32], 0.0).then_inc(pool_done.sem, 1)
                        with pool.Fori(0, TB) as t:
                            pool.wait_ge(qk_split.sem, qk_split.at(t + 1))

                            def slot(a, s):
                                return stack[:, t, a, :, s * D:(s + 1) * D]

                            pool.tensor_copy(slot(0, 3), slot(0, 0))
                            pool.tensor_copy(slot(0, 4), slot(0, 0))
                            pool.tensor_copy(slot(0, 5), slot(0, 1))
                            pool.tensor_copy(slot(1, 2), slot(1, 0))
                            pool.tensor_copy(slot(1, 5), slot(1, 0))
                            pool.tensor_copy(slot(1, 3), slot(1, 1))

                    def qkv(pe, t, k):
                        pe.wait_ge(split_done.sem, split_done.at(t + 1))
                        pe.wait_ge(qkv_taken.sem, qkv_taken.at(t - 1))
                        for n in range(3):
                            cols = slice(n * C, n * C + C)
                            mm = split_products(
                                pe, qkv_ps[k][n][:, 0:C],
                                (lambda s: ph[:, k, s, :], lambda s: pl[:, k, s, :], p3[0:RA, k, :]),
                                (lambda s: wh[:, s, cols], lambda s: wl[:, s, cols], w3[0:RA, cols]))
                        mm.then_inc(qkv_ready.sem, 1)

                    def take(act, t, k):
                        act.wait_ge(qkv_ready.sem, qkv_ready.at(t + 1))
                        act.wait_ge(qk_split.sem, qk_split.at(t - 1))
                        for n in range(2):
                            act.activation(qk[:, k, n, :, :].rearrange("p h d -> p (h d)"), qkv_ps[k][n][:, 0:C], ACT.Copy,
                                           scale=SCALE if n == 0 and not is3 else 1.0)
                        act.activation(val[:, t, :, 0:D], qkv_ps[k][2][:, 0:C].rearrange("p (h d) -> p h d", h=H),
                                       ACT.Copy).then_inc(qkv_taken.sem, 1)
                        if is3:
                            act.wait_ge(qk_step.sem, qk_step.at(11 * t + 5))
                            act.activation(hs[:, 2, :], hs[:, 1, :], ACT.Sqrt, scale=1.0 / D, bias=eps_col[:, 0:1]
                                           ).then_inc(qk_std.sem, 1)

                    per = 11 if is3 else 3

                    def parts(dve, t, k):
                        n = 0

                        def link(ins):
                            nonlocal n
                            n += 1
                            ins.then_inc(qk_step.sem, 1)
                            dve.wait_ge(qk_step.sem, qk_step.at(per * t + n))
                        dve.wait_ge(qkv_taken.sem, qkv_taken.at(t + 1))
                        both = qk[:, k, :, :, :].rearrange("p a h d -> p (a h) d")
                        if is3:
                            link(dve.tensor_reduce(hs[:, 0, :], both, AX_X, ALU.add))
                            link(dve.tensor_scalar(hs[:, 0, :], hs[:, 0, :], 1.0 / D, None, ALU.mult))
                            link(dve.tensor_tensor(both, both, hs[:, 0, :].unsqueeze(2).broadcast_to([P, 2 * H, D]),
                                                   ALU.subtract))
                            link(dve.tensor_tensor(cen[:, :, :], both, both, ALU.mult))
                            link(dve.tensor_reduce(hs[:, 1, :], cen[:, :, :], AX_X, ALU.add))
                            dve.wait_ge(qk_std.sem, qk_std.at(t + 1))
                            link(dve.reciprocal(hs[:, 3, :], hs[:, 2, :]))
                            link(dve.tensor_tensor(both, both, hs[:, 3, :].unsqueeze(2).broadcast_to([P, 2 * H, D]),
                                                   ALU.mult))
                            link(dve.tensor_tensor(qk[:, k, :, :, :].rearrange("p a h d -> p a h d"), qk[:, k, :, :, :],
                                                   gqk[:, :, :].unsqueeze(2).broadcast_to([P, 2, H, D]), ALU.mult))
                        src = qk[:, k, :, :, :]
                        def slot(a, s):
                            return stack[:, t, a, :, s * D:(s + 1) * D]
                        for a in range(2):
                            ins = dve.tensor_copy(slot(a, 0), src[:, a])
                        link(ins)
                        for a in range(2):
                            ins = dve.tensor_tensor(rem[:, a, :, :], src[:, a], slot(a, 0), ALU.subtract)
                        link(ins)
                        for a in range(2):
                            ins = dve.tensor_copy(slot(a, 1), rem[:, a, :, :])
                        link(ins)
                        dve.tensor_tensor(slot(0, 2), rem[:, 0, :, :], slot(0, 1), ALU.subtract)
                        dve.tensor_tensor(slot(1, 4), rem[:, 1, :, :], slot(1, 1), ALU.subtract).then_inc(qk_split.sem, 1)

                    @block.tensor
                    def _(pe):
                        turn(pe, 0, 0)
                        turn(pe, 1, 1)
                        pe.wait_ge(w_step.sem, w_step.at(SPLIT_STEPS))
                        with pe.Fori(0, TB // 2 - 1) as i:
                            for k in range(2):
                                qkv(pe, 2 * i + k, k)
                                turn(pe, 2 * i + k + 2, k)
                        qkv(pe, TB - 2, 0)
                        qkv(pe, TB - 1, 1)

                    @block.scalar
                    def _(act):
                        if is3:
                            act.wait_ge(loaded.sem, loaded.at(32))
                        deviations(None, act, (TB * b, TB * b + TB))
                        modulate(act, 0, b, 0)
                        modulate(act, 1, b, 1)
                        with act.Fori(0, TB // 2 - 1) as i:
                            for k in range(2):
                                take(act, 2 * i + k, k)
                                modulate(act, 2 * i + k + 2, b, k)
                        take(act, TB - 2, 0)
                        take(act, TB - 1, 1)

                    @block.vector
                    def _(dve):
                        if is3:
                            dve.wait_ge(loaded.sem, loaded.at(32))
                            dve.tensor_scalar(gqk[:, 0, :], gqk[:, 0, :], SCALE, None, ALU.mult).then_inc(dve_done.sem, 1)
                            dve.wait_ge(dve_done.sem, dve_done.at(1))
                        dve.wait_ge(pool_done.sem, pool_done.at(TB + 3))
                        deviations(dve, None, (TB * b, TB * b + TB))

                        t0 = TB * b
                        normalise(dve, 0, t0, 0)
                        normalise(dve, 1, t0 + 1, 1)
                        split_wq(dve)
                        split(dve, 0, 0)
                        normalise(dve, 2, t0 + 2, 0)
                        split(dve, 1, 1)
                        with dve.Fori(0, TB // 2 - 2) as i:
                            for k in range(2):
                                normalise(dve, 2 * i + k + 3, 2 * i + (k + 3 + t0), 1 - k)
                                parts(dve, 2 * i + k, k)
                                split(dve, 2 * i + k + 2, k)
                        normalise(dve, TB - 1, t0 + TB - 1, 1)
                        parts(dve, TB - 4, 0)
                        split(dve, TB - 2, 0)
                        parts(dve, TB - 3, 1)
                        split(dve, TB - 1, 1)
                        parts(dve, TB - 2, 0)
                        parts(dve, TB - 1, 1)
                wq_passed()
                if b == 0:
                    wp_cleared.passed(1)
                if is3:
                    loaded.passed(32)
                    dve_done.passed(1)
                    qk_std.passed(TB)
                pool_done.passed(TB + 3)
                stats_in.passed(TB)
                for s in (std_ready, rstd_ready):
                    s.passed(1)
                for s in (normed, turned, modulated, hi_ready, split_done, qkv_ready, qkv_taken, qk_split):
                    s.passed(TB)
                qk_step.passed(per * TB)

        def attention_phase(l, b, mem, stack, val, oT):
            with ExitStack() as ctx:
                qs, ks = mem.qs, mem.ks
                pr = sb(f"pr{l}{b}", [P, 4, 2, 512], ctx=ctx)
                vg = sb(f"vg{l}{b}", [P, TB, 4, 32], ctx=ctx)
                o_sb = sb(f"o_sb{l}{b}", [P, 2, 512], ctx=ctx)
                inv = sb(f"inv{l}{b}", [P, 4, 4, 32], ctx=ctx)
                rec = sb(f"rec{l}{b}", [P, 16], ctx=ctx)
                mx = sb(f"mx{l}{b}", [P, 4, TB, 2], ctx=ctx)
                nm = sb(f"nm{l}{b}", [P, 4, TB], ctx=ctx)
                mr = sb(f"mr{l}{b}", [P, 4, TB], ctx=ctx)
                mp = sb(f"mp{l}{b}", [P, 4, 3, TB], BF16, ctx=ctx)
                mpT = sb(f"mpT{l}{b}", [4 * 3 * TB, P], BF16, ctx=ctx)
                t_ps = bank(f"t_ps{l}{b}", ctx)
                t_bf = t_ps[:, :].bitcast(BF16)
                row_ps = [bank(f"row_ps{l}{b}{i}", ctx) for i in range(2)]
                col_ps = [bank(f"cps{l}{b}{i}", ctx, (P, 2, 512)) for i in range(2)]
                o_ps = bank(f"o_ps{l}{b}", ctx)
                KT_N = TB
                SLOTS = 2 * KT_N
                LAG = 3

                def fills(it_up, it_down, it_tail):
                    f = []
                    for s in range(SLOTS):
                        if it_down and s == 0:
                            f.append((s, "max", 0))
                        if it_up and s % 4 == 1:
                            f.append((s, "q", s // 4 + 1))
                        if it_up and s % 4 == 2:
                            f.append((s, "k", s // 4 + 1))
                        if it_tail and s == LAG + 1:
                            f.append((s, "den", 1))
                        if it_tail and s == LAG + 2:
                            f.append((s, "inv", 1))
                        if it_down and s == KT_N + LAG + 1:
                            f.append((s, "den", 0))
                        if it_down and s == KT_N + LAG + 2:
                            f.append((s, "inv", 0))
                    return f

                FIRST, SECOND, FULL = (True, False, False), (True, True, False), (True, True, True)
                LAST, AFTER = (False, True, True), (False, False, True)
                N0, N1, NF_, NL_, NA_ = (len(fills(*a)) for a in (FIRST, SECOND, FULL, LAST, AFTER))
                TOTAL = 2 + N0 + N1 + (G - 2) * NF_ + NL_ + NA_

                def filled_before(it, kind):
                    if kind == FIRST:
                        return 2
                    if kind == SECOND:
                        return 2 + N0
                    if kind == AFTER:
                        return TOTAL - NA_
                    return 2 + N0 + N1 + (it - 2) * NF_

                def number(it, kind, what, j):
                    names = [f[1:] for f in fills(*kind)]
                    return filled_before(it, kind) + names.index((what, j))

                def downs(it, kind):
                    up, down, tail = kind
                    r = {}
                    for s in range(SLOTS):
                        if s < LAG and tail:
                            r[s] = (it - 2, SLOTS - LAG + s)
                        if s >= LAG and down:
                            r[s] = (it - 1, s - LAG)
                    return r

                def weighs(it, kind):
                    up, down, tail = kind
                    r = {}
                    for s in range(SLOTS):
                        if s <= LAG and tail:
                            r[s] = (it - 2, SLOTS - LAG - 1 + s)
                        if s > LAG and down:
                            r[s] = (it - 1, s - LAG - 1)
                    return r

                def fill_stacks(pe, group, j, what):
                    rows, a = (KD, 0) if what == "q" else (KA, 1)
                    head = (4 * group + j) % H
                    for t in range(TB):
                        ins = pe.transpose(t_bf[0:rows, t * P:t * P + P], stack[:, t, a, head, 0:rows], identb[:, :])
                    return ins

                def pe_iteration(pe, it, kind):
                    up = kind[0]
                    down_at, weigh_at = downs(it, kind), weighs(it, kind)

                    def fill(what, j):
                        n = number(it, kind, what, j)
                        pe.wait_ge(t_taken.sem, t_taken.at(n))
                        if what in "qk":
                            ins = fill_stacks(pe, it, j, what)
                        elif what == "max":
                            pe.wait_ge(max_step.sem, max_step.at(6 * it))
                            ins = pe.transpose(t_bf[0:4 * 3 * TB, 0:P], mp[:, :, :, :].rearrange("p j i t -> p (j i t)"),
                                               identb[:, :])
                        elif what == "den":
                            group = it - 1 if j == 0 else it - 2
                            pe.wait_ge(o_copied.sem, o_copied.at(2 * group + j + 1))
                            for q in range(512 // P):
                                ins = pe.matmul(t_ps[:, 4 * q:4 * q + 4], o_sb[:, j, q * P:q * P + P], sel_den[:, :],
                                                start=True, stop=True)
                        else:
                            group = it - 1 if j == 0 else it - 2
                            pe.wait_ge(inv_ready.sem, inv_ready.at(2 * group + j + 1))
                            for q in range(512 // P):
                                ins = pe.transpose(t_ps[:, q * P:q * P + P],
                                                   inv[:, q, :, :].rearrange("p j d -> p (j d)"), ident[:, :])
                        ins.then_inc(t_filled.sem, 1)

                    def scores(ge, e, pair):
                        qh, kt = e // KT_N, e % KT_N
                        n = 32 * ge + 2 * e + pair
                        pe.wait_ge(probs.sem, probs.at(n - 1))
                        for h in range(2):
                            slot = (4 * ge + 2 * pair + h) % RING
                            ins = pe.matmul(col_ps[pair][:, h, :], ks[0:KA, slot, kt * P:kt * P + P],
                                            qs[0:KA, slot, qh * 512:qh * 512 + 512], start=True, stop=True)
                        ins.then_inc(colscores.sem, 1)

                    def weigh(ge, e):
                        qh, kt = e // KT_N, e % KT_N
                        if qh == 0:
                            pe.wait_ge(v_staged.sem, v_staged.at(TB * ge + kt + 1))
                        if kt == 0:
                            pe.wait_ge(o_copied.sem, o_copied.at(2 * ge + qh))
                        pe.wait_ge(probs.sem, probs.at(32 * ge + 2 * e + 2))
                        for j in range(4):
                            ins = pe.matmul(o_ps[32 * j:32 * j + 32, :], vg[:, kt, j, :], pr[:, (2 * e + j // 2) % 4, j % 2, :],
                                            start=kt == 0, stop=kt == KT_N - 1)
                        ins.then_inc(weighed.sem, 1)

                    def maxima(s, u):
                        j = s // 4
                        if s % 4 == 0 and u == 0:
                            n = number(it, kind, "k", j) + 1 if j else filled_before(it, kind)
                            pe.wait_ge(t_taken.sem, t_taken.at(n))
                        n = 64 * it + 4 * s + u
                        t, half = (s % 4) * 2 + u // 2, u % 2
                        slot = (4 * it + j) % RING
                        pe.wait_ge(rowmax.sem, rowmax.at(n - 1))
                        pe.matmul(row_ps[u % 2][:, :], qs[0:KD, slot, t * P:t * P + P],
                                  ks[0:KD, slot, half * 512:half * 512 + 512], start=True, stop=True
                                  ).then_inc(rowscores.sem, 1)

                    for s in range(SLOTS):
                        if kind[1] and s == LAG:
                            pe.wait_ge(max_rows_in.sem, max_rows_in.at(64 * it))
                        for u in range(4):
                            if s in down_at and u % 2 == 0:
                                scores(*down_at[s], u // 2)
                            if up:
                                maxima(s, u)
                            if s in weigh_at and u == 2:
                                weigh(*weigh_at[s])
                        for slot, what, j in fills(*kind):
                            if slot == s:
                                fill(what, j)

                def act_iteration(act, it, kind):
                    down_at, weigh_at = downs(it, kind), weighs(it, kind)

                    def empty(what, j):
                        act.wait_ge(t_filled.sem, t_filled.at(number(it, kind, what, j) + 1))
                        if what == "max":
                            act.wait_ge(max_rows_in.sem, max_rows_in.at(64 * (it - 1)))
                            act.activation(mpT[:, :], t_bf[0:4 * 3 * TB, 0:P], ACT.Copy).then_inc(t_taken.sem, 1)
                        else:
                            into, rows = (qs, KD) if what == "q" else (ks, KA)
                            act.activation(into[0:rows, (4 * it + j) % RING, :], t_bf[0:rows, :], ACT.Copy
                                           ).then_inc(t_taken.sem, 1)

                    def exps(ge, e):
                        for pair in range(2):
                            n = 32 * ge + 2 * e + pair
                            act.wait_ge(colscores.sem, colscores.at(n + 1))
                            if pair == 0:
                                act.wait_ge(weighed.sem, weighed.at(16 * ge + e - 1))
                            act.activation(pr[:, (2 * e + pair) % 4, :, :], col_ps[pair][:, :, :], ACT.Exp
                                           ).then_inc(probs.sem, 1)

                    def copy_o(ge, qh):
                        act.wait_ge(weighed.sem, weighed.at(16 * ge + KT_N * (qh + 1)))
                        act.activation(o_sb[:, qh, :], o_ps[:, :], ACT.Copy).then_inc(o_copied.sem, 1)

                    for s in range(SLOTS):
                        if s in down_at:
                            exps(*down_at[s])
                        if s in weigh_at and weigh_at[s][1] % KT_N == KT_N - 1:
                            copy_o(weigh_at[s][0], weigh_at[s][1] // KT_N)
                        for slot, what, j in fills(*kind):
                            if slot == s and what in ("q", "k", "max"):
                                empty(what, j)

                def dve_iteration(dve, it, kind):
                    up = kind[0]

                    def wait_fill(what, j):
                        dve.wait_ge(t_filled.sem, t_filled.at(number(it, kind, what, j) + 1))

                    def reduce(s):
                        j = s // 4
                        for u in range(4):
                            t, half = (s % 4) * 2 + u // 2, u % 2
                            dve.wait_ge(rowscores.sem, rowscores.at(64 * it + 4 * s + u + 1))
                            dve.tensor_reduce(mx[:, j, t, half:half + 1], row_ps[u % 2][:, :], AX_X, ALU.max
                                              ).then_inc(rowmax.sem, 1)

                    def invert(ge, qh):
                        wait_fill("den", qh)
                        dve.reciprocal(rec[:, :], t_ps[:, 0:16]).then_inc(t_taken.sem, 1)
                        dve.wait_ge(t_taken.sem, t_taken.at(number(it, kind, "den", qh) + 1))
                        dve.wait_ge(inv_ready.sem, inv_ready.at(2 * ge + qh))
                        dve.tensor_copy(inv[:, :, :, :], rec[:, :].rearrange("p (q j) -> p q j", j=4).unsqueeze(3)
                                        .broadcast_to([P, 4, 4, 32])).then_inc(inv_ready.sem, 1)

                    def normalise(ge, qh):
                        wait_fill("inv", qh)
                        dve.tensor_tensor(oT[:, ge, qh * 512:qh * 512 + 512], o_sb[:, qh, :], t_ps[:, :], ALU.mult
                                          ).then_inc(t_taken.sem, 1)

                    def maximum_parts():
                        n = 0

                        def link(ins):
                            nonlocal n
                            n += 1
                            ins.then_inc(max_step.sem, 1)
                            dve.wait_ge(max_step.sem, max_step.at(6 * it + n))
                        dve.wait_ge(rowmax.sem, rowmax.at(64 * it + 64))
                        link(dve.tensor_reduce(nm[:, :, :], mx[:, :, :, :], AX_X, ALU.max))
                        link(dve.tensor_scalar(mp[:, :, 0, :], nm[:, :, :], -1.0, None, ALU.mult))
                        link(dve.scalar_tensor_tensor(mr[:, :, :], nm[:, :, :], -1.0, mp[:, :, 0, :], ALU.mult, ALU.subtract))
                        link(dve.tensor_copy(mp[:, :, 1, :], mr[:, :, :]))
                        link(dve.tensor_tensor(mr[:, :, :], mr[:, :, :], mp[:, :, 1, :], ALU.subtract))
                        link(dve.tensor_copy(mp[:, :, 2, :], mr[:, :, :]))

                    for s in range(SLOTS):
                        if up:
                            reduce(s)
                        for slot, what, j in fills(*kind):
                            if slot == s and what == "den":
                                invert(it - 1 if j == 0 else it - 2, j)
                            if slot == s and what == "inv":
                                normalise(it - 1 if j == 0 else it - 2, j)
                    if up:
                        maximum_parts()

                def iterate(eng, one):
                    one(eng, 0, FIRST)
                    one(eng, 1, SECOND)
                    with eng.Fori(2, G) as it:
                        one(eng, it, FULL)
                    one(eng, G, LAST)
                    one(eng, G + 1, AFTER)

                with nc.Block() as block:
                    @block.tensor
                    def _(pe):
                        fill_stacks(pe, 0, 0, "q").then_inc(t_filled.sem, 1)
                        pe.wait_ge(t_taken.sem, t_taken.at(1))
                        fill_stacks(pe, 0, 0, "k").then_inc(t_filled.sem, 1)
                        iterate(pe, pe_iteration)

                    @block.scalar
                    def _(act):
                        act.preload_act_table(ACT.Exp)
                        for n, (into, rows) in enumerate(((qs, KD), (ks, KA))):
                            act.wait_ge(t_filled.sem, t_filled.at(n + 1))
                            act.activation(into[0:rows, 0, :], t_bf[0:rows, :], ACT.Copy).then_inc(t_taken.sem, 1)
                        iterate(act, act_iteration)

                    @block.vector
                    def _(dve):
                        iterate(dve, dve_iteration)

                    @block.gpsimd
                    def _(pool):
                        with pool.Fori(0, G) as g:
                            for kt in range(TB):
                                pool.wait_ge(weighed.sem, weighed.at(16 * g - KT_N + kt + 1))
                                pool.tensor_copy(vg[:, kt, :, :], val[:, kt, bass.ds(4 * g, 4), :]).then_inc(v_staged.sem, 1)

                    @block.sync
                    def _(sp):
                        def rows_of(g, after):
                            sp.wait_ge(t_taken.sem, t_taken.at(after))
                            for j in range(4):
                                sp.dma_start(qs[KD:KA, (4 * g + j) % RING, :], mpT[3 * TB * j:3 * TB * (j + 1), :]
                                             ).then_inc(max_rows_in.sem, 16)
                        rows_of(0, filled_before(1, SECOND) + 1)
                        with sp.Fori(1, G) as g:
                            rows_of(g, filled_before(g + 1, FULL) + 1)
                t_filled.passed(TOTAL)
                t_taken.passed(TOTAL)
                rowscores.passed(64 * G)
                rowmax.passed(64 * G)
                colscores.passed(32 * G)
                probs.passed(32 * G)
                weighed.passed(16 * G)
                o_copied.passed(2 * G)
                o_normed.passed(2 * G)
                inv_ready.passed(2 * G)
                max_step.passed(6 * G)
                v_staged.passed(TB * G)
                max_rows_in.passed(64 * G)

        def project_phase(l, b, mem, oT):
            with ExitStack() as ctx:
                wp = mem.wp
                y = sb(f"y{l}{b}", [P, 2, C], ctx=ctx)
                ps = [bank(f"pp{l}{b}{k}", ctx) for k in range(2)]
                again = b + 1 < B
                with nc.Block() as block:
                    @block.sync
                    def _(sp):
                        if again:
                            mem.load_qkv(sp)

                    @block.tensor
                    def _(pe):
                        pe.wait_ge(proj_loaded.sem, proj_loaded.at(16 * 17))
                        for t in range(TB):
                            if t > 1:
                                pe.wait_ge(gated.sem, gated.at(t - 1))
                            for g in range(G):
                                mm = pe.matmul(ps[t % 2][:, 0:C], oT[:, g, t * P:t * P + P], wp[:, g, :],
                                               start=g == 0, stop=g == G - 1)
                            mm.then_inc(mm_done.sem, 1)

                    @block.vector
                    def _(dve):
                        for t in range(TB):
                            tile = TB * b + t
                            dve.wait_ge(mm_done.sem, mm_done.at(t + 1))
                            dve.tensor_tensor(y[:, t % 2, :], ps[t % 2][:, 0:C], gate_b[:, l, 0, b, :], ALU.mult
                                              ).then_inc(gated.sem, 1)
                            dve.wait_ge(gated.sem, gated.at(t + 1))
                            dve.tensor_tensor(x[:, tile, :], x[:, tile, :], y[:, t % 2, :], ALU.add).then_inc(added.sem, 1)
                            dve.wait_ge(added.sem, added.at(t + 1))
                            dve.bn_stats(stats[:, tile, :], x[:, tile, :])
                if not again:
                    proj_loaded.passed(16 * 17)
                for s in (mm_done, gated, added):
                    s.passed(TB)

        def mlp_phases(l, experts):
            CH = 256
            NCH = NT * P // CH
            with ExitStack() as ctx:
                hh = sb(f"hh{l}", [P, 2, NT * P], F32R, ctx=ctx)
                hl = sb(f"hl{l}", [P, 2, NT * P], F32R, ctx=ctx)
                h3 = sb(f"h3{l}", [RA, NT * P], F32R, ctx=ctx)
                w1r = sb(f"w1r{l}", [P, 3, FF], ctx=ctx)
                w2r = sb(f"w2r{l}", [P, NF + 1, C], ctx=ctx)

                w1h = sb(f"w1h{l}", [P, 2, FF], F32R, ctx=ctx)
                w1l = sb(f"w1l{l}", [P, 2, FF], F32R, ctx=ctx)
                w13 = sb(f"w13{l}", [RA, FF], F32R, ctx=ctx)
                w2h = sb(f"w2h{l}", [P, NF + 1, C], F32R, ctx=ctx)
                w2l = sb(f"w2l{l}", [P, NF, C], F32R, ctx=ctx)
                ones2 = sb(f"ones2{l}", [P, P], F32R, ctx=ctx)
                load_w1, split_w1, w1_passed = split_weights(
                    FF, w1h, w1l, w13, w1r, sb(f"w1_tail{l}", [RA, FF], ctx=ctx), True, w_loaded, w_step)

                def load_up(sp, ex):
                    load_w1(sp, w["fc1_w"][l][ex], w["fc1_b"][l][ex])

                def load_down(sp, ex):
                    sp.dma_start(w2r[:, 0:NF, :], w["fc2_w"][l][ex].rearrange("(k p) c -> p k c", p=P)
                                 ).then_inc(w2_loaded.sem, 16)
                    for r in range(2):
                        sp.dma_start(w2r[r:r + 1, NF, :], w["fc2_b"][l][ex]).then_inc(w2_loaded.sem, 16)
                with ExitStack() as ctx2:
                    xn = sb(f"xm{l}", [P, 2, XN], ctx=ctx2)
                    m = sb(f"mm{l}", [P, 2, 3, P], ctx=ctx2)
                    turn_ps = [bank(f"tm{l}{k}", ctx2) for k in range(2)]

                    def cols(t):
                        return bass.ds(t * P, P)
                    normalise, turn, modulate, split = norm_stages(
                        ctx2, l, 2, xn, m, turn_ps, lambda t, k: hh[:, :, cols(t)], lambda t, k: hl[:, :, cols(t)],
                        lambda t, k: h3[:, cols(t)], False)
                    with nc.Block() as block:
                        @block.gpsimd
                        def _(pool):
                            pool.memset(xn[:, :, 2 * P + RS:XN], 1.0).then_inc(pool_done.sem, 1)
                            pool.memset(w2r[:, NF, :], 0.0).then_inc(pool_done.sem, 1)

                        @block.sync
                        def _(sp):
                            load_up(sp, 0)
                            sp.wait_ge(pool_done.sem, pool_done.at(2))
                            load_down(sp, 0)

                        @block.tensor
                        def _(pe):
                            pe.wait_ge(pool_done.sem, pool_done.at(2))
                            with pe.Fori(0, NT // 2) as i:
                                for k in range(2):
                                    turn(pe, 2 * i + k, k)

                        @block.scalar
                        def _(act):
                            deviations(None, act, (0, NT))
                            for b in range(B):
                                with act.Fori(0, TB // 2) as i:
                                    for k in range(2):
                                        modulate(act, 2 * i + (k + TB * b), b, k)

                        @block.vector
                        def _(dve):
                            deviations(dve, None, (0, NT))
                            normalise(dve, 0, 0, 0)
                            normalise(dve, 1, 1, 1)
                            with dve.Fori(0, NT // 2 - 1) as i:
                                for k in range(2):
                                    normalise(dve, 2 * i + k + 2, 2 * i + k + 2, k)
                                    split(dve, 2 * i + k, k)
                            split(dve, NT - 2, 0)
                            split(dve, NT - 1, 1)
                    pool_done.passed(2)
                    stats_in.passed(NT)
                    std_ready.passed(1)
                    rstd_ready.passed(1)
                    for s in (normed, turned, modulated, hi_ready, split_done):
                        s.passed(NT)
                if experts > 1:
                    gate_phase(hh, hl, h3)
                for ex in range(experts):
                    with ExitStack() as ctx2:
                        PAIRS = (NF + 1) // 2
                        g = sb(f"g{l}{ex}", [P, 2, 2, CH], ctx=ctx2)
                        gh = sb(f"gh{l}{ex}", [P, 2, NF, CH], F32R, ctx=ctx2)
                        gl = sb(f"gl{l}{ex}", [P, 2, NF, CH], F32R, ctx=ctx2)
                        y = sb(f"ym{l}{ex}", [P, 2, C], ctx=ctx2)
                        up_ps = [bank(f"up{l}{ex}{i}", ctx2) for i in range(PAIRS)]
                        dn_ps = [bank(f"dn{l}{ex}{i}", ctx2) for i in range(2)]
                        size = [min(2, NF - 2 * q) for q in range(PAIRS)]

                        def up(pe, c, k):
                            for q in range(PAIRS):
                                n = PAIRS * c + q
                                pe.wait_ge(gelu_done.sem, gelu_done.at(n - PAIRS + 1))
                                pbank = up_ps[q]
                                for i in range(size[q]):
                                    f = 2 * q + i
                                    cols = slice(f * P, f * P + P)
                                    mm = split_products(
                                        pe, pbank[:, i * CH:i * CH + CH],
                                        (lambda s: w1h[:, s, cols], lambda s: w1l[:, s, cols], w13[0:RA, cols]),
                                        (lambda s: hh[:, s, bass.ds(c * CH, CH)], lambda s: hl[:, s, bass.ds(c * CH, CH)],
                                         h3[0:RA, bass.ds(c * CH, CH)]))
                                mm.then_inc(up_ready.sem, 1)

                        def gelu(act, c, k):
                            for q in range(PAIRS):
                                n = PAIRS * c + q
                                act.wait_ge(up_ready.sem, up_ready.at(n + 1))
                                act.wait_ge(g_split.sem, g_split.at(n - 1 if q else n))
                                act.activation(g[:, q % 2, 0:size[q], :].rearrange("p i c -> p (i c)"),
                                               up_ps[q][:, 0:size[q] * CH], ACT.Gelu_apprx_tanh).then_inc(gelu_done.sem, 1)

                        def split_g(dve, c, k):
                            dve.wait_ge(mm_done.sem, mm_done.at(2 * (c - 1)))
                            for q in range(PAIRS):
                                n = PAIRS * c + q
                                dve.wait_ge(gelu_done.sem, gelu_done.at(n + 1))
                                fs = slice(2 * q, 2 * q + size[q])
                                dve.tensor_copy(gh[:, k, fs, :], g[:, q % 2, 0:size[q], :]).then_inc(g_hi.sem, 1)
                                dve.wait_ge(g_hi.sem, g_hi.at(n + 1))
                                dve.tensor_tensor(gl[:, k, fs, :], g[:, q % 2, 0:size[q], :], gh[:, k, fs, :].bitcast(F32),
                                                  ALU.subtract).then_inc(g_split.sem, 1)

                        def down(pe, c, k):
                            pe.wait_ge(g_split.sem, g_split.at(PAIRS * (c + 1)))
                            for i in range(2):
                                n = 2 * c + i
                                pe.wait_ge(gated.sem, gated.at(n - 1))
                                o = dn_ps[i][:, 0:C]
                                tok = slice(i * P, i * P + P)
                                for f in range(NF):
                                    pe.matmul(o, gh[:, k, f, tok], w2h[:, f, :], start=f == 0, stop=False)
                                    pe.matmul(o, gh[:, k, f, tok], w2l[:, f, :], start=False, stop=False)
                                    pe.matmul(o, gl[:, k, f, tok], w2h[:, f, :], start=False, stop=False)
                                pe.matmul(o, ones2[:, :], w2h[:, NF, :], start=False, stop=True).then_inc(mm_done.sem, 1)

                        def residual(dve, c, b, k):
                            for i in range(2):
                                n = 2 * c + i
                                dve.wait_ge(mm_done.sem, mm_done.at(n + 1))
                                dve.scalar_tensor_tensor(y[:, i, :], dn_ps[i][:, 0:C], cw[:, n, ex:ex + 1],
                                                         gate_b[:, l, 1, b, :], ALU.mult, ALU.mult).then_inc(gated.sem, 1)
                                dve.wait_ge(gated.sem, gated.at(n + 1))
                                dve.tensor_tensor(x[:, n, :], x[:, n, :], y[:, i, :], ALU.add).then_inc(added.sem, 1)
                                if ex == experts - 1:
                                    dve.wait_ge(added.sem, added.at(n + 1))
                                    dve.bn_stats(stats[:, n, :], x[:, n, :])

                        def split_w2(dve):
                            step = Chain(dve, w2_step)
                            dve.wait_ge(w2_loaded.sem, w2_loaded.at(48))
                            step(dve.tensor_copy(ones2[:, :], mix[:, 2:3].broadcast_to([P, P])))
                            step(dve.tensor_copy(w2h[:, :, :], w2r[:, :, :]))
                            step(dve.tensor_tensor(w2l[:, :, :], w2r[:, 0:NF, :], w2h[:, 0:NF, :].bitcast(F32), ALU.subtract))
                            step(dve.tensor_tensor(w2r[:, NF, :], w2r[:, NF, :], w2h[:, NF, :].bitcast(F32), ALU.subtract))
                            step(dve.tensor_scalar(w2r[:, NF, :], w2r[:, NF, :], mix[:, 3:4], None, ALU.mult))
                            step(dve.scalar_tensor_tensor(w2h[:, NF, :], w2h[:, NF, :].bitcast(F32), ident[:, 0:1],
                                                          w2r[:, NF, :], ALU.mult, ALU.add))

                        with nc.Block() as block:
                            @block.sync
                            def _(sp):
                                if ex + 1 < experts:
                                    sp.wait_ge(w_step.sem, w_step.at(SPLIT_STEPS))
                                    sp.wait_ge(w2_step.sem, w2_step.at(6))
                                    load_up(sp, ex + 1)
                                    load_down(sp, ex + 1)

                            @block.tensor
                            def _(pe):
                                pe.wait_ge(w_step.sem, w_step.at(SPLIT_STEPS))
                                up(pe, 0, 0)
                                with pe.Fori(0, NCH // 2 - 1) as i:
                                    for k in range(2):
                                        up(pe, 2 * i + k + 1, 1 - k)
                                        down(pe, 2 * i + k, k)
                                up(pe, NCH - 1, 1)
                                down(pe, NCH - 2, 0)
                                down(pe, NCH - 1, 1)

                            @block.scalar
                            def _(act):
                                act.preload_act_table(ACT.Gelu_apprx_tanh)
                                with act.Fori(0, NCH) as c:
                                    gelu(act, c, 0)

                            @block.vector
                            def _(dve):
                                split_w1(dve)
                                split_w2(dve)
                                split_g(dve, 0, 0)
                                with dve.Fori(0, NCH // 2 - 1) as i:
                                    for k in range(2):
                                        split_g(dve, 2 * i + k + 1, 1 - k)
                                        residual(dve, 2 * i + k, i // (NCH // 2 // B), k)
                                split_g(dve, NCH - 1, 1)
                                residual(dve, NCH - 2, B - 1, 0)
                                residual(dve, NCH - 1, B - 1, 1)
                    w1_passed()
                    w2_loaded.passed(48)
                    w2_step.passed(6)
                    for s in (up_ready, gelu_done, g_hi, g_split):
                        s.passed(PAIRS * NCH)
                    for s in (mm_done, gated, added):
                        s.passed(NT)

        def gate_phase(hh, hl, h3):
            with ExitStack() as ctx:
                raw = sb("wg_raw", [P, 3, P], ctx=ctx)
                gh = sb("wg_h", [P, 2, P], F32R, ctx=ctx)
                gl = sb("wg_l", [P, 2, P], F32R, ctx=ctx)
                g3 = sb("wg_3", [RA, P], F32R, ctx=ctx)
                lT = sb("lT", [EXPERTS, NT * P], ctx=ctx)
                lg = sb("lg", [P, NT, EXPERTS], ctx=ctx)
                top1 = sb("top1", [P, NT], ctx=ctx)
                ex = sb("ex", [P, NT, EXPERTS], ctx=ctx)
                rank = sb("rank", [P, NT, EXPERTS], ctx=ctx)
                cmp = sb("cmp", [P, NT, EXPERTS], ctx=ctx)
                ps = [bank(f"lg_ps{i}", ctx) for i in range(4)]
                col = bank("lg_col", ctx)
                load_gate, split_gate, gate_passed = split_weights(
                    P, gh, gl, g3, raw, sb("wg_tail", [RA, P], ctx=ctx), False, loaded, gate_step,
                    cols=EXPERTS)
                with nc.Block() as block:
                    @block.gpsimd
                    def _(pool):
                        pool.memset(raw[:, :, :], 0.0).then_inc(pool_done.sem, 1)

                    @block.sync
                    def _(sp):
                        sp.wait_ge(pool_done.sem, pool_done.at(1))
                        load_gate(sp, w["gate_w"], None)

                    @block.vector
                    def _(dve):
                        split_gate(dve)
                gate_passed()
                pool_done.passed(1)
                with nc.Block() as block:
                    @block.tensor
                    def _(pe):
                        for c in range(4):
                            cols = slice(c * 512, c * 512 + 512)
                            split_products(pe, ps[c][:, :],
                                           (lambda s: gh[:, s, :], lambda s: gl[:, s, :], g3[0:RA, :]),
                                           (lambda s: hh[:, s, cols], lambda s: hl[:, s, cols], h3[0:RA, cols])
                                           ).then_inc(pe_done.sem, 1)
                        for c in range(4):
                            pe.wait_ge(act_done.sem, act_done.at(c + 1))
                            for t in range(4 * c, 4 * c + 4):
                                mm = pe.transpose(col[:, 4 * t:4 * t + 4], lT[:, t * P:t * P + P], ident[0:4, 0:4])
                        mm.then_inc(pe_done.sem, 1)

                    @block.scalar
                    def _(act):
                        for c in range(4):
                            act.wait_ge(pe_done.sem, pe_done.at(c + 1))
                            act.activation(lT[:, c * 512:c * 512 + 512], ps[c][0:EXPERTS, :], ACT.Copy).then_inc(act_done.sem, 1)
                        act.wait_ge(dve_done.sem, dve_done.at(3))
                        act.activation(ex[:, :, :], cmp[:, :, :], ACT.Exp).then_inc(act_done.sem, 1)

                    @block.vector
                    def _(dve):
                        step = Chain(dve, dve_done)
                        dve.wait_ge(pe_done.sem, pe_done.at(5))
                        step(dve.tensor_copy(lg[:, :, :].rearrange("p t e -> p (t e)"), col[:, 0:NT * EXPERTS]))
                        step(dve.tensor_reduce(top1[:, :], lg[:, :, :], AX_X, ALU.max))
                        step(dve.tensor_tensor(cmp[:, :, :], lg[:, :, :],
                                               top1[:, :].unsqueeze(2).broadcast_to([P, NT, EXPERTS]), ALU.subtract))
                        step(dve.memset(rank[:, :, :], 0.0))
                        dve.wait_ge(act_done.sem, act_done.at(5))
                        for f in range(EXPERTS):
                            step(dve.tensor_tensor(cmp[:, :, :], lg[:, :, f:f + 1].broadcast_to([P, NT, EXPERTS]),
                                                   lg[:, :, :], ALU.is_gt))
                            step(dve.tensor_tensor(rank[:, :, :], rank[:, :, :], cmp[:, :, :], ALU.add))
                            if f < EXPERTS - 1:
                                n = EXPERTS - 1 - f
                                step(dve.tensor_tensor(cmp[:, :, f + 1:], lg[:, :, f:f + 1].broadcast_to([P, NT, n]),
                                                       lg[:, :, f + 1:], ALU.is_equal))
                                step(dve.tensor_tensor(rank[:, :, f + 1:], rank[:, :, f + 1:], cmp[:, :, f + 1:], ALU.add))
                        step(dve.scalar_tensor_tensor(ex[:, :, :], rank[:, :, :], 2.0, ex[:, :, :], ALU.is_lt, ALU.mult))
                        step(dve.tensor_reduce(top1[:, :], ex[:, :, :], AX_X, ALU.add))
                        step(dve.reciprocal(top1[:, :], top1[:, :]))
                        step(dve.tensor_tensor(cw[:, :, :], ex[:, :, :],
                                               top1[:, :].unsqueeze(2).broadcast_to([P, NT, EXPERTS]), ALU.mult))
                pe_done.passed(5)
                act_done.passed(5)
                dve_done.passed(4 + 4 * 2 + 3 * 2 + 4)

        def rotate_phase(mem):
            with ExitStack() as ctx:
                xT = sb("xT", [P, 2, 3, P], ctx=ctx)
                turn_ps = [bank(f"rt{k}", ctx) for k in range(2)]
                ps = [bank(f"rp{k}", ctx) for k in range(2)]
                KROWS = (P, P, R)

                def turn(pe, t, k):
                    pe.wait_ge(modulated.sem, modulated.at(t - 1))
                    for s in range(3):
                        mm = pe.transpose(turn_ps[k][0:KROWS[s], s * P:s * P + P], x[:, t, s * P:s * P + KROWS[s]], ident[:, :])
                    mm.then_inc(turned.sem, 1)

                with nc.Block() as block:
                    @block.sync
                    def _(sp):
                        mem.load_qkv(sp)

                    @block.tensor
                    def _(pe):
                        turn(pe, 0, 0)
                        for t in range(NT):
                            if t + 1 < NT:
                                turn(pe, t + 1, (t + 1) % 2)
                            pe.wait_ge(modulated.sem, modulated.at(t + 1))
                            pe.wait_ge(added.sem, added.at(t - 1))
                            for s in range(3):
                                K = KROWS[s]
                                mm = pe.matmul(ps[t % 2][:, 0:C], xT[0:K, t % 2, s, :], m_rot[0:K, t // TB, s, :],
                                               start=s == 0, stop=s == 2)
                            mm.then_inc(mm_done.sem, 1)

                    @block.scalar
                    def _(act):
                        for t in range(NT):
                            act.wait_ge(turned.sem, turned.at(t + 1))
                            act.wait_ge(mm_done.sem, mm_done.at(t - 1))
                            act.activation(xT[:, t % 2, 0:2, :].rearrange("p s c -> p (s c)"), turn_ps[t % 2][:, 0:2 * P], ACT.Copy)
                            act.activation(xT[0:R, t % 2, 2, :], turn_ps[t % 2][0:R, 2 * P:3 * P], ACT.Copy
                                           ).then_inc(modulated.sem, 1)

                    @block.vector
                    def _(dve):
                        for t in range(NT):
                            dve.wait_ge(mm_done.sem, mm_done.at(t + 1))
                            dve.tensor_tensor(x[:, t, :], x[:, t, :], ps[t % 2][:, 0:C], ALU.add).then_inc(added.sem, 1)
                            dve.wait_ge(added.sem, added.at(t + 1))
                            dve.bn_stats(stats[:, t, :], x[:, t, :])
                for s in (turned, modulated, mm_done, added):
                    s.passed(NT)

        stage = 0
        for l in range(3):
            with ExitStack() as layer:
                mem = LayerMemory(l, layer)
                if l == 0:
                    modulation(mem)
                    rotation()
                elif l == 1:
                    rotate_phase(mem)
                if upto == stage:
                    break
                stage += 1
                for b in range(B):
                    with ExitStack() as ctx:
                        oT = sb(f"oT{l}{b}", [P, G, L], ctx=ctx)
                        with ExitStack() as ctx2:
                            stack = sb(f"stack{l}{b}", [P, TB, 2, H, SW], BF16, ctx=ctx2)
                            val = sb(f"val{l}{b}", [P, TB, H, 32], ctx=ctx2)
                            qkv_phase(l, b, mem, stack, val)
                            attention_phase(l, b, mem, stack, val, oT)
                        project_phase(l, b, mem, oT)
            if upto == stage:
                break
            stage += 1
            mlp_phases(l, EXPERTS if l == 1 else 1)
            if l == 1:
                with nc.Block() as block:
                    @block.gpsimd
                    def _(pool):
                        pool.memset(cw[:, :, :], 1.0)
            if upto == stage:
                break
            stage += 1
        with nc.Block() as block:
            @block.sync
            def _(sp):
                sp.dma_start(out.rearrange("b (t p) c -> p (b t) c", p=P), x[:, :, :]).then_inc(stored.sem, 16)
                sp.wait_ge(stored.sem, stored.at(16))


def constants():
    import numpy as np
    f = np.float32
    eye = np.eye(P, dtype=f)
    mix = np.zeros((P, 4), f)
    mix[0:2 * R, 0] = 1
    mix[RS, 0] = 1
    mix[0:RA, 1] = 1 - mix[0:RA, 0]
    mix[0:2, 2] = 1
    mix[1, 3] = 1
    sel = np.zeros((P, 4), f)
    for j in range(4):
        sel[32 * j + D, j] = 1
    rows = (np.arange(C)[:, None] >= np.arange(RK)[None, :]).astype(f)
    tri = np.stack([np.triu(np.ones((RK, RK), f), 1), np.eye(RK, dtype=f)], 1)
    i = np.arange(SQUARINGS)
    k = 1.0 / np.maximum(TAYLOR - 1 - i, 1)
    pw = np.broadcast_to(np.stack([2.0 ** i, 2.0 ** -(i + 1) - 1, k])[None], (RK, 3, SQUARINGS)).astype(f)
    return {"const_ident": eye, "const_mix": mix, "const_sel": sel, "const_rows": rows, "const_tri": tri, "const_pow": pw}


def laid_out(inputs):
    import numpy as np
    a = {k: np.ascontiguousarray(v) for k, v in inputs.items()}
    r = {
        "x": a["x"], "condT": np.ascontiguousarray(a["cond_1152"].T),
        "rot_P": a["L1_cond_P"], "rot_PT": np.ascontiguousarray(a["L1_cond_P"].T),
        "g_q": a["L3_cond_g_q"], "g_k": a["L3_cond_g_k"], "gate_w": a["L2_cond_w_gate"],
    }
    iu, ju = np.triu_indices(RK, k=1)
    grid = np.zeros((C, RK, RK), a["L1_cond_W"].dtype)
    grid[:, iu, ju] = a["L1_cond_W"].T
    r["rot_W"] = grid.reshape(C, RK * RK)
    grid = np.zeros((RK, RK), a["L1_cond_b"].dtype)
    grid[iu, ju] = a["L1_cond_b"]
    r["rot_b"] = grid.reshape(1, RK * RK)
    names = [("L0_cond_W_qkv", "L0_cond_b_qkv", "L0_cond_W_proj", "L0_cond_b_proj", "L0_cond_W_ada", "L0_cond_b_ada",
              "L0_cond_W_fc1", "L0_cond_b_fc1", "L0_cond_W_fc2", "L0_cond_b_fc2"),
             ("L2_cond_w_qkv", "L2_cond_b_qkv", "L2_cond_w_proj", "L2_cond_b_proj", "L2_cond_w_adaln", "L2_cond_b_adaln",
              "L2_cond_w1", "L2_cond_b1", "L2_cond_w2", "L2_cond_b2"),
             ("L3_cond_w_qkv", "L3_cond_b_qkv", "L3_cond_w_proj", "L3_cond_b_proj", "L3_cond_w_mod", "L3_cond_b_mod",
              "L3_cond_w1", "L3_cond_b1", "L3_cond_w2", "L3_cond_b2")]
    kinds = ("qkv_w", "qkv_b", "proj_w", "proj_b", "ada_w", "ada_b", "fc1_w", "fc1_b", "fc2_w", "fc2_b")
    for l, row in enumerate(names):
        for kind, name in zip(kinds, row):
            r[f"{kind}{l}"] = a[name]
    return r


def declare(nc, arrays):
    import numpy as np
    ap = {}
    for name, v in arrays.items():
        ap[name] = nc.dram_tensor(f"in_{name}", v.shape, mybir.dt.from_np(v.dtype), kind="ExternalInput").ap()
    out = nc.dram_tensor("out", (B, L, C), F32, kind="ExternalOutput").ap()
    w = {k: v for k, v in ap.items()}

    def row(v):
        return v.rearrange("(o c) -> o c", o=1)
    w["qkv_w"] = [ap[f"qkv_w{l}"] for l in range(3)]
    w["qkv_b"] = [row(ap[f"qkv_b{l}"]) for l in range(3)]
    w["proj_w"] = [ap[f"proj_w{l}"] for l in range(3)]
    w["proj_b"] = [row(ap[f"proj_b{l}"]) for l in range(3)]
    w["ada_w"] = [ap[f"ada_w{l}"] for l in range(3)]
    w["ada_b"] = [ap[f"ada_b{l}"] for l in range(3)]
    for kind in ("fc1_w", "fc2_w"):
        w[kind] = [[ap[f"{kind}{l}"][e] for e in range(EXPERTS)] if l == 1 else [ap[f"{kind}{l}"]] for l in range(3)]
    for kind in ("fc1_b", "fc2_b"):
        w[kind] = [[ap[f"{kind}{l}"][e:e + 1, :] for e in range(EXPERTS)] if l == 1 else [row(ap[f"{kind}{l}"])]
                   for l in range(3)]
    return ap["x"], out, w


def kernel(**inputs):
    import concourse.bacc as bacc
    from concourse.bass_utils import run_bass_kernel_spmd

    nc = bacc.Bacc("TRN2", target_bir_lowering=False, num_devices=1)
    arrays = {**laid_out(inputs), **constants()}
    x_in, out, w = declare(nc, arrays)
    build(nc, x_in, out, w)
    r = run_bass_kernel_spmd(nc, [{f"in_{k}": v for k, v in arrays.items()}], core_ids=[0])
    return r.results[0]["out"]
```

```python
from contextlib import ExitStack

import concourse.bass as bass
from concourse import mybir

F32 = mybir.dt.float32
F32R = mybir.dt.float32r
BF16 = mybir.dt.bfloat16
ALU = mybir.AluOpType
ACT = mybir.ActivationFunctionType
AX_X = mybir.AxisListType.X

P = 128
B, L, C = 2, 1024, 288
H = 16
D = C // H
TB = L // P
NT = B * TB
R = C - 2 * P
RS = 3 * R
RA = RS + 2
SLAB = (P, P, RS)
XN = 2 * P + RA
FF = 4 * C
NF = FF // P
EXPERTS = 4
RK = 64
QR_P, QR_T = 96, 3
PARTS = 6
KD = PARTS * D
KA = KD + 3
SW = 112
G = H // 4
SCALE = float(D) ** -0.5
EPS = 1e-6
CREDIT = 64
SPLIT_STEPS = 5
RING = 10
QR_UNROLL = 4
SQUARINGS = 20
TAYLOR = 12


class Signal:

    def __init__(self, sem):
        self.sem = sem
        self.base = CREDIT

    def at(self, n):
        return self.base + n

    def passed(self, n):
        self.base += n


class Chain:

    def __init__(self, eng, counted):
        self.eng, self.counted, self.n = eng, counted, 0

    def __call__(self, ins):
        self.n += 1
        ins.then_inc(self.counted.sem, 1)
        self.eng.wait_ge(self.counted.sem, self.counted.at(self.n))
        return self.n


def build(nc, x_in, out, w):
    top = ExitStack()
    with top:
        used = {}

        def fresh(name):
            used[name] = used.get(name, 0) + 1
            return name if used[name] == 1 else f"{name}_{used[name]}"

        def sb(name, shape, dt=F32, ctx=top):
            name = fresh(name)
            return ctx.enter_context(nc.sbuf_tensor(name, shape, dt))

        def bank(name, ctx, shape=(P, 512), dt=F32):
            return ctx.enter_context(nc.psum_tensor(fresh(name), list(shape), dt))

        signals = []

        def signal(name):
            s = Signal(top.enter_context(nc.semaphore(name)))
            signals.append(s)
            return s

        loaded = signal("loaded")
        w_loaded = signal("w_loaded")
        biases_in = signal("biases_in")
        x_loaded = signal("x_loaded")
        ada_in = [signal(f"ada_in{l}") for l in range(3)]
        grid_in = signal("grid_in")
        gate_step = signal("gate_step")
        w2_loaded = signal("w2_loaded")
        w2_step = signal("w2_step")
        proj_loaded = signal("proj_loaded")
        wp_cleared = signal("wp_cleared")
        stored = signal("stored")
        max_rows_in = signal("max_rows_in")
        dve_done = signal("dve_done")
        act_done = signal("act_done")
        pe_done = signal("pe_done")
        pool_done = signal("pool_done")
        stats_in = signal("stats_in")
        std_ready = signal("std_ready")
        rstd_ready = signal("rstd_ready")
        normed = signal("normed")
        turned = signal("turned")
        modulated = signal("modulated")
        hi_ready = signal("hi_ready")
        split_done = signal("split_done")
        qkv_ready = signal("qkv_ready")
        qkv_taken = signal("qkv_taken")
        qk_step = signal("qk_step")
        qk_std = signal("qk_std")
        qk_split = signal("qk_split")
        t_filled = signal("t_filled")
        t_taken = signal("t_taken")
        rowscores = signal("rowscores")
        rowmax = signal("rowmax")
        colscores = signal("colscores")
        probs = signal("probs")
        weighed = signal("weighed")
        o_copied = signal("o_copied")
        inv_ready = signal("inv_ready")
        max_step = signal("max_step")
        v_staged = signal("v_staged")
        mm_done = signal("mm_done")
        gated = signal("gated")
        added = signal("added")
        up_ready = signal("up_ready")
        gelu_done = signal("gelu_done")
        g_hi = signal("g_hi")
        g_split = signal("g_split")
        w_step = signal("w_step")
        qr_col = signal("qr_col")
        qr_row = signal("qr_row")
        qr_dots = signal("qr_dots")
        qr_copy = signal("qr_copy")
        qr_step = signal("qr_step")

        x = sb("x", [P, NT, C])
        stats = sb("stats", [P, NT, 6])
        mv = sb("mv", [P, NT, 2])
        std = sb("std", [P, NT])
        rstd = sb("rstd", [P, NT])
        modc = sb("modc", [P, 3, 4, 3, B])
        gate_b = sb("gate_b", [P, 3, 2, B, C])
        ident = sb("ident", [P, P])
        identb = sb("identb", [P, P], BF16)
        m_rot = sb("m_rot", [P, B, 3, C])
        cw = sb("cw", [P, NT, EXPERTS])
        eps_col = sb("eps_col", [P, 1])
        s_thirds = sb("s_thirds", [QR_P, QR_T, B])
        mix = sb("mix", [P, 4])
        sel_den = sb("sel_den", [P, 4])

        with nc.Block() as block:
            @block.gpsimd
            def _(pool):
                for s in signals:
                    pool.nop().then_inc(s.sem, CREDIT)
                pool.memset(eps_col[:, :], EPS)

        def modulation(mem):
            with ExitStack() as ctx:
                wa = sb("wa", [P, 3, 3, 6 * C], ctx=ctx)
                condT = sb("condT", [P, 3, B], ctx=ctx)
                sT = sb("sT", [P, 3, B], ctx=ctx)
                sTb = sb("sTb", [P, 3, B, P], ctx=ctx)
                bias_c = sb("bias_c", [P, 3, 4, 3], ctx=ctx)
                bias_g = sb("bias_g", [P, 3, 2, C], ctx=ctx)
                col_ps = bank("col_ps", ctx, (P, 3, 4, 3, 8))
                gate_ps = bank("gate_ps", ctx, (P, 4, 512))
                KROWS = (P, P, R)
                BIASES = 3 * (2 + 4 * 5)
                with nc.Block() as block:
                    @block.sync
                    def _(sp):
                        def load(dst, src):
                            sp.dma_start(dst, src).then_inc(biases_in.sem, 16)

                        for s in range(3):
                            sp.dma_start(condT[0:KROWS[s], s, :], w["condT"][s * P:s * P + KROWS[s], :]
                                         ).then_inc(loaded.sem, 16)
                        for dst, src in ((s_thirds[:, :, :], w["condT"].rearrange("(t p) b -> p t b", p=QR_P)),
                                         (ident[:, :], w["const_ident"]), (mix[:, :], w["const_mix"]),
                                         (sel_den[:, :], w["const_sel"])):
                            sp.dma_start(dst, src).then_inc(loaded.sem, 16)
                        for l in range(3):
                            wd, bd = w["ada_w"][l], w["ada_b"][l]
                            for s in range(3):
                                sp.dma_start(wa[0:KROWS[s], l, s, :], wd[s * P:s * P + KROWS[s], :]
                                             ).then_inc(ada_in[l].sem, 16)
                        for l in range(3):
                            wd, bd = w["ada_w"][l], w["ada_b"][l]
                            for gi, six in enumerate((2, 5)):
                                load(bias_g[:, l, gi, :],
                                     bd[six * C:six * C + C].rearrange("(o c) -> o c", o=1).broadcast_to([P, C]))
                            for ki, six in enumerate((0, 1, 3, 4)):
                                for s in range(2):
                                    load(bias_c[:, l, ki, s:s + 1],
                                         bd[six * C + s * P:six * C + s * P + P].rearrange("(c o) -> c o", o=1))
                                for r in range(3):
                                    load(bias_c[R * r:R * r + R, l, ki, 2:3],
                                         bd[six * C + 2 * P:six * C + C].rearrange("(c o) -> c o", o=1))

                        sp.dma_start(x[:, :, :], x_in.rearrange("b (t p) c -> p (b t) c", p=P)).then_inc(x_loaded.sem, 16)
                        mem.load_qkv(sp)

                    @block.scalar
                    def _(act):
                        act.wait_ge(loaded.sem, loaded.at(16 * 7))
                        for s in range(3):
                            act.activation(sT[0:KROWS[s], s, :], condT[0:KROWS[s], s, :], ACT.Silu).then_inc(
                                act_done.sem, 1)
                        act.activation(s_thirds[:, :, :], s_thirds[:, :, :], ACT.Silu)

                    @block.gpsimd
                    def _(pool):
                        pool.memset(modc[:, :, :, :, :], 0.0).then_inc(pool_done.sem, 1)
                        pool.wait_ge(pool_done.sem, pool_done.at(1))
                        for ki in (1, 3):
                            pool.memset(modc[:, :, ki, :, :], 1.0).then_inc(pool_done.sem, 1)
                        pool.memset(cw[:, :, :], 1.0).then_inc(pool_done.sem, 1)

                    @block.tensor
                    def _(pe):
                        pe.wait_ge(dve_done.sem, dve_done.at(3))
                        for l in range(3):
                            pe.wait_ge(ada_in[l].sem, ada_in[l].at(16 * 3))
                            for ki, six in enumerate((0, 1, 3, 4)):
                                for s in range(3):
                                    for r in range(3 if s == 2 else 1):
                                        n = R if s == 2 else P
                                        for kt in range(3):
                                            K = KROWS[kt]
                                            pe.matmul(col_ps[R * r:R * r + n, l, ki, s, 0:B],
                                                      wa[0:K, l, kt, six * C + s * P:six * C + s * P + n],
                                                      sT[0:K, kt, :], start=kt == 0, stop=kt == 2)
                            for gi, six in enumerate((2, 5)):
                                for b in range(B):
                                    n = 2 * gi + b
                                    if l > 0 and n == 0:
                                        pe.wait_ge(dve_done.sem, dve_done.at(4 + 4 * l))
                                    for kt in range(3):
                                        K = KROWS[kt]
                                        mm = pe.matmul(gate_ps[:, n, 0:C], sTb[0:K, kt, b, :],
                                                       wa[0:K, l, kt, six * C:six * C + C],
                                                       start=kt == 0, stop=kt == 2)
                            mm.then_inc(pe_done.sem, 1)

                    @block.vector
                    def _(dve):
                        dve.wait_ge(act_done.sem, act_done.at(3))
                        for s in range(3):
                            K = KROWS[s]
                            dve.tensor_copy(sTb[0:K, s, :, :],
                                            sT[0:K, s, :].unsqueeze(2).broadcast_to([K, B, P])).then_inc(dve_done.sem, 1)
                        dve.tensor_copy(identb[:, :], ident[:, :]).then_inc(dve_done.sem, 1)
                        dve.wait_ge(biases_in.sem, biases_in.at(16 * BIASES))
                        for l in range(3):
                            dve.wait_ge(pe_done.sem, pe_done.at(l + 1))
                            for gi in range(2):
                                for b in range(B):
                                    dve.tensor_tensor(gate_b[:, l, gi, b, :], gate_ps[:, 2 * gi + b, 0:C],
                                                      bias_g[:, l, gi, :], ALU.add).then_inc(dve_done.sem, 1)
                        dve.wait_ge(pool_done.sem, pool_done.at(4))
                        for l in range(3):
                            for ki in range(4):
                                for s in range(3):
                                    n = SLAB[s]
                                    dve.tensor_scalar(modc[0:n, l, ki, s, :], col_ps[0:n, l, ki, s, 0:B],
                                                      bias_c[0:n, l, ki, s:s + 1], float(ki % 2), ALU.add, ALU.add
                                                      ).then_inc(dve_done.sem, 1)
                        dve.wait_ge(x_loaded.sem, x_loaded.at(16))
                        for t in range(NT):
                            dve.bn_stats(stats[:, t, :], x[:, t, :]).then_inc(dve_done.sem, 1)
                loaded.passed(16 * 7)
                biases_in.passed(16 * BIASES)
                x_loaded.passed(16)
                for arrived in ada_in:
                    arrived.passed(16 * 3)
                act_done.passed(3)
                pool_done.passed(4)
                pe_done.passed(3)
                dve_done.passed(4 + 12 + 36 + NT)

        def rotation():
            with ExitStack() as ctx:
                z = sb("z", [QR_P, QR_T, RK], ctx=ctx)
                row_mask = sb("row_mask", [QR_P, QR_T, RK], ctx=ctx)
                v = sb("v", [QR_P, QR_T], ctx=ctx)
                e = sb("e", [QR_P, 1], ctx=ctx)
                ya = sb("ya", [QR_P, 2, RK], ctx=ctx)
                small = sb("small", [QR_P, 8], ctx=ctx)
                wr = sb("wr", [QR_P, 2, RK], ctx=ctx)
                dots = bank("dots", ctx)
                two = bank("two", ctx)
                wide = bank("wide", ctx)
                wide2 = bank("wide2", ctx)
                INV = 6
                KROWS = (P, P, R)
                tri = sb("tri", [RK, 2, RK], ctx=ctx)
                pT = sb("pT", [RK, C], ctx=ctx)
                uT = sb("uT", [RK, C], ctx=ctx)
                power = sb("power", [RK, 2, RK], ctx=ctx)
                prod = sb("prod", [RK, RK], ctx=ctx)
                tmp = sb("tmp", [RK, RK], ctx=ctx)
                s1 = sb("s1", [RK, 8], ctx=ctx)
                wv = sb("wv", [QR_P, QR_T, 8, 512], ctx=ctx)
                bias_v = sb("bias_v", [B, 8, 512], ctx=ctx)
                vrow = sb("vrow", [B, 8, 512], ctx=ctx)
                skew = sb("skew", [RK, B, 2, RK], ctx=ctx)
                up = sb("up", [RK, B, RK], ctx=ctx)
                term = sb("term", [RK, B, 2, RK], ctx=ctx)
                sq = sb("sq", [RK, B, 2, RK], ctx=ctx)
                kept = sb("kept", [RK, B, 2, RK], ctx=ctx)
                absA = sb("absA", [RK, B, RK], ctx=ctx)
                rs = sb("rs", [RK, B], ctx=ctx)
                big = sb("big", [B, 1], ctx=ctx)
                bigd = sb("bigd", [B, B], ctx=ctx)
                onesr = sb("onesr", [B, RK], ctx=ctx)
                nrm = sb("nrm", [RK, B], ctx=ctx)
                pw = sb("pw", [RK, 3, SQUARINGS], ctx=ctx)
                gt = sb("gt", [RK, B, SQUARINGS], ctx=ctx)
                ngt = sb("ngt", [RK, B, SQUARINGS], ctx=ctx)
                sf = sb("sf", [RK, B, SQUARINGS], ctx=ctx)
                sc = sb("sc", [RK, B], ctx=ctx)
                g_u = sb("g_u", [RK, B, C], ctx=ctx)
                NL = 3 + 3 + B
                AT_ENTRIES, AT_NORM, AT_TERMS, AT_SQUARES = 16, 28, 28, 40
                HORNER = TAYLOR - 1
                mark = {}
                eye4 = tri[:, 1, :].unsqueeze(1).broadcast_to([RK, 2 * B, RK])
                sk4 = skew[:, :, :, :].rearrange("p b s c -> p (b s) c")
                tm4 = term[:, :, :, :].rearrange("p b s c -> p (b s) c")
                sq4 = sq[:, :, :, :].rearrange("p b s c -> p (b s) c")
                two4 = two[0:RK, 0:2 * B * RK].rearrange("p (a c) -> p a c", a=2 * B)

                def repeat(eng, first, count, body):
                    loops = count // QR_UNROLL
                    if loops > 1:
                        with eng.Fori(0, loops) as i:
                            for u in range(QR_UNROLL):
                                body(QR_UNROLL * i + (first + u), QR_UNROLL * i + u, u)
                    done = loops * QR_UNROLL if loops > 1 else 0
                    for n in range(done, count):
                        body(first + n, n, n % QR_UNROLL)

                with nc.Block() as block:
                    @block.sync
                    def _(sp):
                        sp.dma_start(z[:, :, :], w["rot_P"].rearrange("(t p) d -> p t d", p=QR_P)).then_inc(loaded.sem, 16)
                        sp.dma_start(row_mask[:, :, :], w["const_rows"].rearrange("(t p) d -> p t d", p=QR_P)
                                     ).then_inc(loaded.sem, 16)

                        def load(dst, src):
                            sp.dma_start(dst, src).then_inc(w2_loaded.sem, 16)
                        load(tri[:, :, :], w["const_tri"])
                        load(pT[:, :], w["rot_PT"])
                        load(pw[:, :, :], w["const_pow"])
                        for t in range(QR_T):
                            load(wv[:, t, :, :].rearrange("p a b -> p (a b)"), w["rot_W"][t * QR_P:(t + 1) * QR_P, :])
                        for b in range(B):
                            load(bias_v[b:b + 1, :, :].rearrange("p a b -> p (a b)"), w["rot_b"])
                        sp.wait_ge(dve_done.sem, dve_done.at(8))
                        for b in range(B):
                            sp.dma_start(up[:, b, :], vrow[b:b + 1, :, :].rearrange("o a b -> o (a b)").rearrange(
                                "o (i j) -> o i j", j=RK)).then_inc(grid_in.sem, 16)

                    @block.vector
                    def _(dve):
                        STEPS = 9

                        def reflect(j, beside=None):
                            base = STEPS * j

                            def step(ins):
                                return ins.then_inc(qr_step.sem, 1)

                            def after(k):
                                dve.wait_ge(qr_step.sem, qr_step.at(base + k))

                            dve.tensor_tensor(v[:, :], z[:, :, bass.ds(j, 1)].rearrange("p t o -> p (t o)"),
                                              row_mask[:, :, bass.ds(j, 1)].rearrange("p t o -> p (t o)"),
                                              ALU.mult).then_inc(qr_col.sem, 1)
                            if beside is not None:
                                beside()
                            dve.wait_ge(qr_copy.sem, qr_copy.at(2 * j + 1))
                            alpha = ya[:, 1, bass.ds(j, 1)]
                            norm2 = ya[:, 0, bass.ds(j, 1)]
                            step(dve.tensor_scalar(small[:, 1:2], alpha, 0.0, 2.0, ALU.is_ge, ALU.mult))
                            after(1)
                            dve.wait_ge(qr_copy.sem, qr_copy.at(2 * j + 2))
                            step(dve.scalar_tensor_tensor(small[:, 2:3], small[:, 1:2], -1.0, small[:, 0:1],
                                                          ALU.add, ALU.mult))
                            after(2)
                            step(dve.scalar_tensor_tensor(small[:, 3:4], alpha, small[:, 2:3], norm2,
                                                          ALU.mult, ALU.add))
                            step(dve.scalar_tensor_tensor(v[:, 0:1], e[:, :], small[:, 2:3], v[:, 0:1],
                                                          ALU.mult, ALU.add))
                            after(3)
                            step(dve.tensor_scalar(small[:, 4:5], small[:, 3:4], 1e-37, None, ALU.max))
                            step(dve.scalar_tensor_tensor(wr[:, 0, :], ya[:, 1, :], small[:, 2:3], ya[:, 0, :],
                                                          ALU.mult, ALU.add))
                            after(5)
                            step(dve.reciprocal(small[:, 5:6], small[:, 4:5]))
                            after(7)
                            step(dve.tensor_scalar(wr[:, 1, :], wr[:, 0, :], small[:, 5:6], -1.0, ALU.mult, ALU.mult))
                            dve.tensor_copy(e[:, :], ident[0:QR_P, bass.ds(j + 1, 1)]).then_inc(qr_row.sem, 1)
                            after(8)
                            for t in range(QR_T):
                                ins = dve.scalar_tensor_tensor(z[:, t, :], wr[:, 1, :], v[:, t:t + 1], z[:, t, :],
                                                               ALU.mult, ALU.add)
                                if t == 0:
                                    ins.then_inc(qr_row.sem, 1)
                            step(ins)
                            after(9)

                        step = Chain(dve, dve_done)
                        products = 0

                        def product():
                            nonlocal products
                            products += 1
                            dve.wait_ge(pe_done.sem, pe_done.at(products))

                        def entries(c, u):
                            dve.wait_ge(pe_done.sem, pe_done.at(c + 1))
                            dve.tensor_tensor(vrow[:, bass.ds(c, 1), :].rearrange("p o c -> p (o c)"),
                                              (wide if u % 2 == 0 else wide2)[0:B, :],
                                              bias_v[:, bass.ds(c, 1), :].rearrange("p o c -> p (o c)"), ALU.add
                                              ).then_inc(dve_done.sem, 1)

                        def horner(i):
                            dve.wait_ge(up_ready.sem, up_ready.at(i + 1))
                            dve.tensor_scalar(sq4, two4, pw[:, 2, bass.ds(i, 1)], None, ALU.mult).then_inc(g_hi.sem, 1)
                            dve.wait_ge(g_hi.sem, g_hi.at(i + 1))
                            dve.tensor_tensor(tm4, sq4, eye4, ALU.add).then_inc(g_split.sem, 1)

                        def keep_squares(i):
                            for b in range(B):
                                dve.tensor_scalar(kept[:, b, :, :], term[:, b, :, :], ngt[:, b, bass.ds(i, 1)], None,
                                                  ALU.mult).then_inc(modulated.sem, 1)
                            dve.wait_ge(modulated.sem, modulated.at(2 * i + 2))
                            dve.wait_ge(mm_done.sem, mm_done.at(i + 1))
                            for b in range(B):
                                ins = dve.scalar_tensor_tensor(
                                    term[:, b, :, :], two[0:RK, 2 * b * RK:(2 * b + 2) * RK].rearrange("p (s c) -> p s c", s=2),
                                    gt[:, b, bass.ds(i, 1)], kept[:, b, :, :], ALU.mult, ALU.add)
                            ins.then_inc(added.sem, 1)
                            dve.wait_ge(added.sem, added.at(i + 1))

                        dve.wait_ge(loaded.sem, loaded.at(32))
                        dve.tensor_copy(e[:, :], ident[0:QR_P, 0:1]).then_inc(qr_row.sem, 1)
                        repeat(dve, 0, AT_ENTRIES + 1, lambda j, n, u: reflect(j))
                        dve.wait_ge(w2_loaded.sem, w2_loaded.at(16 * NL))
                        repeat(dve, AT_ENTRIES + 1, 8, lambda j, n, u: reflect(j, lambda: entries(n, u)))
                        step.n = products = 8
                        repeat(dve, AT_ENTRIES + 9, AT_NORM - AT_ENTRIES - 9, lambda j, n, u: reflect(j))
                        dve.wait_ge(grid_in.sem, grid_in.at(16 * B))
                        product()
                        tr = two[0:RK, 0:B * RK].rearrange("p (b c) -> p b c", b=B)
                        step(dve.tensor_tensor(skew[:, :, 0, :], up[:, :, :], tr, ALU.subtract))
                        step(dve.tensor_scalar(skew[:, :, 1, :], skew[:, :, 0, :], -1.0, None, ALU.mult))
                        step(dve.tensor_tensor(absA[:, :, :], skew[:, :, 0, :], skew[:, :, 1, :], ALU.max))
                        step(dve.tensor_reduce(rs[:, :], absA[:, :, :], AX_X, ALU.add))
                        mark["sums"] = step(dve.memset(onesr[:, :], 1.0))
                        product()
                        step(dve.tensor_reduce(big[:, :], wide[0:B, 0:RK], AX_X, ALU.max))
                        mark["norm"] = step(dve.tensor_scalar(bigd[:, :], ident[0:B, 0:B], big[:, 0:1], None, ALU.mult))
                        product()
                        step(dve.tensor_copy(nrm[:, :], wide2[0:RK, 0:B]))
                        for b in range(B):
                            step(dve.tensor_scalar(gt[:, b, :], pw[:, 0, :], nrm[:, b:b + 1], None, ALU.is_lt))
                        step(dve.tensor_scalar(ngt[:, :, :], gt[:, :, :], -1.0, 1.0, ALU.mult, ALU.add))
                        step(dve.tensor_tensor(sf[:, :, :], gt[:, :, :],
                                               pw[:, 1, :].unsqueeze(1).broadcast_to([RK, B, SQUARINGS]), ALU.mult))
                        step(dve.tensor_reduce(sc[:, :], sf[:, :, :], AX_X, ALU.min))
                        step(dve.tensor_scalar(sc[:, :], sc[:, :], 1.0, None, ALU.add))
                        for b in range(B):
                            step(dve.tensor_scalar(skew[:, b, :, :], skew[:, b, :, :], sc[:, b:b + 1], None, ALU.mult))
                        step(dve.tensor_scalar(sq4, sk4, 1.0 / TAYLOR, None, ALU.mult))
                        mark["first"] = step(dve.tensor_tensor(tm4, sq4, eye4, ALU.add))
                        repeat(dve, AT_NORM, AT_TERMS + 1 - AT_NORM, lambda j, n, u: reflect(j))
                        repeat(dve, AT_TERMS + 1, HORNER, lambda j, n, u: reflect(j, lambda: horner(n)))
                        repeat(dve, AT_TERMS + 1 + HORNER, AT_SQUARES - AT_TERMS - HORNER, lambda j, n, u: reflect(j))
                        dve.wait_ge(g_split.sem, g_split.at(HORNER))
                        repeat(dve, AT_SQUARES + 1, SQUARINGS, lambda j, n, u: reflect(j, lambda: keep_squares(n)))
                        repeat(dve, AT_SQUARES + 1 + SQUARINGS, RK - AT_SQUARES - 1 - SQUARINGS, lambda j, n, u: reflect(j))
                        step(dve.tensor_tensor(tm4, tm4, eye4, ALU.subtract))

                        step(dve.tensor_tensor(tmp[:, :], z[0:RK, 0, :], tri[:, 1, :], ALU.mult))
                        step(dve.tensor_reduce(s1[:, 0:1], tmp[:, :], AX_X, ALU.add))
                        step(dve.reciprocal(s1[:, 1:2], s1[:, 0:1]))
                        step(dve.tensor_tensor(tmp[:, :], z[0:RK, 0, :], tri[:, 0, :], ALU.mult))
                        step(dve.tensor_scalar(power[:, 0, :], tmp[:, :], s1[:, 1:2], -1.0, ALU.mult, ALU.mult))
                        mark["power", 0] = step(dve.tensor_tensor(prod[:, :], power[:, 0, :], tri[:, 1, :], ALU.add))
                        product()
                        mark["turned"] = step(dve.tensor_copy(power[:, 1, :], wide[0:RK, 0:RK]))
                        for k in range(1, INV):
                            product()
                            mark["power", k] = step(dve.tensor_copy(power[:, :, :].rearrange("p a c -> p (a c)"),
                                                                    wide[0:RK, 0:2 * RK]))
                            product()
                            mark["prod", k] = step(dve.tensor_tensor(prod[:, :], wide2[0:RK, 0:RK], prod[:, :], ALU.add))
                        product()
                        mark["uT"] = step(dve.tensor_scalar(uT[:, :], wide2[0:RK, 0:C], s1[:, 1:2], None, ALU.mult))
                        product()
                        for b in range(B):
                            mark["g", b] = step(dve.tensor_copy(g_u[:, b, :], (wide if b == 0 else wide2)[0:RK, 0:C]))
                        for i in range(3 * B):
                            K = KROWS[i % 3]
                            product()
                            mark["m", i] = step(dve.tensor_copy(m_rot[0:K, i // 3, i % 3, :],
                                                                (wide if i % 2 == 0 else wide2)[0:K, 0:C]))
                        mark["steps"] = step.n
                        mark["products"] = products

                    @block.scalar
                    def _(act):
                        act.preload_act_table(ACT.Sqrt)

                        def take(j):
                            act.wait_ge(qr_dots.sem, qr_dots.at(j + 1))
                            act.activation(ya[:, :, :].rearrange("p a b -> p (a b)"), dots[0:QR_P, 0:2 * RK], ACT.Copy
                                           ).then_inc(qr_copy.sem, 1)
                            act.activation(small[:, 0:1], dots[0:QR_P, bass.ds(j, 1)], ACT.Sqrt).then_inc(qr_copy.sem, 1)

                        repeat(act, 0, RK, lambda j, n, u: take(j))

                    @block.tensor
                    def _(pe):
                        def products(j):
                            pe.wait_ge(qr_row.sem, qr_row.at(2 * j + 1))
                            pe.wait_ge(qr_copy.sem, qr_copy.at(2 * j))
                            pe.matmul(dots[0:QR_P, RK:2 * RK], e[:, :].broadcast_to([QR_P, QR_P]), z[:, 0, :],
                                      start=True, stop=True)
                            pe.wait_ge(qr_col.sem, qr_col.at(j + 1))
                            for t in range(QR_T):
                                ins = pe.matmul(dots[0:QR_P, 0:RK], v[:, t:t + 1].broadcast_to([QR_P, QR_P]), z[:, t, :],
                                                start=t == 0, stop=t == QR_T - 1)
                            ins.then_inc(qr_dots.sem, 1)

                        def after(name):
                            pe.wait_ge(dve_done.sem, dve_done.at(mark[name]))

                        def done(ins):
                            ins.then_inc(pe_done.sem, 1)

                        def entries(c, u):
                            pe.wait_ge(dve_done.sem, dve_done.at(c - 1))
                            for t in range(QR_T):
                                mm = pe.matmul((wide if u % 2 == 0 else wide2)[0:B, :], s_thirds[:, t, :],
                                               wv[:, t, bass.ds(c, 1), :].rearrange("p o c -> p (o c)"),
                                               start=t == 0, stop=t == QR_T - 1)
                            done(mm)

                        def four(left):
                            for b in range(B):
                                for s in (1, 0):
                                    o = (2 * b + s) * RK
                                    if b == 0 and s == 1:
                                        pe.matmul(two[:, o:o + RK], left[:, b, :, :].rearrange("p s c -> p (s c)"),
                                                  term[:, b, s, :], start=True, stop=True)
                                        continue
                                    mm = pe.matmul(two[0:RK, o:o + RK], left[:, b, 1 - s, :], term[:, b, s, :],
                                                   start=True, stop=True)
                            return mm

                        def with_term(j, i):
                            products(j)
                            pe.wait_ge(g_split.sem, g_split.at(i))
                            four(skew).then_inc(up_ready.sem, 1)

                        def with_square(j, i):
                            products(j)
                            pe.wait_ge(added.sem, added.at(i))
                            four(term).then_inc(mm_done.sem, 1)

                        def with_entries(j, c, u):
                            products(j)
                            entries(c, u)

                        repeat(pe, 0, AT_ENTRIES, lambda j, n, u: products(j))
                        pe.wait_ge(w2_loaded.sem, w2_loaded.at(16 * NL))
                        repeat(pe, AT_ENTRIES, 8, with_entries)
                        repeat(pe, AT_ENTRIES + 8, AT_NORM - AT_ENTRIES - 8, lambda j, n, u: products(j))
                        pe.wait_ge(grid_in.sem, grid_in.at(16 * B))
                        for b in range(B):
                            mm = pe.transpose(two[0:RK, b * RK:(b + 1) * RK], up[:, b, :], ident[0:RK, 0:RK])
                        done(mm)
                        after("sums")
                        done(pe.transpose(wide[0:B, 0:RK], rs[:, :], ident[0:RK, 0:RK]))
                        after("norm")
                        done(pe.matmul(wide2[0:RK, 0:B], onesr[:, :], bigd[:, :], start=True, stop=True))
                        after("first")

                        repeat(pe, AT_NORM, AT_TERMS - AT_NORM, lambda j, n, u: products(j))
                        repeat(pe, AT_TERMS, HORNER, lambda j, n, u: with_term(j, n))
                        repeat(pe, AT_TERMS + HORNER, AT_SQUARES - AT_TERMS - HORNER, lambda j, n, u: products(j))
                        pe.wait_ge(g_split.sem, g_split.at(HORNER))
                        repeat(pe, AT_SQUARES, SQUARINGS, lambda j, n, u: with_square(j, n))
                        repeat(pe, AT_SQUARES + SQUARINGS, RK - AT_SQUARES - SQUARINGS, lambda j, n, u: products(j))
                        after(("power", 0))
                        done(pe.transpose(wide[0:RK, 0:RK], power[:, 0, :], ident[0:RK, 0:RK]))
                        after("turned")
                        for k in range(1, INV):
                            pe.matmul(wide[0:RK, 0:RK], power[:, 1, :], power[:, 0, :], start=True, stop=True)
                            done(pe.matmul(wide[0:RK, RK:2 * RK], power[:, 0, :], power[:, 1, :], start=True, stop=True))
                            after(("power", k))
                            done(pe.matmul(wide2[0:RK, 0:RK], power[:, 1, :], prod[:, :], start=True, stop=True))
                            after(("prod", k))
                        done(pe.matmul(wide2[0:RK, 0:C], prod[:, :], pT[:, :], start=True, stop=True))
                        after("uT")
                        for b in range(B):
                            mm = pe.matmul((wide if b == 0 else wide2)[0:RK, 0:C], term[:, b, 1, :], uT[:, :],
                                           start=True, stop=True)
                        done(mm)
                        after(("g", 1))
                        for i in range(3 * B):
                            if i > 1:
                                after(("m", i - 2))
                            K, s = KROWS[i % 3], i % 3
                            done(pe.matmul((wide if i % 2 == 0 else wide2)[0:K, 0:C], uT[:, s * P:s * P + K],
                                           g_u[:, i // 3, :], start=True, stop=True))
                loaded.passed(32)
                w2_loaded.passed(16 * NL)
                grid_in.passed(16 * B)
                qr_step.passed(9 * RK)
                qr_col.passed(RK)
                qr_row.passed(2 * RK + 1)
                qr_dots.passed(RK)
                qr_copy.passed(2 * RK)
                dve_done.passed(mark["steps"])
                pe_done.passed(mark["products"])
                for s in (up_ready, g_hi, g_split):
                    s.passed(HORNER)
                modulated.passed(2 * SQUARINGS)
                mm_done.passed(SQUARINGS)
                added.passed(SQUARINGS)

        def load_slabs(sp, raw, width, w_dram, bias_dram, landed):
            for s in range(2):
                sp.dma_start(raw[:, s, 0:width], w_dram[s * P:s * P + P, :]).then_inc(landed.sem, 16)
            for r in range(3):
                sp.dma_start(raw[R * r:R * r + R, 2, 0:width], w_dram[2 * P:C, :]).then_inc(landed.sem, 16)
            for r in range(2 if bias_dram is not None else 0):
                sp.dma_start(raw[RS + r:RS + r + 1, 2, 0:width], bias_dram).then_inc(landed.sem, 16)

        def split_weights(width, hi, lo, third, raw, tail, loads, landed, counted):

            def split(dve):
                step = Chain(dve, counted)
                dve.wait_ge(landed.sem, landed.at(16 * loads))
                step(dve.tensor_copy(hi[:, :, :], raw[:, 0:2, 0:width]))
                dve.tensor_tensor(lo[:, :, :], raw[:, 0:2, 0:width], hi[:, :, :].bitcast(F32), ALU.subtract)
                step(dve.tensor_copy(third[0:RA, :], raw[0:RA, 2, 0:width]))
                step(dve.tensor_tensor(tail[:, :], raw[0:RA, 2, 0:width], third[0:RA, :].bitcast(F32), ALU.subtract))
                step(dve.tensor_scalar(tail[:, :], tail[:, :], mix[0:RA, 1:2], None, ALU.mult))
                step(dve.scalar_tensor_tensor(third[0:RA, :], third[0:RA, :].bitcast(F32), mix[0:RA, 0:1], tail[:, :],
                                              ALU.mult, ALU.add))

            def passed():
                landed.passed(16 * loads)
                counted.passed(SPLIT_STEPS)
            return split, passed

        def deviations(dve, act, tiles):
            t0, t1 = tiles
            if dve is not None:
                for t in range(t0, t1):
                    dve.bn_aggr(mv[:, t, :], stats[:, t, :]).then_inc(stats_in.sem, 1)
                dve.wait_ge(std_ready.sem, std_ready.at(1))
                dve.reciprocal(rstd[:, t0:t1], std[:, t0:t1]).then_inc(rstd_ready.sem, 1)
                dve.wait_ge(rstd_ready.sem, rstd_ready.at(1))
            if act is not None:
                act.preload_act_table(ACT.Sqrt)
                act.wait_ge(stats_in.sem, stats_in.at(t1 - t0))
                act.activation(std[:, t0:t1], mv[:, t0:t1, 1], ACT.Sqrt, bias=eps_col[:, 0:1]).then_inc(std_ready.sem, 1)

        def norm_stages(ctx, l, ki, xn, m, turn_ps, hi_at, lo_at, third_at, reused):

            def normalise(dve, t, tile, k):
                dve.wait_ge(turned.sem, turned.at(t - 1))
                dve.tensor_scalar(xn[:, k, 0:2 * P], x[:, tile, 0:2 * P], mv[:, tile, 0:1], rstd[:, bass.ds(tile, 1)], ALU.subtract, ALU.mult)
                dve.tensor_scalar(xn[:, k, 2 * P:2 * P + RS].rearrange("p (r c) -> p r c", r=3),
                                  x[:, tile, 2 * P:C].unsqueeze(1).broadcast_to([P, 3, R]), mv[:, tile, 0:1],
                                  rstd[:, bass.ds(tile, 1)],
                                  ALU.subtract, ALU.mult).then_inc(normed.sem, 1)

            def turn(pe, t, k):
                pe.wait_ge(normed.sem, normed.at(t + 1))
                pe.wait_ge(modulated.sem, modulated.at(t - 1))
                for s in range(3):
                    n = RA if s == 2 else P
                    mm = pe.transpose(turn_ps[k][0:n, s * P:s * P + P], xn[:, k, s * P:s * P + n], ident[:, :])
                mm.then_inc(turned.sem, 1)

            def modulate(act, t, b, k):
                act.wait_ge(turned.sem, turned.at(t + 1))
                act.wait_ge(split_done.sem, split_done.at(t - 1))
                for s in range(3):
                    n = RA if s == 2 else P
                    a = act.activation(m[0:n, k, s, :], turn_ps[k][0:n, s * P:s * P + P], ACT.Identity,
                                       scale=modc[0:n, l, ki + 1, s, b:b + 1], bias=modc[0:n, l, ki, s, b:b + 1])
                a.then_inc(modulated.sem, 1)

            def split(dve, t, k):
                dve.wait_ge(modulated.sem, modulated.at(t + 1))
                if reused:
                    dve.wait_ge(qkv_ready.sem, qkv_ready.at(t - 1))
                hi, lo, third = hi_at(t, k), lo_at(t, k), third_at(t, k)
                dve.tensor_copy(hi, m[:, k, 0:2, :])
                dve.tensor_copy(third[0:RA], m[0:RA, k, 2, :]).then_inc(hi_ready.sem, 1)
                dve.wait_ge(hi_ready.sem, hi_ready.at(t + 1))
                dve.tensor_tensor(lo, m[:, k, 0:2, :], hi.bitcast(F32), ALU.subtract)
                dve.tensor_tensor(third[R:2 * R], m[R:2 * R, k, 2, :], third[R:2 * R].bitcast(F32), ALU.subtract
                                  ).then_inc(split_done.sem, 1)
            return normalise, turn, modulate, split

        def split_products(pe, out_ap, lhs, rhs):
            (lh, ll, l3), (rh, rl, r3) = lhs, rhs
            n = 0
            for s in range(2):
                for a, b in ((lh, rh), (lh, rl), (ll, rh)):
                    pe.matmul(out_ap, a(s), b(s), start=n == 0, stop=False)
                    n += 1
            return pe.matmul(out_ap, l3, r3, start=False, stop=True)

        class LayerMemory:

            def __init__(self, l, ctx):
                self.l = l
                self.qs = sb(f"qs{l}", [P, RING, L], BF16, ctx=ctx)
                self.ks = sb(f"ks{l}", [P, RING, L], BF16, ctx=ctx)
                self.wp = sb(f"wp{l}", [P, G, C], ctx=ctx)
                given = self.ks[:, :, :].rearrange("p r c -> p (r c)").bitcast(F32)
                self.raw = given[:, 0:9 * C].rearrange("p (s c) -> p s c", s=3)
                self.tail = given[0:RA, 9 * C:12 * C]

            def splitter(self, ctx):
                self.hi = sb(f"wqh{self.l}", [P, 2, 3 * C], F32R, ctx=ctx)
                self.lo = sb(f"wql{self.l}", [P, 2, 3 * C], F32R, ctx=ctx)
                self.third = sb(f"wq3{self.l}", [RA, 3 * C], F32R, ctx=ctx)
                return split_weights(3 * C, self.hi, self.lo, self.third, self.raw, self.tail, 7, w_loaded, w_step)

            def load_qkv(self, sp):
                load_slabs(sp, self.raw, 3 * C, w["qkv_w"][self.l], w["qkv_b"][self.l], w_loaded)

            def clear_projection(self, pool):
                pool.memset(self.wp[:, :, :], 0.0).then_inc(wp_cleared.sem, 1)

            def load_projection(self, sp):
                sp.wait_ge(wp_cleared.sem, wp_cleared.at(1))
                for g in range(G):
                    for j in range(4):
                        h = 4 * g + j
                        sp.dma_start(self.wp[32 * j:32 * j + D, g, :], w["proj_w"][self.l][h * D:(h + 1) * D, :]
                                     ).then_inc(proj_loaded.sem, 16)
                sp.dma_start(self.wp[D:D + 1, 0, :], w["proj_b"][self.l]).then_inc(proj_loaded.sem, 16)

        def qkv_phase(l, b, mem, stack, val):
            with ExitStack() as ctx:
                split_wq, wq_passed = mem.splitter(ctx)
                wh, wl, w3 = mem.hi, mem.lo, mem.third
                xn = sb(f"xn{l}{b}", [P, 2, XN], ctx=ctx)
                m = sb(f"m{l}{b}", [P, 2, 3, P], ctx=ctx)
                ph = sb(f"ph{l}{b}", [P, 2, 2, P], F32R, ctx=ctx)
                pl = sb(f"pl{l}{b}", [P, 2, 2, P], F32R, ctx=ctx)
                p3 = sb(f"p3{l}{b}", [RA, 2, P], F32R, ctx=ctx)
                qk = sb(f"qk{l}{b}", [P, 2, 2, H, D], ctx=ctx)
                rem = sb(f"rem{l}{b}", [P, 2, H, D], ctx=ctx)
                turn_ps = [bank(f"turn{l}{b}{k}", ctx) for k in range(2)]
                qkv_ps = [[bank(f"qkv{l}{b}{k}{n}", ctx) for n in range(3)] for k in range(2)]
                is3 = l == 2
                if is3:
                    cen = mem.qs[:, 0:2, :].rearrange("p r c -> p (r c)").bitcast(F32)[:, 0:2 * C].rearrange("p (h d) -> p h d", d=D)
                    hs = sb(f"hs{b}", [P, 4, 2 * H], ctx=ctx)
                    gqk = sb(f"gqk{b}", [P, 2, D], ctx=ctx)
                normalise, turn, modulate, split = norm_stages(
                    ctx, l, 0, xn, m, turn_ps, lambda t, k: ph[:, k], lambda t, k: pl[:, k], lambda t, k: p3[:, k], True)

                with nc.Block() as block:
                    @block.sync
                    def _(sp):
                        if is3:
                            for n, g in enumerate((w["g_q"], w["g_k"])):
                                sp.dma_start(gqk[:, n, :], g.rearrange("(o c) -> o c", o=1).broadcast_to([P, D])
                                             ).then_inc(loaded.sem, 16)
                        if is3 and b == 0:
                            mem.load_qkv(sp)
                        if b == 0:
                            mem.load_projection(sp)

                    @block.gpsimd
                    def _(pool):
                        pool.memset(xn[:, :, 2 * P + RS:XN], 1.0).then_inc(pool_done.sem, 1)
                        if b == 0:
                            mem.clear_projection(pool)
                        for t in range(TB):
                            pool.memset(stack[:, t, 1, :, KD:KA], 1.0).then_inc(pool_done.sem, 1)
                        pool.memset(val[:, :, :, D:D + 1], 1.0).then_inc(pool_done.sem, 1)
                        pool.memset(val[:, :, :, D + 1:32], 0.0).then_inc(pool_done.sem, 1)
                        with pool.Fori(0, TB) as t:
                            pool.wait_ge(qk_split.sem, qk_split.at(t + 1))

                            def slot(a, s):
                                return stack[:, t, a, :, s * D:(s + 1) * D]

                            pool.tensor_copy(slot(0, 3), slot(0, 0))
                            pool.tensor_copy(slot(0, 5), slot(0, 1))
                            pool.tensor_copy(slot(1, 3), slot(1, 1))

                    def qkv(pe, t, k):
                        pe.wait_ge(split_done.sem, split_done.at(t + 1))
                        pe.wait_ge(qkv_taken.sem, qkv_taken.at(t - 1))
                        for n in range(3):
                            cols = slice(n * C, n * C + C)
                            mm = split_products(
                                pe, qkv_ps[k][n][:, 0:C],
                                (lambda s: ph[:, k, s, :], lambda s: pl[:, k, s, :], p3[0:RA, k, :]),
                                (lambda s: wh[:, s, cols], lambda s: wl[:, s, cols], w3[0:RA, cols]))
                        mm.then_inc(qkv_ready.sem, 1)

                    def take(act, t, k):
                        act.wait_ge(qkv_ready.sem, qkv_ready.at(t + 1))
                        act.wait_ge(qk_split.sem, qk_split.at(t - 1))
                        for n in range(2):
                            act.activation(qk[:, k, n, :, :].rearrange("p h d -> p (h d)"), qkv_ps[k][n][:, 0:C], ACT.Copy,
                                           scale=SCALE if n == 0 and not is3 else 1.0)
                        act.activation(val[:, t, :, 0:D], qkv_ps[k][2][:, 0:C].rearrange("p (h d) -> p h d", h=H),
                                       ACT.Copy).then_inc(qkv_taken.sem, 1)

                    def head_deviations(act, t):
                        if is3:
                            act.wait_ge(qk_step.sem, qk_step.at(11 * t + 5))
                            act.activation(hs[:, 2, :], hs[:, 1, :], ACT.Sqrt, scale=1.0 / D, bias=eps_col[:, 0:1]
                                           ).then_inc(qk_std.sem, 1)

                    def repeat(act, t):
                        act.wait_ge(qk_split.sem, qk_split.at(t + 1))
                        for a, s in ((0, 3 + 1), (1, 2), (1, 5)):
                            act.activation(stack[:, t, a, :, s * D:(s + 1) * D], stack[:, t, a, :, 0:D], ACT.Copy)

                    per = 11 if is3 else 3

                    def parts(dve, t, k, beside=None):
                        n = 0

                        def link(ins):
                            nonlocal n
                            n += 1
                            ins.then_inc(qk_step.sem, 1)
                            dve.wait_ge(qk_step.sem, qk_step.at(per * t + n))
                        dve.wait_ge(qkv_taken.sem, qkv_taken.at(t + 1))
                        both = qk[:, k, :, :, :].rearrange("p a h d -> p (a h) d")
                        if is3:
                            link(dve.tensor_reduce(hs[:, 0, :], both, AX_X, ALU.add))
                            link(dve.tensor_scalar(hs[:, 0, :], hs[:, 0, :], 1.0 / D, None, ALU.mult))
                            link(dve.tensor_tensor(both, both, hs[:, 0, :].unsqueeze(2).broadcast_to([P, 2 * H, D]),
                                                   ALU.subtract))
                            link(dve.tensor_tensor(cen[:, :, :], both, both, ALU.mult))
                            link(dve.tensor_reduce(hs[:, 1, :], cen[:, :, :], AX_X, ALU.add))
                            if beside is not None:
                                beside()
                            dve.wait_ge(qk_std.sem, qk_std.at(t + 1))
                            link(dve.reciprocal(hs[:, 3, :], hs[:, 2, :]))
                            link(dve.tensor_tensor(both, both, hs[:, 3, :].unsqueeze(2).broadcast_to([P, 2 * H, D]),
                                                   ALU.mult))
                            link(dve.tensor_tensor(qk[:, k, :, :, :].rearrange("p a h d -> p a h d"), qk[:, k, :, :, :],
                                                   gqk[:, :, :].unsqueeze(2).broadcast_to([P, 2, H, D]), ALU.mult))
                        src = qk[:, k, :, :, :]
                        def slot(a, s):
                            return stack[:, t, a, :, s * D:(s + 1) * D]
                        for a in range(2):
                            ins = dve.tensor_copy(slot(a, 0), src[:, a])
                        link(ins)
                        for a in range(2):
                            ins = dve.tensor_tensor(rem[:, a, :, :], src[:, a], slot(a, 0), ALU.subtract)
                        link(ins)
                        for a in range(2):
                            ins = dve.tensor_copy(slot(a, 1), rem[:, a, :, :])
                        link(ins)
                        dve.tensor_tensor(slot(0, 2), rem[:, 0, :, :], slot(0, 1), ALU.subtract)
                        dve.tensor_tensor(slot(1, 4), rem[:, 1, :, :], slot(1, 1), ALU.subtract).then_inc(qk_split.sem, 1)

                    @block.tensor
                    def _(pe):
                        pe.wait_ge(pool_done.sem, pool_done.at(1))
                        turn(pe, 0, 0)
                        turn(pe, 1, 1)
                        pe.wait_ge(w_step.sem, w_step.at(SPLIT_STEPS))
                        with pe.Fori(0, TB // 2 - 1) as i:
                            for k in range(2):
                                qkv(pe, 2 * i + k, k)
                                turn(pe, 2 * i + k + 2, k)
                        qkv(pe, TB - 2, 0)
                        qkv(pe, TB - 1, 1)

                    @block.scalar
                    def _(act):
                        if is3:
                            act.wait_ge(loaded.sem, loaded.at(32))
                        deviations(None, act, (TB * b, TB * b + TB))
                        modulate(act, 0, b, 0)
                        modulate(act, 1, b, 1)
                        take(act, 0, 0)
                        with act.Fori(0, TB // 2 - 1) as i:
                            for k in range(2):
                                modulate(act, 2 * i + k + 2, b, k)
                                head_deviations(act, 2 * i + k)
                                take(act, 2 * i + k + 1, 1 - k)
                                repeat(act, 2 * i + k)
                        head_deviations(act, TB - 2)
                        take(act, TB - 1, 1)
                        repeat(act, TB - 2)
                        head_deviations(act, TB - 1)
                        repeat(act, TB - 1)

                    @block.vector
                    def _(dve):
                        if is3:
                            dve.wait_ge(loaded.sem, loaded.at(32))
                            dve.tensor_scalar(gqk[:, 0, :], gqk[:, 0, :], SCALE, None, ALU.mult).then_inc(dve_done.sem, 1)
                            dve.wait_ge(dve_done.sem, dve_done.at(1))
                        deviations(dve, None, (TB * b, TB * b + TB))

                        def parts_and_split(t, k):
                            if is3:
                                parts(dve, t, k, lambda: split(dve, t + 2, k))
                            else:
                                parts(dve, t, k)
                                split(dve, t + 2, k)

                        t0 = TB * b
                        normalise(dve, 0, t0, 0)
                        normalise(dve, 1, t0 + 1, 1)
                        split_wq(dve)
                        split(dve, 0, 0)
                        normalise(dve, 2, t0 + 2, 0)
                        split(dve, 1, 1)
                        with dve.Fori(0, TB // 2 - 2) as i:
                            for k in range(2):
                                normalise(dve, 2 * i + k + 3, 2 * i + (k + 3 + t0), 1 - k)
                                parts_and_split(2 * i + k, k)
                        normalise(dve, TB - 1, t0 + TB - 1, 1)
                        parts_and_split(TB - 4, 0)
                        parts_and_split(TB - 3, 1)
                        parts(dve, TB - 2, 0)
                        parts(dve, TB - 1, 1)
                wq_passed()
                if b == 0:
                    wp_cleared.passed(1)
                if is3:
                    loaded.passed(32)
                    dve_done.passed(1)
                    qk_std.passed(TB)
                pool_done.passed(TB + 3)
                stats_in.passed(TB)
                for s in (std_ready, rstd_ready):
                    s.passed(1)
                for s in (normed, turned, modulated, hi_ready, split_done, qkv_ready, qkv_taken, qk_split):
                    s.passed(TB)
                qk_step.passed(per * TB)

        def attention_phase(l, b, mem, stack, val, oT):
            with ExitStack() as ctx:
                qs, ks = mem.qs, mem.ks
                pr = sb(f"pr{l}{b}", [P, 4, 2, 512], ctx=ctx)
                vg = sb(f"vg{l}{b}", [P, TB, 4, 32], ctx=ctx)
                o_sb = sb(f"o_sb{l}{b}", [P, 2, 512], ctx=ctx)
                inv = sb(f"inv{l}{b}", [P, 4, 4, 32], ctx=ctx)
                rec = sb(f"rec{l}{b}", [P, 16], ctx=ctx)
                mx = sb(f"mx{l}{b}", [P, 4, TB, 2], ctx=ctx)
                nm = sb(f"nm{l}{b}", [P, 4, TB], ctx=ctx)
                mr = sb(f"mr{l}{b}", [P, 4, TB], ctx=ctx)
                mp = sb(f"mp{l}{b}", [P, 4, 3, TB], BF16, ctx=ctx)
                mpT = sb(f"mpT{l}{b}", [4 * 3 * TB, P], BF16, ctx=ctx)
                t_ps = bank(f"t_ps{l}{b}", ctx)
                t_bf = t_ps[:, :].bitcast(BF16)
                row_ps = bank(f"row_ps{l}{b}", ctx, (P, 2, 512))
                col_ps = [bank(f"cps{l}{b}{i}", ctx, (P, 2, 512)) for i in range(2)]
                o_ps = bank(f"o_ps{l}{b}", ctx)
                KT_N = TB
                SLOTS = 2 * KT_N
                LAG = 3

                def fills(it_up, it_down, it_tail):
                    f = []
                    for s in range(SLOTS):
                        if it_down and s == 0:
                            f.append((s, "max", 0))
                        if it_up and s % 4 == 1:
                            f.append((s, "q", s // 4 + 1))
                        if it_up and s % 4 == 2:
                            f.append((s, "k", s // 4 + 1))
                        if it_tail and s == LAG + 1:
                            f.append((s, "den", 1))
                        if it_tail and s == LAG + 2:
                            f.append((s, "inv", 1))
                        if it_down and s == KT_N + LAG + 1:
                            f.append((s, "den", 0))
                        if it_down and s == KT_N + LAG + 2:
                            f.append((s, "inv", 0))
                    return f

                FIRST, SECOND, FULL = (True, False, False), (True, True, False), (True, True, True)
                LAST, AFTER = (False, True, True), (False, False, True)
                N0, N1, NF_, NL_, NA_ = (len(fills(*a)) for a in (FIRST, SECOND, FULL, LAST, AFTER))
                TOTAL = 2 + N0 + N1 + (G - 2) * NF_ + NL_ + NA_

                def filled_before(it, kind):
                    if kind == FIRST:
                        return 2
                    if kind == SECOND:
                        return 2 + N0
                    if kind == AFTER:
                        return TOTAL - NA_
                    return 2 + N0 + N1 + (it - 2) * NF_

                def number(it, kind, what, j):
                    names = [f[1:] for f in fills(*kind)]
                    return filled_before(it, kind) + names.index((what, j))

                def downs(it, kind):
                    up, down, tail = kind
                    r = {}
                    for s in range(SLOTS):
                        if s < LAG and tail:
                            r[s] = (it - 2, SLOTS - LAG + s)
                        if s >= LAG and down:
                            r[s] = (it - 1, s - LAG)
                    return r

                def weighs(it, kind):
                    up, down, tail = kind
                    r = {}
                    for s in range(SLOTS):
                        if s <= LAG and tail:
                            r[s] = (it - 2, SLOTS - LAG - 1 + s)
                        if s > LAG and down:
                            r[s] = (it - 1, s - LAG - 1)
                    return r

                def fill_stacks(pe, group, j, what):
                    rows, a = (KD, 0) if what == "q" else (KA, 1)
                    head = (4 * group + j) % H
                    for t in range(TB):
                        ins = pe.transpose(t_bf[0:rows, t * P:t * P + P], stack[:, t, a, head, 0:rows], identb[:, :])
                    return ins

                def wide_rows(s, u):
                    return (row_ps, col_ps[0], col_ps[1])[(2 * s + u) % 3]

                def pe_iteration(pe, it, kind):
                    up = kind[0]
                    down_at, weigh_at = downs(it, kind), weighs(it, kind)

                    def fill(what, j):
                        n = number(it, kind, what, j)
                        pe.wait_ge(t_taken.sem, t_taken.at(n))
                        if what in "qk":
                            ins = fill_stacks(pe, it, j, what)
                        elif what == "max":
                            pe.wait_ge(max_step.sem, max_step.at(6 * it))
                            ins = pe.transpose(t_bf[0:4 * 3 * TB, 0:P], mp[:, :, :, :].rearrange("p j i t -> p (j i t)"),
                                               identb[:, :])
                        elif what == "den":
                            group = it - 1 if j == 0 else it - 2
                            pe.wait_ge(o_copied.sem, o_copied.at(2 * group + j + 1))
                            for q in range(512 // P):
                                ins = pe.matmul(t_ps[:, 4 * q:4 * q + 4], o_sb[:, j, q * P:q * P + P], sel_den[:, :],
                                                start=True, stop=True)
                        else:
                            group = it - 1 if j == 0 else it - 2
                            pe.wait_ge(inv_ready.sem, inv_ready.at(2 * group + j + 1))
                            for q in range(512 // P):
                                ins = pe.transpose(t_ps[:, q * P:q * P + P],
                                                   inv[:, q, :, :].rearrange("p j d -> p (j d)"), ident[:, :])
                        ins.then_inc(t_filled.sem, 1)

                    def scores(ge, e, pair):
                        qh, kt = e // KT_N, e % KT_N
                        n = 32 * ge + 2 * e + pair
                        pe.wait_ge(probs.sem, probs.at(n - 1))
                        for h in range(2):
                            slot = (4 * ge + 2 * pair + h) % RING
                            ins = pe.matmul(col_ps[pair][:, h, :], ks[0:KA, slot, kt * P:kt * P + P],
                                            qs[0:KA, slot, qh * 512:qh * 512 + 512], start=True, stop=True)
                        ins.then_inc(colscores.sem, 1)

                    def weigh(ge, e):
                        qh, kt = e // KT_N, e % KT_N
                        if qh == 0:
                            pe.wait_ge(v_staged.sem, v_staged.at(TB * ge + kt + 1))
                        if kt == 0:
                            pe.wait_ge(o_copied.sem, o_copied.at(2 * ge + qh))
                        pe.wait_ge(probs.sem, probs.at(32 * ge + 2 * e + 2))
                        for j in range(4):
                            ins = pe.matmul(o_ps[32 * j:32 * j + 32, :], vg[:, kt, j, :], pr[:, (2 * e + j // 2) % 4, j % 2, :],
                                            start=kt == 0, stop=kt == KT_N - 1)
                        ins.then_inc(weighed.sem, 1)

                    def maxima(s, u):
                        j = s // 4
                        if s % 4 == 0 and u == 0:
                            n = number(it, kind, "k", j) + 1 if j else filled_before(it, kind)
                            pe.wait_ge(t_taken.sem, t_taken.at(n))
                        n = 64 * it + 4 * s + u
                        t, half = (s % 4) * 2 + u // 2, u % 2
                        slot = (4 * it + j) % RING
                        pe.wait_ge(rowmax.sem, rowmax.at(n - 1))
                        pe.matmul(row_ps[:, u % 2, :], qs[0:KD, slot, t * P:t * P + P],
                                  ks[0:KD, slot, half * 512:half * 512 + 512], start=True, stop=True
                                  ).then_inc(rowscores.sem, 1)

                    def maxima_only(s):
                        j = s // 4
                        if s % 4 == 0:
                            pe.wait_ge(t_taken.sem, t_taken.at(number(it, kind, "k", j) + 1 if j else
                                                               filled_before(it, kind)))
                        for u in range(2):
                            n = 64 * it + 4 * s + 2 * u
                            t, slot = (s % 4) * 2 + u, (4 * it + j) % RING
                            pe.wait_ge(rowmax.sem, rowmax.at(n - 4))
                            for half in range(2):
                                ins = pe.matmul(wide_rows(s, u)[:, half, :], qs[0:KD, slot, t * P:t * P + P],
                                                ks[0:KD, slot, half * 512:half * 512 + 512], start=True, stop=True)
                            ins.then_inc(rowscores.sem, 2)

                    for s in range(SLOTS):
                        if kind[1] and s == LAG:
                            pe.wait_ge(max_rows_in.sem, max_rows_in.at(64 * it))
                        if kind == FIRST:
                            maxima_only(s)
                        for u in range(4 if kind != FIRST else 0):
                            if up:
                                maxima(s, u)
                            if s in down_at and u < 2:
                                scores(*down_at[s], u)
                            if s in weigh_at and u == 2:
                                weigh(*weigh_at[s])
                        for slot, what, j in fills(*kind):
                            if slot == s:
                                fill(what, j)

                def act_iteration(act, it, kind):
                    down_at, weigh_at = downs(it, kind), weighs(it, kind)

                    def empty(what, j):
                        act.wait_ge(t_filled.sem, t_filled.at(number(it, kind, what, j) + 1))
                        if what == "max":
                            act.wait_ge(max_rows_in.sem, max_rows_in.at(64 * (it - 1)))
                            act.activation(mpT[:, :], t_bf[0:4 * 3 * TB, 0:P], ACT.Copy).then_inc(t_taken.sem, 1)
                        else:
                            into, rows = (qs, KD) if what == "q" else (ks, KA)
                            act.activation(into[0:rows, (4 * it + j) % RING, :], t_bf[0:rows, :], ACT.Copy
                                           ).then_inc(t_taken.sem, 1)

                    def exps(ge, e):
                        for pair in range(2):
                            n = 32 * ge + 2 * e + pair
                            act.wait_ge(colscores.sem, colscores.at(n + 1))
                            if pair == 0:
                                act.wait_ge(weighed.sem, weighed.at(16 * ge + e - 1))
                            act.activation(pr[:, (2 * e + pair) % 4, :, :], col_ps[pair][:, :, :], ACT.Exp
                                           ).then_inc(probs.sem, 1)

                    def copy_o(ge, qh):
                        act.wait_ge(weighed.sem, weighed.at(16 * ge + KT_N * (qh + 1)))
                        act.activation(o_sb[:, qh, :], o_ps[:, :], ACT.Copy).then_inc(o_copied.sem, 1)

                    for s in range(SLOTS):
                        if s in down_at:
                            exps(*down_at[s])
                        if s in weigh_at and weigh_at[s][1] % KT_N == KT_N - 1:
                            copy_o(weigh_at[s][0], weigh_at[s][1] // KT_N)
                        for slot, what, j in fills(*kind):
                            if slot == s and what in ("q", "k", "max"):
                                empty(what, j)

                def dve_iteration(dve, it, kind):
                    up = kind[0]

                    def wait_fill(what, j):
                        dve.wait_ge(t_filled.sem, t_filled.at(number(it, kind, what, j) + 1))

                    def reduce(s):
                        j = s // 4
                        for u in range(2 if kind == FIRST else 0):
                            t = (s % 4) * 2 + u
                            dve.wait_ge(rowscores.sem, rowscores.at(64 * it + 4 * s + 2 * u + 2))
                            dve.tensor_reduce(mx[:, j, t, :], wide_rows(s, u)[:, :, :], AX_X, ALU.max
                                              ).then_inc(rowmax.sem, 2)
                        for u in range(4 if kind != FIRST else 0):
                            t, half = (s % 4) * 2 + u // 2, u % 2
                            dve.wait_ge(rowscores.sem, rowscores.at(64 * it + 4 * s + u + 1))
                            dve.tensor_reduce(mx[:, j, t, half:half + 1], row_ps[:, u % 2, :], AX_X, ALU.max
                                              ).then_inc(rowmax.sem, 1)

                    def invert(ge, qh):
                        wait_fill("den", qh)
                        dve.reciprocal(rec[:, :], t_ps[:, 0:16]).then_inc(t_taken.sem, 1)
                        dve.wait_ge(t_taken.sem, t_taken.at(number(it, kind, "den", qh) + 1))
                        dve.wait_ge(inv_ready.sem, inv_ready.at(2 * ge + qh))
                        dve.tensor_copy(inv[:, :, :, :], rec[:, :].rearrange("p (q j) -> p q j", j=4).unsqueeze(3)
                                        .broadcast_to([P, 4, 4, 32])).then_inc(inv_ready.sem, 1)

                    def normalise(ge, qh):
                        wait_fill("inv", qh)
                        dve.tensor_tensor(oT[:, ge, qh * 512:qh * 512 + 512], o_sb[:, qh, :], t_ps[:, :], ALU.mult
                                          ).then_inc(t_taken.sem, 1)

                    def maximum_parts():
                        n = 0

                        def link(ins):
                            nonlocal n
                            n += 1
                            ins.then_inc(max_step.sem, 1)
                            dve.wait_ge(max_step.sem, max_step.at(6 * it + n))
                        dve.wait_ge(rowmax.sem, rowmax.at(64 * it + 64))
                        link(dve.tensor_reduce(nm[:, :, :], mx[:, :, :, :], AX_X, ALU.max))
                        link(dve.tensor_scalar(mp[:, :, 0, :], nm[:, :, :], -1.0, None, ALU.mult))
                        link(dve.scalar_tensor_tensor(mr[:, :, :], nm[:, :, :], -1.0, mp[:, :, 0, :], ALU.mult, ALU.subtract))
                        link(dve.tensor_copy(mp[:, :, 1, :], mr[:, :, :]))
                        link(dve.tensor_tensor(mr[:, :, :], mr[:, :, :], mp[:, :, 1, :], ALU.subtract))
                        link(dve.tensor_copy(mp[:, :, 2, :], mr[:, :, :]))

                    for s in range(SLOTS):
                        if up:
                            reduce(s)
                        for slot, what, j in fills(*kind):
                            if slot == s and what == "den":
                                invert(it - 1 if j == 0 else it - 2, j)
                            if slot == s and what == "inv":
                                normalise(it - 1 if j == 0 else it - 2, j)
                    if up:
                        maximum_parts()

                def iterate(eng, one):
                    one(eng, 0, FIRST)
                    one(eng, 1, SECOND)
                    with eng.Fori(2, G) as it:
                        one(eng, it, FULL)
                    one(eng, G, LAST)
                    one(eng, G + 1, AFTER)

                with nc.Block() as block:
                    @block.tensor
                    def _(pe):
                        fill_stacks(pe, 0, 0, "q").then_inc(t_filled.sem, 1)
                        pe.wait_ge(t_taken.sem, t_taken.at(1))
                        fill_stacks(pe, 0, 0, "k").then_inc(t_filled.sem, 1)
                        iterate(pe, pe_iteration)

                    @block.scalar
                    def _(act):
                        act.preload_act_table(ACT.Exp)
                        for n, (into, rows) in enumerate(((qs, KD), (ks, KA))):
                            act.wait_ge(t_filled.sem, t_filled.at(n + 1))
                            act.activation(into[0:rows, 0, :], t_bf[0:rows, :], ACT.Copy).then_inc(t_taken.sem, 1)
                        iterate(act, act_iteration)

                    @block.vector
                    def _(dve):
                        iterate(dve, dve_iteration)

                    @block.gpsimd
                    def _(pool):
                        with pool.Fori(0, G) as g:
                            for kt in range(TB):
                                pool.wait_ge(weighed.sem, weighed.at(16 * g - KT_N + kt + 1))
                                pool.tensor_copy(vg[:, kt, :, :], val[:, kt, bass.ds(4 * g, 4), :]).then_inc(v_staged.sem, 1)

                    @block.sync
                    def _(sp):
                        def rows_of(g, after):
                            sp.wait_ge(t_taken.sem, t_taken.at(after))
                            for j in range(4):
                                sp.dma_start(qs[KD:KA, (4 * g + j) % RING, :], mpT[3 * TB * j:3 * TB * (j + 1), :]
                                             ).then_inc(max_rows_in.sem, 16)
                        rows_of(0, filled_before(1, SECOND) + 1)
                        with sp.Fori(1, G) as g:
                            rows_of(g, filled_before(g + 1, FULL) + 1)
                t_filled.passed(TOTAL)
                t_taken.passed(TOTAL)
                rowscores.passed(64 * G)
                rowmax.passed(64 * G)
                colscores.passed(32 * G)
                probs.passed(32 * G)
                weighed.passed(16 * G)
                o_copied.passed(2 * G)
                inv_ready.passed(2 * G)
                max_step.passed(6 * G)
                v_staged.passed(TB * G)
                max_rows_in.passed(64 * G)

        def project_phase(l, b, mem, oT):
            with ExitStack() as ctx:
                wp = mem.wp
                y = sb(f"y{l}{b}", [P, 2, C], ctx=ctx)
                ps = [bank(f"pp{l}{b}{k}", ctx) for k in range(2)]
                again = b + 1 < B
                with nc.Block() as block:
                    @block.sync
                    def _(sp):
                        if again:
                            mem.load_qkv(sp)

                    @block.tensor
                    def _(pe):
                        pe.wait_ge(proj_loaded.sem, proj_loaded.at(16 * 17))
                        for t in range(TB):
                            if t > 1:
                                pe.wait_ge(gated.sem, gated.at(t - 1))
                            for g in range(G):
                                mm = pe.matmul(ps[t % 2][:, 0:C], oT[:, g, t * P:t * P + P], wp[:, g, :],
                                               start=g == 0, stop=g == G - 1)
                            mm.then_inc(mm_done.sem, 1)

                    @block.vector
                    def _(dve):
                        for t in range(TB):
                            tile = TB * b + t
                            dve.wait_ge(mm_done.sem, mm_done.at(t + 1))
                            dve.tensor_tensor(y[:, t % 2, :], ps[t % 2][:, 0:C], gate_b[:, l, 0, b, :], ALU.mult
                                              ).then_inc(gated.sem, 1)
                            dve.wait_ge(gated.sem, gated.at(t + 1))
                            dve.tensor_tensor(x[:, tile, :], x[:, tile, :], y[:, t % 2, :], ALU.add).then_inc(added.sem, 1)
                            dve.wait_ge(added.sem, added.at(t + 1))
                            dve.bn_stats(stats[:, tile, :], x[:, tile, :])
                if not again:
                    proj_loaded.passed(16 * 17)
                for s in (mm_done, gated, added):
                    s.passed(TB)

        def mlp_phases(l, experts):
            CH = 256
            NCH = NT * P // CH
            with ExitStack() as ctx:
                hh = sb(f"hh{l}", [P, 2, NT * P], F32R, ctx=ctx)
                hl = sb(f"hl{l}", [P, 2, NT * P], F32R, ctx=ctx)
                h3 = sb(f"h3{l}", [RA, NT * P], F32R, ctx=ctx)
                w1r = sb(f"w1r{l}", [P, 3, FF], ctx=ctx)
                w2r = sb(f"w2r{l}", [P, NF + 1, C], ctx=ctx)

                w1h = sb(f"w1h{l}", [P, 2, FF], F32R, ctx=ctx)
                w1l = sb(f"w1l{l}", [P, 2, FF], F32R, ctx=ctx)
                w13 = sb(f"w13{l}", [RA, FF], F32R, ctx=ctx)
                w2h = sb(f"w2h{l}", [P, NF + 1, C], F32R, ctx=ctx)
                w2l = sb(f"w2l{l}", [P, NF, C], F32R, ctx=ctx)
                ones2 = sb(f"ones2{l}", [P, P], F32R, ctx=ctx)
                split_w1, w1_passed = split_weights(
                    FF, w1h, w1l, w13, w1r, sb(f"w1_tail{l}", [RA, FF], ctx=ctx), 7, w_loaded, w_step)

                def load_up(sp, ex):
                    load_slabs(sp, w1r, FF, w["fc1_w"][l][ex], w["fc1_b"][l][ex], w_loaded)

                def load_down(sp, ex):
                    sp.dma_start(w2r[:, 0:NF, :], w["fc2_w"][l][ex].rearrange("(k p) c -> p k c", p=P)
                                 ).then_inc(w2_loaded.sem, 16)
                    for r in range(2):
                        sp.dma_start(w2r[r:r + 1, NF, :], w["fc2_b"][l][ex]).then_inc(w2_loaded.sem, 16)
                with ExitStack() as ctx2:
                    xn = sb(f"xm{l}", [P, 2, XN], ctx=ctx2)
                    m = sb(f"mm{l}", [P, 2, 3, P], ctx=ctx2)
                    turn_ps = [bank(f"tm{l}{k}", ctx2) for k in range(2)]

                    def cols(t):
                        return bass.ds(t * P, P)
                    normalise, turn, modulate, split = norm_stages(
                        ctx2, l, 2, xn, m, turn_ps, lambda t, k: hh[:, :, cols(t)], lambda t, k: hl[:, :, cols(t)],
                        lambda t, k: h3[:, cols(t)], False)
                    with nc.Block() as block:
                        @block.gpsimd
                        def _(pool):
                            pool.memset(xn[:, :, 2 * P + RS:XN], 1.0).then_inc(pool_done.sem, 1)
                            pool.memset(w2r[:, NF, :], 0.0).then_inc(pool_done.sem, 1)

                        @block.sync
                        def _(sp):
                            load_up(sp, 0)
                            sp.wait_ge(pool_done.sem, pool_done.at(2))
                            load_down(sp, 0)

                        @block.tensor
                        def _(pe):
                            pe.wait_ge(pool_done.sem, pool_done.at(2))
                            with pe.Fori(0, NT // 2) as i:
                                for k in range(2):
                                    turn(pe, 2 * i + k, k)

                        @block.scalar
                        def _(act):
                            deviations(None, act, (0, NT))
                            for b in range(B):
                                with act.Fori(0, TB // 2) as i:
                                    for k in range(2):
                                        modulate(act, 2 * i + (k + TB * b), b, k)

                        @block.vector
                        def _(dve):
                            deviations(dve, None, (0, NT))
                            normalise(dve, 0, 0, 0)
                            normalise(dve, 1, 1, 1)
                            with dve.Fori(0, NT // 4 - 1) as i:
                                for u in range(4):
                                    normalise(dve, 4 * i + u + 2, 4 * i + u + 2, u % 2)
                                    split(dve, 4 * i + u, u % 2)
                            for t in (NT - 4, NT - 3):
                                normalise(dve, t + 2, t + 2, t % 2)
                                split(dve, t, t % 2)
                            split(dve, NT - 2, 0)
                            split(dve, NT - 1, 1)
                    pool_done.passed(2)
                    stats_in.passed(NT)
                    std_ready.passed(1)
                    rstd_ready.passed(1)
                    for s in (normed, turned, modulated, hi_ready, split_done):
                        s.passed(NT)
                if experts > 1:
                    gate_phase(hh, hl, h3)
                for ex in range(experts):
                    with ExitStack() as ctx2:
                        PAIRS = (NF + 1) // 2
                        g = sb(f"g{l}{ex}", [P, 2, 2, CH], ctx=ctx2)
                        gh = sb(f"gh{l}{ex}", [P, 2, NF, CH], F32R, ctx=ctx2)
                        gl = sb(f"gl{l}{ex}", [P, 2, NF, CH], F32R, ctx=ctx2)
                        y = sb(f"ym{l}{ex}", [P, 2, C], ctx=ctx2)
                        up_ps = [bank(f"up{l}{ex}{i}", ctx2) for i in range(PAIRS)]
                        dn_ps = [bank(f"dn{l}{ex}{i}", ctx2) for i in range(2)]
                        size = [min(2, NF - 2 * q) for q in range(PAIRS)]

                        def up(pe, c, k):
                            for q in range(PAIRS):
                                n = PAIRS * c + q
                                pe.wait_ge(gelu_done.sem, gelu_done.at(n - PAIRS + 1))
                                pbank = up_ps[q]
                                for i in range(size[q]):
                                    f = 2 * q + i
                                    cols = slice(f * P, f * P + P)
                                    mm = split_products(
                                        pe, pbank[:, i * CH:i * CH + CH],
                                        (lambda s: w1h[:, s, cols], lambda s: w1l[:, s, cols], w13[0:RA, cols]),
                                        (lambda s: hh[:, s, bass.ds(c * CH, CH)], lambda s: hl[:, s, bass.ds(c * CH, CH)],
                                         h3[0:RA, bass.ds(c * CH, CH)]))
                                mm.then_inc(up_ready.sem, 1)

                        def gelu(act, c, k):
                            for q in range(PAIRS):
                                n = PAIRS * c + q
                                act.wait_ge(up_ready.sem, up_ready.at(n + 1))
                                act.wait_ge(g_split.sem, g_split.at(n - 1 if q else n))
                                act.activation(g[:, q % 2, 0:size[q], :].rearrange("p i c -> p (i c)"),
                                               up_ps[q][:, 0:size[q] * CH], ACT.Gelu_apprx_tanh).then_inc(gelu_done.sem, 1)

                        def split_g(dve, c, k):
                            dve.wait_ge(mm_done.sem, mm_done.at(2 * (c - 1)))
                            for q in range(PAIRS):
                                n = PAIRS * c + q
                                dve.wait_ge(gelu_done.sem, gelu_done.at(n + 1))
                                fs = slice(2 * q, 2 * q + size[q])
                                dve.tensor_copy(gh[:, k, fs, :], g[:, q % 2, 0:size[q], :]).then_inc(g_hi.sem, 1)
                                dve.wait_ge(g_hi.sem, g_hi.at(n + 1))
                                dve.tensor_tensor(gl[:, k, fs, :], g[:, q % 2, 0:size[q], :], gh[:, k, fs, :].bitcast(F32),
                                                  ALU.subtract).then_inc(g_split.sem, 1)

                        def down(pe, c, k):
                            pe.wait_ge(g_split.sem, g_split.at(PAIRS * (c + 1)))
                            for i in range(2):
                                n = 2 * c + i
                                pe.wait_ge(gated.sem, gated.at(n - 1))
                                o = dn_ps[i][:, 0:C]
                                tok = slice(i * P, i * P + P)
                                for f in range(NF):
                                    pe.matmul(o, gh[:, k, f, tok], w2h[:, f, :], start=f == 0, stop=False)
                                    pe.matmul(o, gh[:, k, f, tok], w2l[:, f, :], start=False, stop=False)
                                    pe.matmul(o, gl[:, k, f, tok], w2h[:, f, :], start=False, stop=False)
                                pe.matmul(o, ones2[:, :], w2h[:, NF, :], start=False, stop=True).then_inc(mm_done.sem, 1)

                        def residual(dve, c, b, k):
                            for i in range(2):
                                n = 2 * c + i
                                dve.wait_ge(mm_done.sem, mm_done.at(n + 1))
                                dve.scalar_tensor_tensor(y[:, i, :], dn_ps[i][:, 0:C], cw[:, n, ex:ex + 1],
                                                         gate_b[:, l, 1, b, :], ALU.mult, ALU.mult).then_inc(gated.sem, 1)
                                dve.wait_ge(gated.sem, gated.at(n + 1))
                                dve.tensor_tensor(x[:, n, :], x[:, n, :], y[:, i, :], ALU.add).then_inc(added.sem, 1)
                                if ex == experts - 1:
                                    dve.wait_ge(added.sem, added.at(n + 1))
                                    dve.bn_stats(stats[:, n, :], x[:, n, :])

                        def split_w2(dve):
                            step = Chain(dve, w2_step)
                            dve.wait_ge(w2_loaded.sem, w2_loaded.at(48))
                            step(dve.tensor_copy(ones2[:, :], mix[:, 2:3].broadcast_to([P, P])))
                            step(dve.tensor_copy(w2h[:, :, :], w2r[:, :, :]))
                            step(dve.tensor_tensor(w2l[:, :, :], w2r[:, 0:NF, :], w2h[:, 0:NF, :].bitcast(F32), ALU.subtract))
                            step(dve.tensor_tensor(w2r[:, NF, :], w2r[:, NF, :], w2h[:, NF, :].bitcast(F32), ALU.subtract))
                            step(dve.tensor_scalar(w2r[:, NF, :], w2r[:, NF, :], mix[:, 3:4], None, ALU.mult))
                            step(dve.scalar_tensor_tensor(w2h[:, NF, :], w2h[:, NF, :].bitcast(F32), ident[:, 0:1],
                                                          w2r[:, NF, :], ALU.mult, ALU.add))

                        with nc.Block() as block:
                            @block.sync
                            def _(sp):
                                if ex + 1 < experts:
                                    sp.wait_ge(w_step.sem, w_step.at(SPLIT_STEPS))
                                    sp.wait_ge(w2_step.sem, w2_step.at(6))
                                    load_up(sp, ex + 1)
                                    load_down(sp, ex + 1)

                            @block.tensor
                            def _(pe):
                                pe.wait_ge(w_step.sem, w_step.at(SPLIT_STEPS))
                                up(pe, 0, 0)
                                with pe.Fori(0, NCH // 2 - 1) as i:
                                    for k in range(2):
                                        up(pe, 2 * i + k + 1, 1 - k)
                                        down(pe, 2 * i + k, k)
                                up(pe, NCH - 1, 1)
                                down(pe, NCH - 2, 0)
                                down(pe, NCH - 1, 1)

                            @block.scalar
                            def _(act):
                                act.preload_act_table(ACT.Gelu_apprx_tanh)
                                with act.Fori(0, NCH) as c:
                                    gelu(act, c, 0)

                            @block.vector
                            def _(dve):
                                split_w1(dve)
                                split_w2(dve)
                                split_g(dve, 0, 0)
                                with dve.Fori(0, NCH // 2 - 1) as i:
                                    for k in range(2):
                                        split_g(dve, 2 * i + k + 1, 1 - k)
                                        residual(dve, 2 * i + k, i // (NCH // 2 // B), k)
                                split_g(dve, NCH - 1, 1)
                                residual(dve, NCH - 2, B - 1, 0)
                                residual(dve, NCH - 1, B - 1, 1)
                    w1_passed()
                    w2_loaded.passed(48)
                    w2_step.passed(6)
                    for s in (up_ready, gelu_done, g_hi, g_split):
                        s.passed(PAIRS * NCH)
                    for s in (mm_done, gated, added):
                        s.passed(NT)

        def gate_phase(hh, hl, h3):
            with ExitStack() as ctx:
                raw = sb("wg_raw", [P, 3, P], ctx=ctx)
                gh = sb("wg_h", [P, 2, P], F32R, ctx=ctx)
                gl = sb("wg_l", [P, 2, P], F32R, ctx=ctx)
                g3 = sb("wg_3", [RA, P], F32R, ctx=ctx)
                lT = sb("lT", [EXPERTS, NT * P], ctx=ctx)
                lg = sb("lg", [P, NT, EXPERTS], ctx=ctx)
                top1 = sb("top1", [P, NT], ctx=ctx)
                ex = sb("ex", [P, NT, EXPERTS], ctx=ctx)
                rank = sb("rank", [P, NT, EXPERTS], ctx=ctx)
                cmp = sb("cmp", [P, NT, EXPERTS], ctx=ctx)
                ps = [bank(f"lg_ps{i}", ctx) for i in range(4)]
                col = bank("lg_col", ctx)
                split_gate, gate_passed = split_weights(
                    P, gh, gl, g3, raw, sb("wg_tail", [RA, P], ctx=ctx), 5, loaded, gate_step)
                with nc.Block() as block:
                    @block.gpsimd
                    def _(pool):
                        pool.memset(raw[:, :, :], 0.0).then_inc(pool_done.sem, 1)

                    @block.sync
                    def _(sp):
                        sp.wait_ge(pool_done.sem, pool_done.at(1))
                        load_slabs(sp, raw, EXPERTS, w["gate_w"], None, loaded)

                    @block.vector
                    def _(dve):
                        split_gate(dve)
                gate_passed()
                pool_done.passed(1)
                with nc.Block() as block:
                    @block.tensor
                    def _(pe):
                        for c in range(4):
                            cols = slice(c * 512, c * 512 + 512)
                            split_products(pe, ps[c][:, :],
                                           (lambda s: gh[:, s, :], lambda s: gl[:, s, :], g3[0:RA, :]),
                                           (lambda s: hh[:, s, cols], lambda s: hl[:, s, cols], h3[0:RA, cols])
                                           ).then_inc(pe_done.sem, 1)
                        for c in range(4):
                            pe.wait_ge(act_done.sem, act_done.at(c + 1))
                            for t in range(4 * c, 4 * c + 4):
                                mm = pe.transpose(col[:, 4 * t:4 * t + 4], lT[:, t * P:t * P + P], ident[0:4, 0:4])
                        mm.then_inc(pe_done.sem, 1)

                    @block.scalar
                    def _(act):
                        for c in range(4):
                            act.wait_ge(pe_done.sem, pe_done.at(c + 1))
                            act.activation(lT[:, c * 512:c * 512 + 512], ps[c][0:EXPERTS, :], ACT.Copy).then_inc(act_done.sem, 1)
                        act.wait_ge(dve_done.sem, dve_done.at(3))
                        act.activation(ex[:, :, :], cmp[:, :, :], ACT.Exp).then_inc(act_done.sem, 1)

                    @block.vector
                    def _(dve):
                        step = Chain(dve, dve_done)
                        dve.wait_ge(pe_done.sem, pe_done.at(5))
                        step(dve.tensor_copy(lg[:, :, :].rearrange("p t e -> p (t e)"), col[:, 0:NT * EXPERTS]))
                        step(dve.tensor_reduce(top1[:, :], lg[:, :, :], AX_X, ALU.max))
                        step(dve.tensor_tensor(cmp[:, :, :], lg[:, :, :],
                                               top1[:, :].unsqueeze(2).broadcast_to([P, NT, EXPERTS]), ALU.subtract))
                        step(dve.memset(rank[:, :, :], 0.0))
                        dve.wait_ge(act_done.sem, act_done.at(5))
                        for f in range(EXPERTS):
                            step(dve.tensor_tensor(cmp[:, :, :], lg[:, :, f:f + 1].broadcast_to([P, NT, EXPERTS]),
                                                   lg[:, :, :], ALU.is_gt))
                            step(dve.tensor_tensor(rank[:, :, :], rank[:, :, :], cmp[:, :, :], ALU.add))
                            if f < EXPERTS - 1:
                                n = EXPERTS - 1 - f
                                step(dve.tensor_tensor(cmp[:, :, f + 1:], lg[:, :, f:f + 1].broadcast_to([P, NT, n]),
                                                       lg[:, :, f + 1:], ALU.is_equal))
                                step(dve.tensor_tensor(rank[:, :, f + 1:], rank[:, :, f + 1:], cmp[:, :, f + 1:], ALU.add))
                        step(dve.scalar_tensor_tensor(ex[:, :, :], rank[:, :, :], 2.0, ex[:, :, :], ALU.is_lt, ALU.mult))
                        step(dve.tensor_reduce(top1[:, :], ex[:, :, :], AX_X, ALU.add))
                        step(dve.reciprocal(top1[:, :], top1[:, :]))
                        step(dve.tensor_tensor(cw[:, :, :], ex[:, :, :],
                                               top1[:, :].unsqueeze(2).broadcast_to([P, NT, EXPERTS]), ALU.mult))
                pe_done.passed(5)
                act_done.passed(5)
                dve_done.passed(4 + 4 * 2 + 3 * 2 + 4)

        def rotate_phase(mem):
            with ExitStack() as ctx:
                xT = sb("xT", [P, 2, 3, P], ctx=ctx)
                turn_ps = [bank(f"rt{k}", ctx) for k in range(2)]
                ps = [bank(f"rp{k}", ctx) for k in range(2)]
                KROWS = (P, P, R)

                def turn(pe, t, k):
                    pe.wait_ge(modulated.sem, modulated.at(t - 1))
                    for s in range(3):
                        mm = pe.transpose(turn_ps[k][0:KROWS[s], s * P:s * P + P], x[:, t, s * P:s * P + KROWS[s]], ident[:, :])
                    mm.then_inc(turned.sem, 1)

                with nc.Block() as block:
                    @block.sync
                    def _(sp):
                        mem.load_qkv(sp)

                    @block.tensor
                    def _(pe):
                        turn(pe, 0, 0)
                        for t in range(NT):
                            if t + 1 < NT:
                                turn(pe, t + 1, (t + 1) % 2)
                            pe.wait_ge(modulated.sem, modulated.at(t + 1))
                            pe.wait_ge(added.sem, added.at(t - 1))
                            for s in range(3):
                                K = KROWS[s]
                                mm = pe.matmul(ps[t % 2][:, 0:C], xT[0:K, t % 2, s, :], m_rot[0:K, t // TB, s, :],
                                               start=s == 0, stop=s == 2)
                            mm.then_inc(mm_done.sem, 1)

                    @block.scalar
                    def _(act):
                        for t in range(NT):
                            act.wait_ge(turned.sem, turned.at(t + 1))
                            act.wait_ge(mm_done.sem, mm_done.at(t - 1))
                            act.activation(xT[:, t % 2, 0:2, :].rearrange("p s c -> p (s c)"), turn_ps[t % 2][:, 0:2 * P], ACT.Copy)
                            act.activation(xT[0:R, t % 2, 2, :], turn_ps[t % 2][0:R, 2 * P:3 * P], ACT.Copy
                                           ).then_inc(modulated.sem, 1)

                    @block.vector
                    def _(dve):
                        for t in range(NT):
                            dve.wait_ge(mm_done.sem, mm_done.at(t + 1))
                            dve.tensor_tensor(x[:, t, :], x[:, t, :], ps[t % 2][:, 0:C], ALU.add).then_inc(added.sem, 1)
                            dve.wait_ge(added.sem, added.at(t + 1))
                            dve.bn_stats(stats[:, t, :], x[:, t, :])
                for s in (turned, modulated, mm_done, added):
                    s.passed(NT)

        for l in range(3):
            with ExitStack() as layer:
                mem = LayerMemory(l, layer)
                if l == 0:
                    modulation(mem)
                    rotation()
                elif l == 1:
                    rotate_phase(mem)
                for b in range(B):
                    with ExitStack() as ctx:
                        oT = sb(f"oT{l}{b}", [P, G, L], ctx=ctx)
                        with ExitStack() as ctx2:
                            stack = sb(f"stack{l}{b}", [P, TB, 2, H, SW], BF16, ctx=ctx2)
                            val = sb(f"val{l}{b}", [P, TB, H, 32], ctx=ctx2)
                            qkv_phase(l, b, mem, stack, val)
                            attention_phase(l, b, mem, stack, val, oT)
                        project_phase(l, b, mem, oT)
            mlp_phases(l, EXPERTS if l == 1 else 1)
            if l == 1:
                with nc.Block() as block:
                    @block.gpsimd
                    def _(pool):
                        pool.memset(cw[:, :, :], 1.0)
        with nc.Block() as block:
            @block.sync
            def _(sp):
                sp.dma_start(out.rearrange("b (t p) c -> p (b t) c", p=P), x[:, :, :]).then_inc(stored.sem, 16)
                sp.wait_ge(stored.sem, stored.at(16))


def constants():
    import numpy as np
    f = np.float32
    eye = np.eye(P, dtype=f)
    mix = np.zeros((P, 4), f)
    mix[0:2 * R, 0] = 1
    mix[RS, 0] = 1
    mix[0:RA, 1] = 1 - mix[0:RA, 0]
    mix[0:2, 2] = 1
    mix[1, 3] = 1
    sel = np.zeros((P, 4), f)
    for j in range(4):
        sel[32 * j + D, j] = 1
    rows = (np.arange(C)[:, None] >= np.arange(RK)[None, :]).astype(f)
    tri = np.stack([np.triu(np.ones((RK, RK), f), 1), np.eye(RK, dtype=f)], 1)
    i = np.arange(SQUARINGS)
    k = 1.0 / np.maximum(TAYLOR - 1 - i, 1)
    pw = np.broadcast_to(np.stack([2.0 ** i, 2.0 ** -(i + 1) - 1, k])[None], (RK, 3, SQUARINGS)).astype(f)
    return {"const_ident": eye, "const_mix": mix, "const_sel": sel, "const_rows": rows, "const_tri": tri, "const_pow": pw}


def laid_out(inputs):
    import numpy as np
    a = {k: np.ascontiguousarray(v) for k, v in inputs.items()}
    r = {
        "x": a["x"], "condT": np.ascontiguousarray(a["cond_1152"].T),
        "rot_P": a["L1_cond_P"], "rot_PT": np.ascontiguousarray(a["L1_cond_P"].T),
        "g_q": a["L3_cond_g_q"], "g_k": a["L3_cond_g_k"], "gate_w": a["L2_cond_w_gate"],
    }
    iu, ju = np.triu_indices(RK, k=1)
    grid = np.zeros((C, RK, RK), a["L1_cond_W"].dtype)
    grid[:, iu, ju] = a["L1_cond_W"].T
    r["rot_W"] = grid.reshape(C, RK * RK)
    grid = np.zeros((RK, RK), a["L1_cond_b"].dtype)
    grid[iu, ju] = a["L1_cond_b"]
    r["rot_b"] = grid.reshape(1, RK * RK)
    names = [("L0_cond_W_qkv", "L0_cond_b_qkv", "L0_cond_W_proj", "L0_cond_b_proj", "L0_cond_W_ada", "L0_cond_b_ada",
              "L0_cond_W_fc1", "L0_cond_b_fc1", "L0_cond_W_fc2", "L0_cond_b_fc2"),
             ("L2_cond_w_qkv", "L2_cond_b_qkv", "L2_cond_w_proj", "L2_cond_b_proj", "L2_cond_w_adaln", "L2_cond_b_adaln",
              "L2_cond_w1", "L2_cond_b1", "L2_cond_w2", "L2_cond_b2"),
             ("L3_cond_w_qkv", "L3_cond_b_qkv", "L3_cond_w_proj", "L3_cond_b_proj", "L3_cond_w_mod", "L3_cond_b_mod",
              "L3_cond_w1", "L3_cond_b1", "L3_cond_w2", "L3_cond_b2")]
    kinds = ("qkv_w", "qkv_b", "proj_w", "proj_b", "ada_w", "ada_b", "fc1_w", "fc1_b", "fc2_w", "fc2_b")
    for l, row in enumerate(names):
        for kind, name in zip(kinds, row):
            r[f"{kind}{l}"] = a[name]
    return r


def declare(nc, arrays):
    import numpy as np
    ap = {}
    for name, v in arrays.items():
        ap[name] = nc.dram_tensor(f"in_{name}", v.shape, mybir.dt.from_np(v.dtype), kind="ExternalInput").ap()
    out = nc.dram_tensor("out", (B, L, C), F32, kind="ExternalOutput").ap()
    w = {k: v for k, v in ap.items()}

    def row(v):
        return v.rearrange("(o c) -> o c", o=1)
    w["qkv_w"] = [ap[f"qkv_w{l}"] for l in range(3)]
    w["qkv_b"] = [row(ap[f"qkv_b{l}"]) for l in range(3)]
    w["proj_w"] = [ap[f"proj_w{l}"] for l in range(3)]
    w["proj_b"] = [row(ap[f"proj_b{l}"]) for l in range(3)]
    w["ada_w"] = [ap[f"ada_w{l}"] for l in range(3)]
    w["ada_b"] = [ap[f"ada_b{l}"] for l in range(3)]
    for kind in ("fc1_w", "fc2_w"):
        w[kind] = [[ap[f"{kind}{l}"][e] for e in range(EXPERTS)] if l == 1 else [ap[f"{kind}{l}"]] for l in range(3)]
    for kind in ("fc1_b", "fc2_b"):
        w[kind] = [[ap[f"{kind}{l}"][e:e + 1, :] for e in range(EXPERTS)] if l == 1 else [row(ap[f"{kind}{l}"])]
                   for l in range(3)]
    return ap["x"], out, w


def kernel(**inputs):
    import concourse.bacc as bacc
    from concourse.bass_utils import run_bass_kernel_spmd

    nc = bacc.Bacc("TRN2", target_bir_lowering=False, num_devices=1)
    arrays = {**laid_out(inputs), **constants()}
    x_in, out, w = declare(nc, arrays)
    build(nc, x_in, out, w)
    r = run_bass_kernel_spmd(nc, [{f"in_{k}": v for k, v in arrays.items()}], core_ids=[0])
    return r.results[0]["out"]
```
